# Optimizing a Trainium2 kernel written in Bass

```python
import numpy as np
import jax
import jax.numpy as jnp

def _softmax(x, axis=-1):
    return jax.nn.softmax(x, axis=axis)

def _gelu(x):
    return jax.nn.gelu(x, approximate=True)

def _silu(x):
    return jax.nn.silu(x)

def _sigmoid(x):
    return jax.nn.sigmoid(x)

def _layernorm(x, axis=-1, eps=1e-05):
    m = jnp.mean(x, axis=axis, keepdims=True)
    v = jnp.var(x, axis=axis, keepdims=True)
    return (x - m) / jnp.sqrt(v + eps)

def _scatter_add(tgt, idx, src, axis=0):
    return tgt.at[idx].add(src)

def _segment_sum(src, seg, n):
    return jax.ops.segment_sum(src, seg, n)
kernel_name = 'mk_gnn_preln_d4_gnn_r8_fd9741'

def setup_inputs(seed: int=0):
    np.random.seed(seed)
    _w = jnp.asarray

    def _rec_inputs():
        import jax
        import jax.numpy as jnp
        _gk = jax.random.key(seed)
        x = -0.0005121 + 1.001 * jax.random.normal(jax.random.fold_in(_gk, 1), (12500, 64), jnp.float32)
        _s = jax.random.randint(jax.random.fold_in(_gk, 2), (100000,), 0, 12500, jnp.int32)
        _d = jax.random.randint(jax.random.fold_in(_gk, 3), (100000,), 0, 12500, jnp.int32)
        _loop = jnp.arange(12500, dtype=jnp.int32)
        src = jnp.concatenate([_s, _d, _loop])
        dst = jnp.concatenate([_d, _s, _loop])
        _o = jnp.argsort(dst, stable=True)
        src = src[_o]
        dst = dst[_o]
        edge_attr_32 = 0.000216709 + 1.00012 * jax.random.normal(jax.random.fold_in(_gk, 12), (212500, 32), jnp.float32)
        edge_type_500 = jax.random.randint(jax.random.fold_in(_gk, 14), (212500,), 0, 500, jnp.int32)
        edge_weight = jax.random.uniform(jax.random.fold_in(_gk, 15), (212500,), jnp.float32, 0.0, 0.999998)
        return (x, src, dst, edge_attr_32, edge_type_500, edge_weight)
    x, src, dst, edge_attr_32, edge_type_500, edge_weight = _rec_inputs()

    def _L0_gnn_setup():
        import jax, jax.numpy as jnp
        import numpy as np
        LOWER_THRESHOLD = 0.0
        N_NODES = 6250
        N_EDGES = 100000
        CHANNELS = 64
        key = jax.random.key(seed)
        k1, k2 = jax.random.split(key)
        x = jax.random.normal(k1, (N_NODES, CHANNELS), dtype=jnp.float32)
        adaptive_weight = jnp.ones((), dtype=jnp.float32)
        edge_index = jax.random.randint(k2, (2, N_EDGES), 0, N_NODES, dtype=jnp.int64)
        return {'x': x, 'adaptive_weight': adaptive_weight, 'edge_index': edge_index, 'num_nodes': N_NODES}
    _L0_gnn_all = _L0_gnn_setup()
    _L0_gnn_in = {k: v for k, v in _L0_gnn_all.items() if k in ('adaptive_weight',)}
    del _L0_gnn_all

    def _L1_gnn_setup():
        import jax, jax.numpy as jnp
        import numpy as np
        N_NODES = 6250

        def _gcn_conv(x, W, b, src, dst, dinv, n):
            h = x @ W
            norm = dinv[src] * dinv[dst]
            msg = h[src] * norm[:, None]
            out = jax.ops.segment_sum(msg, dst, num_segments=n)
            return out + b
        key = jax.random.key(seed)
        ks = jax.random.split(key, 10)
        n, e, cin, chid = (N_NODES, 75000, 64, 128)
        x = jax.random.normal(ks[0], (n, cin), dtype=jnp.float32)
        edge_index = jax.random.randint(ks[1], (2, e), 0, n, dtype=jnp.int64)

        def glorot(k, fi, fo):
            s = jnp.sqrt(6.0 / (fi + fo)).astype(jnp.float32)
            return jax.random.uniform(k, (fi, fo), jnp.float32, -s, s)
        return {'x': x, 'edge_index': edge_index, 'W1': glorot(ks[2], cin, chid), 'b1': jnp.zeros((chid,), jnp.float32), 'W2': glorot(ks[3], chid, cin), 'b2': jnp.zeros((cin,), jnp.float32), 'W3': glorot(ks[4], cin, chid), 'b3': jnp.zeros((chid,), jnp.float32), 'W4': glorot(ks[5], chid, cin), 'b4': jnp.zeros((cin,), jnp.float32)}
    _L1_gnn_all = _L1_gnn_setup()
    _L1_gnn_in = {k: v for k, v in _L1_gnn_all.items() if k in ('W1', 'b1', 'W2', 'b2', 'W3', 'b3', 'W4', 'b4')}
    del _L1_gnn_all

    def _L2_gnn_setup():
        import jax, jax.numpy as jnp
        import numpy as np
        N_NODES = 12500
        N_EDGES = 156250
        N_RELS = 500
        D = 64
        key = jax.random.key(seed)
        k1, k2, k3, k4, k5 = jax.random.split(key, 5)
        edge_index = jax.random.randint(k1, (2, N_EDGES), 0, N_NODES, dtype=jnp.int64 if jax.config.jax_enable_x64 else jnp.int32)
        edge_type = jax.random.randint(k2, (N_EDGES,), 0, N_RELS, dtype=edge_index.dtype)
        ent_embed = jax.random.normal(k3, (N_NODES, D), dtype=jnp.float32)
        rel_embed = jax.random.normal(k4, (N_RELS, D), dtype=jnp.float32)
        edge_norm = jax.random.uniform(k5, (N_EDGES,), dtype=jnp.float32)
        return {'edge_index': edge_index, 'edge_type': edge_type, 'ent_embed': ent_embed, 'rel_embed': rel_embed, 'edge_norm': edge_norm}
    _L2_gnn_all = _L2_gnn_setup()
    _L2_gnn_in = {k: v for k, v in _L2_gnn_all.items() if k in ('rel_embed',)}
    del _L2_gnn_all

    def _L3_gnn_setup():
        import jax, jax.numpy as jnp
        import numpy as np
        N_NODES = 6250
        N_EDGES = 100000
        D_NODE = 64
        D_EDGE = 32
        D_HID = 128

        def _mlp(x, W1, b1, W2, b2):
            return jax.nn.relu(x @ W1 + b1) @ W2 + b2
        key = jax.random.key(seed)
        ks = jax.random.split(key, 12)
        inp = {'nodes': jax.random.normal(ks[0], (N_NODES, D_NODE), dtype=jnp.float32), 'row': jax.random.randint(ks[1], (N_EDGES,), 0, N_NODES, dtype=jnp.int32), 'col': jax.random.randint(ks[2], (N_EDGES,), 0, N_NODES, dtype=jnp.int32), 'edge_features': jax.random.normal(ks[3], (N_EDGES, D_EDGE), dtype=jnp.float32)}
        d_in_msg = 2 * D_NODE + D_EDGE
        inp['mW1'] = jax.random.normal(ks[4], (d_in_msg, D_HID), dtype=jnp.float32) / np.sqrt(d_in_msg)
        inp['mb1'] = jnp.zeros((D_HID,), dtype=jnp.float32)
        inp['mW2'] = jax.random.normal(ks[5], (D_HID, D_NODE), dtype=jnp.float32) / np.sqrt(D_HID)
        inp['mb2'] = jnp.zeros((D_NODE,), dtype=jnp.float32)
        d_in_upd = 2 * D_NODE
        inp['uW1'] = jax.random.normal(ks[6], (d_in_upd, D_HID), dtype=jnp.float32) / np.sqrt(d_in_upd)
        inp['ub1'] = jnp.zeros((D_HID,), dtype=jnp.float32)
        inp['uW2'] = jax.random.normal(ks[7], (D_HID, D_NODE), dtype=jnp.float32) / np.sqrt(D_HID)
        inp['ub2'] = jnp.zeros((D_NODE,), dtype=jnp.float32)
        return inp
    _L3_gnn_all = _L3_gnn_setup()
    _L3_gnn_in = {k: v for k, v in _L3_gnn_all.items() if k in ('mW1', 'mb1', 'mW2', 'mb2', 'uW1', 'ub1', 'uW2', 'ub2')}
    del _L3_gnn_all
    return {'x': x, 'src': src, 'dst': dst, 'edge_attr_32': edge_attr_32, 'edge_type_500': edge_type_500, 'edge_weight': edge_weight, 'L0_gnn_adaptive_weight': _L0_gnn_in['adaptive_weight'], 'L1_gnn_W1': _L1_gnn_in['W1'], 'L1_gnn_b1': _L1_gnn_in['b1'], 'L1_gnn_W2': _L1_gnn_in['W2'], 'L1_gnn_b2': _L1_gnn_in['b2'], 'L1_gnn_W3': _L1_gnn_in['W3'], 'L1_gnn_b3': _L1_gnn_in['b3'], 'L1_gnn_W4': _L1_gnn_in['W4'], 'L1_gnn_b4': _L1_gnn_in['b4'], 'L2_gnn_rel_embed': _L2_gnn_in['rel_embed'], 'L3_gnn_mW1': _L3_gnn_in['mW1'], 'L3_gnn_mb1': _L3_gnn_in['mb1'], 'L3_gnn_mW2': _L3_gnn_in['mW2'], 'L3_gnn_mb2': _L3_gnn_in['mb2'], 'L3_gnn_uW1': _L3_gnn_in['uW1'], 'L3_gnn_ub1': _L3_gnn_in['ub1'], 'L3_gnn_uW2': _L3_gnn_in['uW2'], 'L3_gnn_ub2': _L3_gnn_in['ub2']}

def reference(x, src, dst, edge_attr_32, edge_type_500, edge_weight, L0_gnn_adaptive_weight, L1_gnn_W1, L1_gnn_b1, L1_gnn_W2, L1_gnn_b2, L1_gnn_W3, L1_gnn_b3, L1_gnn_W4, L1_gnn_b4, L2_gnn_rel_embed, L3_gnn_mW1, L3_gnn_mb1, L3_gnn_mW2, L3_gnn_mb2, L3_gnn_uW1, L3_gnn_ub1, L3_gnn_uW2, L3_gnn_ub2):
    import jax
    import jax.numpy as jnp

    def _L0_gnn_ref(x, adaptive_weight, edge_index, num_nodes):
        import jax, jax.numpy as jnp
        import numpy as np
        LOWER_THRESHOLD = 0.0
        N_NODES = 6250
        N_EDGES = 100000
        CHANNELS = 64
        row, col = (edge_index[0], edge_index[1])
        ones = jnp.ones((edge_index.shape[1],), dtype=x.dtype)
        deg = jax.ops.segment_sum(ones, row, num_segments=num_nodes)
        deg_inv_sqrt = jnp.where(deg > 0, jax.lax.rsqrt(deg), jnp.zeros_like(deg))
        edge_weight = deg_inv_sqrt[row] * deg_inv_sqrt[col]
        msg = x[row] * edge_weight[:, None]
        msg = jnp.where(msg > LOWER_THRESHOLD, msg, jnp.zeros_like(msg))
        msg = msg * adaptive_weight
        out = x + jax.ops.segment_sum(msg, col, num_segments=num_nodes)
        return out

    def _L1_gnn_ref(x, edge_index, W1, b1, W2, b2, W3, b3, W4, b4):
        import jax, jax.numpy as jnp
        import numpy as np
        N_NODES = 6250

        def _gcn_conv(x, W, b, src, dst, dinv, n):
            h = x @ W
            norm = dinv[src] * dinv[dst]
            msg = h[src] * norm[:, None]
            out = jax.ops.segment_sum(msg, dst, num_segments=n)
            return out + b
        n = x.shape[0]
        loop = jnp.arange(n, dtype=edge_index.dtype)
        src = jnp.concatenate([edge_index[0], loop])
        dst = jnp.concatenate([edge_index[1], loop])
        deg = jax.ops.segment_sum(jnp.ones_like(dst, dtype=x.dtype), dst, num_segments=n)
        dinv = jnp.where(deg > 0, jax.lax.rsqrt(deg), 0.0)
        x_l1 = jax.nn.relu(_gcn_conv(x, W1, b1, src, dst, dinv, n))
        x_l2 = jax.nn.relu(_gcn_conv(x_l1, W2, b2, src, dst, dinv, n))
        x_l1_td = jax.nn.relu(_gcn_conv(x_l2, W3, b3, src, dst, dinv, n)) + x_l1
        x_out = jax.nn.relu(_gcn_conv(x_l1_td, W4, b4, src, dst, dinv, n)) + x
        return x_out

    def _L2_gnn_ref(edge_index, edge_type, ent_embed, rel_embed, edge_norm):
        import jax, jax.numpy as jnp
        import numpy as np
        N_NODES = 12500
        N_EDGES = 156250
        N_RELS = 500
        D = 64
        num_nodes = ent_embed.shape[0]
        src = edge_index[1]
        dst = edge_index[0] % num_nodes
        msg = (ent_embed[src] + rel_embed[edge_type]) * edge_norm[:, None]
        out = jax.ops.segment_sum(msg, dst, num_segments=num_nodes)
        return out

    def _L3_gnn_ref(nodes, row, col, edge_features, mW1, mb1, mW2, mb2, uW1, ub1, uW2, ub2):
        import jax, jax.numpy as jnp
        import numpy as np
        N_NODES = 6250
        N_EDGES = 100000
        D_NODE = 64
        D_EDGE = 32
        D_HID = 128

        def _mlp(x, W1, b1, W2, b2):
            return jax.nn.relu(x @ W1 + b1) @ W2 + b2
        msg_in = jnp.concatenate([nodes[row], nodes[col], edge_features], axis=-1)
        messages = _mlp(msg_in, mW1, mb1, mW2, mb2)
        aggregated = jax.ops.segment_sum(messages, col, num_segments=nodes.shape[0])
        upd_in = jnp.concatenate([nodes, aggregated], axis=-1)
        return _mlp(upd_in, uW1, ub1, uW2, ub2)
    edge_index = jnp.stack([src, dst])
    h = jnp.maximum(_layernorm(x, axis=-1), 0.0)
    x = x + _L0_gnn_ref(h, L0_gnn_adaptive_weight, edge_index, 12500)
    h = jnp.maximum(_layernorm(x, axis=-1), 0.0)
    x = x + _L1_gnn_ref(h, edge_index, L1_gnn_W1, L1_gnn_b1, L1_gnn_W2, L1_gnn_b2, L1_gnn_W3, L1_gnn_b3, L1_gnn_W4, L1_gnn_b4)
    h = jnp.maximum(_layernorm(x, axis=-1), 0.0)
    x = x + _L2_gnn_ref(edge_index, edge_type_500, h, L2_gnn_rel_embed, edge_weight)
    h = jnp.maximum(_layernorm(x, axis=-1), 0.0)
    x = x + _L3_gnn_ref(h, src, dst, edge_attr_32, L3_gnn_mW1, L3_gnn_mb1, L3_gnn_mW2, L3_gnn_mb2, L3_gnn_uW1, L3_gnn_ub1, L3_gnn_uW2, L3_gnn_ub2)
    return x

_drawn_inputs = setup_inputs


def setup_inputs(seed=0):
    import zlib

    import numpy as np

    out = dict(_drawn_inputs(seed))
    spreads = {'L1_gnn_b1': (0.0, 0.294),
     'L1_gnn_b2': (0.0, 0.579),
     'L1_gnn_b3': (0.0, 0.32),
     'L1_gnn_b4': (0.0, 0.303),
     'L3_gnn_mb1': (0.0, 0.1),
     'L3_gnn_mb2': (0.0, 0.1),
     'L3_gnn_ub1': (0.0, 0.8),
     'L3_gnn_ub2': (0.0, 0.62)}
    factors = {}
    for name, (base, spread) in spreads.items():
        noise = np.random.default_rng([zlib.crc32(name.encode()), seed]).standard_normal(out[name].shape)
        drawn = base * np.exp(spread * noise) if base else spread * noise
        out[name] = jnp.asarray(drawn.astype(out[name].dtype))
    for name, factor in factors.items():
        out[name] = (out[name] * factor).astype(out[name].dtype)
    return out
```

```python
from contextlib import ExitStack

import concourse.bass as bass
from concourse import mybir

F32, I32, BF16 = mybir.dt.float32, mybir.dt.int32, mybir.dt.bfloat16
ALU = mybir.AluOpType
ACT = mybir.ActivationFunctionType
AX = mybir.AxisListType

P = 128
U = 8
GE = P * U
SLOTS = 4
PADDED = 65536
ROUND = 12582912.0
EPS = 1e-5
SCATTERS = 4
KB = 4


class Names:
    pass


def feature_major(acc, rows, n, nb):
    return acc[0:rows, 0:n].rearrange("f (p b) -> f b p", b=nb)




def over_windows(eng, k, window, between=None):
    window(0)
    spread = eng.value_load(k.spread_i[0:1, 0:1], min_val=0, max_val=1)
    with eng.If(spread):
        with eng.Fori(1, k.windows) as w:
            if between:
                between(w)
            window(w)


def over_groups(eng, k, w, body):
    if k.rounds > 1:
        with eng.Fori(0, k.rounds - 1) as i:
            body(i, w * k.rounds + i)
    body(k.rounds - 1, w * k.rounds + (k.rounds - 1))


def phase_sems(nc, k, *names):
    made = [k.open_phases.enter_context(nc.semaphore(name)) for name in names]
    k.phase_sems += made
    return made


def clear(nc, k):
    nc.all_engine_barrier()
    first = None
    nums = sorted(s.num for s in k.pass_sems + k.phase_sems)
    for at, num in enumerate(nums):
        first = num if first is None else first
        if at == len(nums) - 1 or nums[at + 1] != num + 1:
            nc.gpsimd.sem_clear(range(first, num + 1))
            first = None
    nc.all_engine_barrier()
    k.open_phases.close()
    k.phase_sems = []


def edge_parts(k, tile, dram):
    full = (k.groups - 1) * GE
    whole, rest = divmod(k.e - full, U)
    parts = [(tile[:, 0:(k.groups - 1) * U].rearrange("p (g u) -> p g u", u=U),
              dram[0:full].rearrange("(g p u) -> p g u", p=P, u=U))]
    last = tile[:, (k.groups - 1) * U:k.groups * U]
    if whole:
        parts.append((last[0:whole, :], dram[full:full + whole * U].rearrange("(p u) -> p u", u=U)))
    if rest:
        parts.append((last[whole:whole + 1, 0:rest], dram[k.e - rest:k.e].rearrange("(a u) -> a u", a=1)))
    return parts


def load_and_index(nc, k, a):
    pads_set, edges_loaded, rest_loaded = phase_sems(nc, k, "pads_set", "edges_loaded", "rest_loaded")
    iota_made, extremes, reduced, step = phase_sems(nc, k, "iota_made", "extremes", "reduced", "index_step")
    zeroed, pads_ready = phase_sems(nc, k, "we_zeroed", "pads_ready")

    with nc.Block() as block:
        src_i, dst_i, src_f, dst_f = k.src_i, k.dst_i, k.src_f, k.dst_f
        G = k.groups

        edge = [(t, d) for tile, dram in ((src_i, a.src), (dst_i, a.dst), (k.typ, a.edge_type_500), (k.wgt, a.edge_weight))
                for t, d in edge_parts(k, tile, dram)]
        row = lambda v, n: v.rearrange("(a n) -> a n", a=1).to_broadcast([n, v.shape[0]])
        col = lambda v: v.rearrange("(n a) -> n a", a=1)
        rest = [(k.x[:, :, :], a.x.rearrange("(p b) f -> p b f", b=k.nb)),
                (k.w1[:, :], a.L1_gnn_W1), (k.w2[:, :], a.L1_gnn_W2), (k.w3[:, :], a.L1_gnn_W3), (k.w4[:, :], a.L1_gnn_W4),
                (k.b1[:, :], col(a.L1_gnn_b1)), (k.b3[:, :], col(a.L1_gnn_b3)),
                (k.b2[:, :], row(a.L1_gnn_b2, P)), (k.b4[:, :], row(a.L1_gnn_b4, P)),
                (k.w_uv[:, 0:128], a.L3_gnn_mW1[0:64, :]), (k.w_uv[:, 128:256], a.L3_gnn_mW1[64:128, :]),
                (k.mb1[:, :], row(a.L3_gnn_mb1, P)), (k.mw2[:, :], a.L3_gnn_mW2), (k.mb2[:, :], row(a.L3_gnn_mb2, P)),
                (k.uw1[:, :], a.L3_gnn_uW1), (k.ub1[:, :], col(a.L3_gnn_ub1)), (k.uw2[:, :], a.L3_gnn_uW2),
                (k.ub2[:, :], row(a.L3_gnn_ub2, P)),
                (k.adapt[:, :], row(a.L0_gnn_adaptive_weight, P))]
        diag = [(k.we[32 * q:32 * q + 32, 128 * q:128 * q + 128], a.L3_gnn_mW1[128:160, :]) for q in range(4)]

        @block.sync
        def _(sp):
            sp.wait_ge(pads_set, 1)
            for to, of in edge:
                sp.dma_start(to, of).then_inc(edges_loaded, 16)
            for to, of in rest:
                sp.dma_start(to, of).then_inc(rest_loaded, 16)
            sp.wait_ge(pads_ready, 1)
            fill = k.groups * GE - k.e
            for pad, of in zip(k.edge_pad, (a.src, a.dst)):
                sp.dma_start(pad[0:k.e].rearrange("(p n) -> p n", p=4), of.rearrange("(p n) -> p n", p=4)).then_inc(rest_loaded, 16)
                sp.dma_start(pad[k.e:k.e + fill].rearrange("(a n) -> a n", a=1), k.fill[0:1, 0:fill]).then_inc(rest_loaded, 16)
            sp.wait_ge(zeroed, 1)
            sp.dma_start(k.table[k.n:k.n + P, :], k.we[:, 0:64]).then_inc(rest_loaded, 16)
            sp.wait_ge(rest_loaded, 16 * (len(rest) + 5))
            for to, of in diag:
                sp.dma_start(to, of).then_inc(rest_loaded, 16)
            sp.wait_ge(rest_loaded, 16 * (len(rest) + 5 + len(diag)))

        @block.gpsimd
        def _(pool):
            nc.gpsimd.iota(k.row_i[:, :], pattern=[[1, P]], base=0, channel_multiplier=0).then_inc(iota_made, 1)
            nc.gpsimd.iota(k.part_i[:, :], pattern=[[0, 1]], base=0, channel_multiplier=1).then_inc(iota_made, 1)
            pool.wait_ge(extremes, 1)
            nc.gpsimd.partition_all_reduce(k.base[:, 0:2 * G], k.ends[:, 0:2 * G], P, bass.bass_isa.ReduceOp.max).then_inc(reduced, 1)

        @block.vector
        def _(dve):
            done = [0]

            def then(ins):
                done[0] += 1
                ins.then_inc(step, 1)
                dve.wait_ge(step, done[0])

            last = slice((G - 1) * U, G * U)
            then(nc.vector.memset(src_i[:, last], PADDED))
            then(nc.vector.memset(dst_i[:, last], PADDED))
            then(nc.vector.memset(k.typ[:, last], 0))
            nc.vector.memset(k.wgt[:, last], 0.0).then_inc(pads_set, 1)
            nc.vector.memset(k.fill[0:1, :], PADDED).then_inc(pads_ready, 1)
            nc.vector.memset(k.we[:, :], 0.0).then_inc(zeroed, 1)
            dve.wait_ge(iota_made, 2)
            then(nc.vector.tensor_copy(k.row_f[:, :], k.row_i[:, :]))
            then(nc.vector.tensor_copy(k.part_f[:, :], k.part_i[:, :]))
            then(nc.vector.tensor_scalar(k.ident[:, :], k.row_f[:, :], k.part_f[:, 0:1], None, ALU.is_equal))
            dve.wait_ge(edges_loaded, 16 * len(edge))
            then(nc.vector.tensor_copy(src_f[:, :], src_i[:, :]))
            then(nc.vector.tensor_copy(dst_f[:, :], dst_i[:, :]))
            then(nc.vector.scalar_tensor_tensor(k.idx[:, :], src_f[:, :], float(PADDED), src_f[:, :], ALU.is_lt, ALU.mult))
            then(nc.vector.tensor_reduce(k.ends[:, 0:G], dst_f.rearrange("p (g u) -> p g u", u=U), AX.X, ALU.min, negate=True))
            then(nc.vector.scalar_tensor_tensor(k.src_hi[:, :], dst_f[:, :], float(PADDED), dst_f[:, :], ALU.is_lt, ALU.mult))
            nc.vector.tensor_reduce(k.ends[:, G:2 * G], k.src_hi.rearrange("p (g u) -> p g u", u=U), AX.X, ALU.max).then_inc(extremes, 1)
            dve.wait_ge(reduced, 1)
            then(nc.vector.tensor_tensor(k.base[:, G:2 * G], k.base[:, G:2 * G], k.base[:, 0:G], ALU.add))
            then(nc.vector.tensor_reduce(k.spread_f[:, 0:1], k.base[:, G:2 * G], AX.X, ALU.max))
            then(nc.vector.tensor_scalar(k.spread_f[:, 0:1], k.spread_f[:, 0:1], float(P), None, ALU.is_ge))
            then(nc.vector.tensor_copy(k.spread_i[:, :], k.spread_f[:, 0:1]))
            then(nc.vector.tensor_scalar(k.spread_f[:, 0:1], k.spread_f[:, 0:1], 1.0, None, ALU.subtract))
            then(nc.vector.tensor_scalar(k.base[:, 0:G], k.base[:, 0:G], k.spread_f[:, 0:1], None, ALU.mult))
            then(nc.vector.tensor_copy(k.base_i[:, :], k.base[:, 0:G]))
            then(nc.vector.tensor_scalar(k.pos[:, :], k.base[:, 0:G], k.part_f[:, 0:1], None, ALU.add))
            then(nc.vector.tensor_tensor(k.rel.rearrange("p (g u) -> p g u", u=U), dst_f.rearrange("p (g u) -> p g u", u=U),
                                         k.base[:, 0:G].unsqueeze(2).to_broadcast([P, G, U]), ALU.subtract))
            then(nc.vector.tensor_scalar(k.src_hi[:, :], src_f[:, :], 1.0 / k.nb, -(k.nb - 1) / (2.0 * k.nb), ALU.mult, ALU.add))
            then(nc.vector.tensor_scalar(k.src_hi[:, :], k.src_hi[:, :], ROUND, None, ALU.add))
            then(nc.vector.tensor_scalar(k.src_hi[:, :], k.src_hi[:, :], ROUND, None, ALU.subtract))
            then(nc.vector.scalar_tensor_tensor(k.src_lo[:, :], k.src_hi[:, :], -float(k.nb), src_f[:, :], ALU.mult, ALU.add))


def count_src(nc, k):
    digits, counted, added, step, rooted = phase_sems(nc, k, "digits_ready", "counted", "counts_added", "degree_step", "rooted")
    hi = k.acc[:, 0:P * U].bitcast(BF16).rearrange("p (s u n) -> p s u n", s=2, u=U)
    lo = k.acc[:, P * U:2 * P * U].bitcast(BF16).rearrange("p (s u n) -> p s u n", s=2, u=U)

    with nc.Block() as block:
        M, NB = k.m, k.nb

        @block.vector
        def _(dve):
            def one_hots(g, s):
                for out, digit, n in ((hi, k.src_hi, M), (lo, k.src_lo, NB)):
                    ins = nc.vector.tensor_tensor(out[:, s, :, 0:n], k.row_f[:, 0:n].unsqueeze(1).to_broadcast([P, U, n]),
                                                  digit[:, bass.ds(g * U, U)].unsqueeze(2).to_broadcast([P, U, n]), ALU.is_equal)
                ins.then_inc(digits, 1)

            nc.vector.memset(k.deg_s[:, :], 0.0).then_inc(added, 1)
            with dve.Fori(0, k.groups // 2) as i:
                for s in range(2):
                    g = 2 * i + s
                    dve.wait_ge(added, g + 1)
                    one_hots(g, s)
                    dve.wait_ge(counted, g + 1)
                    nc.vector.tensor_tensor(k.deg_s[:, :], k.deg_s[:, :], k.ps[0:M, s, 0:NB], ALU.add).then_inc(added, 1)
            dve.wait_ge(added, k.groups + 1)
            nc.vector.tensor_scalar(k.inv_s[:, :], k.deg_s[:, :], 1.0, None, ALU.max).then_inc(step, 1)
            dve.wait_ge(rooted, 1)
            nc.vector.reciprocal(k.inv_s[:, :], k.inv_s[:, :]).then_inc(step, 1)
            nc.vector.tensor_scalar(k.deg_s[:, :], k.deg_s[:, :], 0.0, None, ALU.is_gt).then_inc(step, 1)
            dve.wait_ge(step, 3)
            nc.vector.tensor_tensor(k.inv_s[:, :], k.inv_s[:, :], k.deg_s[:, :], ALU.mult).then_inc(step, 1)

        @block.tensor
        def _(pe):
            with pe.Fori(0, k.groups // 2) as i:
                for s in range(2):
                    g = 2 * i + s
                    pe.wait_ge(digits, g + 1)
                    for u in range(U):
                        ins = nc.tensor.matmul(k.ps[0:M, s, 0:NB], hi[:, s, u, 0:M], lo[:, s, u, 0:NB], start=u == 0, stop=u == U - 1)
                    ins.then_inc(counted, 1)

        @block.scalar
        def _(act):
            act.wait_ge(step, 1)
            nc.scalar.activation(k.inv_s[:, :], k.inv_s[:, :], ACT.Sqrt).then_inc(rooted, 1)


def norm_relu(nc, k, name, scale=None, add_to_x=False, inv_from=None, clear_acc=False, ones=False):
    step, var_ready, std_ready, stored, acc_clear = phase_sems(nc, k, f"{name}_step", f"{name}_var_ready", f"{name}_std_ready", f"{name}_stored", f"{name}_acc_clear")
    M, NB = k.m, k.nb
    sq = k.acc[0:M, 0:NB * 64].rearrange("p (b f) -> p b f", f=64)
    wide = lambda v: v[:, :].unsqueeze(2).to_broadcast([M, NB, 64])

    with nc.Block() as block:

        @block.vector
        def _(dve):
            done = [0]

            def then(ins):
                done[0] += 1
                ins.then_inc(step, 1)
                dve.wait_ge(step, done[0])

            if inv_from is not None:
                nc.vector.tensor_scalar(k.inv_d[:, :], inv_from[:, :], 1.0, None, ALU.add).then_inc(var_ready, 1)
                dve.wait_ge(std_ready, 1)
                then(nc.vector.reciprocal(k.inv_d[:, :], k.inv_d[:, :]))
            then(nc.vector.tensor_reduce(k.mean[:, :], k.x[:, :, :], AX.X, ALU.add))
            then(nc.vector.tensor_scalar(k.mean[:, :], k.mean[:, :], 1.0 / 64, None, ALU.mult))
            then(nc.vector.tensor_tensor(k.t[:, :, :], k.x[:, :, :], wide(k.mean), ALU.subtract))
            then(nc.vector.tensor_tensor(sq, k.t[:, :, :], k.t[:, :, :], ALU.mult))
            then(nc.vector.tensor_reduce(k.var[:, :], sq, AX.X, ALU.add))
            n = 1 + (inv_from is not None)
            nc.vector.tensor_scalar(k.var[:, :], k.var[:, :], 1.0 / 64, EPS, ALU.mult, ALU.add).then_inc(var_ready, 1)
            dve.wait_ge(std_ready, n)
            then(nc.vector.reciprocal(k.var[:, :], k.var[:, :]))
            then(nc.vector.tensor_tensor(k.t[:, :, :], k.t[:, :, :], wide(k.var), ALU.mult))
            then(nc.vector.tensor_scalar(k.t[:, :, :], k.t[:, :, :], 0.0, None, ALU.max))
            if add_to_x:
                then(nc.vector.tensor_tensor(k.x[:, :, :], k.x[:, :, :], k.t[:, :, :], ALU.add))
            if scale is not None:
                then(nc.vector.tensor_tensor(k.t[:, :, :], k.t[:, :, :], wide(scale), ALU.mult))
            if ones:
                nc.vector.memset(k.rows[:, :, :, 64], 1.0).then_inc(acc_clear, 1)
            if clear_acc:
                nc.vector.memset(k.acc[:, :], 0.0).then_inc(acc_clear, 1)
            k.last_step = done[0]

        @block.scalar
        def _(act):
            n = 0
            if inv_from is not None:
                n = 1
                act.wait_ge(var_ready, 1)
                nc.scalar.activation(k.inv_d[:, :], k.inv_d[:, :], ACT.Sqrt).then_inc(std_ready, 1)
            act.wait_ge(var_ready, n + 1)
            nc.scalar.activation(k.var[:, :], k.var[:, :], ACT.Sqrt).then_inc(std_ready, 1)

        @block.sync
        def _(sp):
            sp.wait_ge(step, k.last_step)
            sp.dma_start(k.table_rows, k.t[:, :, :]).then_inc(stored, 16)
            sp.wait_ge(stored, 16)


def sum_by_dst(nc, k, table, width):
    clear(nc, k)
    gathered = k.gather_sems.pop()
    with nc.Block() as block:
        rows, oh, ps = k.rows, k.one_hot, k.ps

        @block.gpsimd
        def _(pool):
            def body(i, r):
                for s in range(SLOTS):
                    pool.wait_ge(k.idx_ready[s], r + 1)
                    pool.sem_inc(k.paced, 1)
                    for u in range(U):
                        nc.gpsimd.indirect_dma_start(rows[:, s, u, 0:64], None, table,
                                                     bass.IndirectOffsetOnAxis(k.idx_slot[:, s, u:u + 1], 0)).then_inc(gathered[s], 16)

            over_windows(pool, k, lambda w: over_groups(pool, k, w, body))

        @block.scalar
        def _(act):
            def body(i, r):
                for s in range(SLOTS):
                    at = bass.ds((SLOTS * i + s) * U, U)
                    act.wait_ge(k.group_done[s], r + 1)
                    nc.scalar.copy(k.idx_slot[:, s, :], k.idx[:, at]).then_inc(k.idx_ready[s], 1)

            over_windows(act, k, lambda w: over_groups(act, k, w, body))

        @block.tensor
        def _(pe):
            for s in range(SLOTS):
                pe.sem_inc(k.group_done[s], 1)

            def body(i, r):
                for s in range(SLOTS):
                    pe.wait_ge(gathered[s], 16 * U * (r + 1))
                    pe.wait_ge(k.hot_ready[s], r + 1)
                    pe.wait_ge(k.summed[s], r + 1)
                    for u in range(U):
                        ins = nc.tensor.matmul(ps[0:width, s, 0:P], rows[:, s, u, 0:width], oh[:, s % 2, u, :], start=u == 0, stop=u == U - 1)
                    ins.then_inc(k.group_done[s], 1)

            over_windows(pe, k, lambda w: over_groups(pe, k, w, body))

        @block.vector
        def _(dve):
            for s in range(SLOTS):
                dve.sem_inc(k.summed[s], 1)

            def body(i, r):
                for s in range(SLOTS):
                    g = SLOTS * i + s
                    dve.wait_ge(k.group_done[(s + 2) % SLOTS], r + s // 2 + 1)
                    one_hot(nc, k, g, s % 2).then_inc(k.hot_ready[s], 1)
                    base = dve.value_load(k.base_i[0:1, bass.ds(g, 1)], min_val=0, max_val=k.n - 1)
                    dve.wait_ge(k.group_done[s], r + 2)
                    dve.wait_ge(k.summed[(s + 3) % SLOTS], r + (s > 0) + 1)
                    at = k.acc[0:width, bass.ds(base, P)]
                    nc.vector.tensor_tensor(at, at, ps[0:width, s, 0:P], ALU.add).then_inc(k.summed[s], 1)

            walk_windows(nc, k, dve, lambda w: over_groups(dve, k, w, body))


def one_hot(nc, k, g, slot):
    return nc.vector.tensor_tensor(k.one_hot[:, slot, :, :], k.row_f[:, :].unsqueeze(1).to_broadcast([P, U, P]),
                                   k.rel[:, bass.ds(g * U, U)].unsqueeze(2).to_broadcast([P, U, P]), ALU.is_equal)


def walk_windows(nc, k, dve, window, tables_ready=None, used_up=None):
    def move(by, at):
        for n, (table, op) in enumerate(((k.rel, -by), (k.pos, by), (k.base, by))):
            table = table[:, 0:k.groups] if table is k.base else table[:, :]
            nc.vector.tensor_scalar(table, table, float(op), None, ALU.add).then_inc(k.table_step, 1)
        dve.wait_ge(k.table_step, 4 * at - 1)
        nc.vector.tensor_copy(k.base_i[:, :], k.base[:, 0:k.groups]).then_inc(k.table_step, 1)
        dve.wait_ge(k.table_step, 4 * at)
        dve.sem_inc(k.paced, 1)

    used_up = used_up or k.summed[SLOTS - 1]

    def between(w):
        dve.wait_ge(used_up, w * k.rounds + 1)
        if tables_ready is not None:
            dve.wait_ge(k.loads_issued, w)
        move(P, w)
        if tables_ready is not None:
            dve.sem_inc(tables_ready, 1)

    window(0)
    spread = dve.value_load(k.spread_i[0:1, 0:1], min_val=0, max_val=1)
    with dve.If(spread):
        with dve.Fori(1, k.windows) as w:
            between(w)
            window(w)
        dve.wait_ge(used_up, k.windows * k.rounds + 1)
        if tables_ready is not None:
            dve.wait_ge(k.loads_issued, k.windows)
        move(-P * (k.windows - 1), k.windows)


class Chain:

    def __init__(self, dve, sem, i, per):
        self.dve, self.sem, self.at, self.left = dve, sem, i * per, per

    def __call__(self, ins):
        ins.then_inc(self.sem, 1)
        self.at, self.left = self.at + 1, self.left - 1
        self.dve.wait_ge(self.sem, self.at)

    def end(self):
        assert self.left == 0


def blocks(v, at, m, width):
    return v[:, at].unsqueeze(2).to_broadcast([m, KB, width])


def rows_of(v, m, width):
    return v[0:m, 0:width].unsqueeze(1).to_broadcast([m, KB, width])


def stage_acc(nc, k, rows, i):
    return nc.scalar.copy(k.stage[0:rows, :, :], feature_major(k.acc, rows, k.n, k.nb)[:, bass.ds(i * KB, KB), :])


def turn_out(nc, k, rows):
    for b in range(KB):
        ins = nc.tensor.transpose(node_psum(k)[:, b, 0:rows], k.stage[0:rows, b, :], k.ident[0:rows, 0:rows])
    return ins


def turn_back(nc, k, bank, rows, width):
    for b in range(KB):
        ins = nc.tensor.transpose(k.ps[0:width, bank, k.m * b:k.m * b + k.m], rows[:, b, :], k.ident[0:k.m, 0:k.m])
    return ins


def node_psum(k):
    return k.ps[0:k.m, 0, :].rearrange("p (b f) -> p b f", b=KB)


def place(nc, k, i):
    return nc.scalar.copy(feature_major(k.acc, 64, k.n, k.nb)[:, bass.ds(i * KB, KB), :],
                          k.ps[0:64, 4, 0:KB * k.m].rearrange("f (b p) -> f b p", b=KB))


def add_adaptive_sum(nc, k):
    staged, turned, added, step = phase_sems(nc, k, "adaptive_staged", "adaptive_turned", "adaptive_added", "adaptive_step")

    with nc.Block() as block:
        steps = k.nb // KB

        @block.scalar
        def _(act):
            stage_acc(nc, k, 65, 0).then_inc(staged, 1)
            with act.Fori(1, steps) as i:
                act.wait_ge(turned, i)
                stage_acc(nc, k, 65, i).then_inc(staged, 1)

        @block.tensor
        def _(pe):
            def body(i):
                pe.wait_ge(staged, i + 1)
                pe.sem_inc(k.paced, 1)
                turn_out(nc, k, 65).then_inc(turned, 1)

            body(0)
            with pe.Fori(1, steps) as i:
                pe.wait_ge(added, i)
                body(i)

        @block.vector
        def _(dve):
            nc.vector.tensor_scalar(k.inv_s[:, :], k.inv_s[:, :], k.adapt[0:k.m, 0:1], None, ALU.mult).then_inc(step, 1)
            dve.wait_ge(step, 1)
            with dve.Fori(0, steps) as i:
                at = bass.ds(i * KB, KB)
                dve.wait_ge(turned, i + 1)
                nc.vector.tensor_copy(k.deg_d[:, at], node_psum(k)[:, :, 64]).then_inc(step, 1)
                nc.vector.tensor_tensor(k.t_rows[:, :, :], node_psum(k)[:, :, 0:64], blocks(k.inv_s, at, k.m, 64), ALU.mult).then_inc(step, 1)
                dve.wait_ge(step, 2 * i + 3)
                nc.vector.tensor_tensor(k.x[:, at, :], k.x[:, at, :], k.t_rows[:, :, :], ALU.add).then_inc(added, 1)
                dve.wait_ge(added, i + 1)


def start_acc(nc, k):
    copied, turned, placed = phase_sems(nc, k, "start_copied", "start_turned", "start_placed")

    with nc.Block() as block:
        steps = k.nb // KB

        @block.vector
        def _(dve):
            def body(i):
                nc.vector.tensor_copy(k.t_rows[:, :, :], k.t[:, bass.ds(i * KB, KB), :]).then_inc(copied, 1)

            body(0)
            with dve.Fori(1, steps) as i:
                dve.wait_ge(turned, i)
                body(i)

        @block.tensor
        def _(pe):
            def body(i):
                pe.wait_ge(copied, i + 1)
                pe.sem_inc(k.paced, 1)
                turn_back(nc, k, 4, k.t_rows, 64).then_inc(turned, 1)

            body(0)
            with pe.Fori(1, steps) as i:
                pe.wait_ge(placed, i)
                body(i)

        @block.scalar
        def _(act):
            with act.Fori(0, steps) as i:
                act.wait_ge(turned, i + 1)
                act.sem_inc(k.paced, 1)
                place(nc, k, i).then_inc(placed, 1)


def convolve_wide(nc, k, name, w_in, bias, w_out, residual):
    staged, turned, scaled, back, back_copied = phase_sems(nc, k, f"{name}_staged", f"{name}_turned", f"{name}_scaled", f"{name}_back", f"{name}_back_copied")
    hidden, relued, kept, out, t_ready = phase_sems(nc, k, f"{name}_hidden", f"{name}_relued", f"{name}_kept", f"{name}_out", f"{name}_t_ready")
    t_turned, placed, saved, stored = phase_sems(nc, k, f"{name}_t_turned", f"{name}_placed", f"{name}_saved", f"{name}_stored")

    with nc.Block() as block:
        M, C, steps = k.m, KB * k.m, k.nb // KB
        out_psum = k.ps[0:M, 3, 0:KB * 64].rearrange("p (b f) -> p b f", b=KB)

        @block.scalar
        def _(act):
            with act.Fori(0, steps) as i:
                stage_acc(nc, k, 64, i).then_inc(staged, 1)
                act.wait_ge(back, i + 1)
                nc.scalar.copy(k.back[0:64, :], k.ps[0:64, 1, 0:C]).then_inc(back_copied, 1)
                act.wait_ge(hidden, i + 1)
                nc.scalar.activation(k.hid[:, :], k.ps[:, 2, 0:C], ACT.Relu, bias=bias[:, 0:1]).then_inc(relued, 1)
                act.wait_ge(t_turned, i + 1)
                act.sem_inc(k.paced, 1)
                place(nc, k, i).then_inc(placed, 1)
                act.wait_ge(placed, i + 1)

        @block.tensor
        def _(pe):
            with pe.Fori(0, steps) as i:
                pe.wait_ge(staged, i + 1)
                pe.sem_inc(k.paced, 1)
                turn_out(nc, k, 64).then_inc(turned, 1)
                pe.wait_ge(scaled, i + 1)
                pe.sem_inc(k.paced, 1)
                turn_back(nc, k, 1, k.sums, 64).then_inc(back, 1)
                pe.wait_ge(back_copied, i + 1)
                nc.tensor.matmul(k.ps[:, 2, 0:C], w_in[:, :], k.back[0:64, :], start=True, stop=True).then_inc(hidden, 1)
                pe.wait_ge(kept, i + 1)
                for b in range(KB):
                    ins = nc.tensor.matmul(out_psum[:, b, :], k.kept[:, M * b:M * b + M], w_out[:, :], start=True, stop=True)
                ins.then_inc(out, 1)
                pe.wait_ge(t_ready, i + 1)
                pe.sem_inc(k.paced, 1)
                turn_back(nc, k, 4, k.t_rows, 64).then_inc(t_turned, 1)

        @block.vector
        def _(dve):
            with dve.Fori(0, steps) as i:
                at = bass.ds(i * KB, KB)
                x1 = k.x1[:, bass.ds(i * C, C)]
                dve.wait_ge(turned, i + 1)
                nc.vector.tensor_tensor(k.sums[:, :, :], node_psum(k)[:, :, 0:64], blocks(k.inv_d, at, M, 64), ALU.mult).then_inc(scaled, 1)
                dve.wait_ge(relued, i + 1)
                if residual:
                    nc.vector.tensor_tensor(k.kept[:, :], k.hid[:, :], x1, ALU.add).then_inc(kept, 1)
                else:
                    nc.vector.tensor_copy(k.kept[:, :], k.hid[:, :]).then_inc(kept, 1)
                    nc.vector.tensor_copy(x1, k.hid[:, :]).then_inc(saved, 1)
                dve.wait_ge(out, i + 1)
                nc.vector.tensor_tensor(k.t_rows[:, :, :], out_psum, blocks(k.inv_d, at, M, 64), ALU.mult).then_inc(t_ready, 1)
                dve.wait_ge(t_ready, i + 1)
                nc.vector.tensor_copy(k.t[:, at, :], k.t_rows[:, :, :]).then_inc(saved, 1)
                dve.wait_ge(saved, (i + 1) * (1 if residual else 2))
                dve.wait_ge(t_turned, i + 1)

        @block.sync
        def _(sp):
            sp.wait_ge(saved, steps * (1 if residual else 2))
            sp.dma_start(k.table_rows, k.t[:, :, :]).then_inc(stored, 16)
            sp.wait_ge(stored, 16)


def convolve_second(nc, k):
    staged, turned, step, t_turned, placed, stored = phase_sems(nc, k, "second_staged", "second_turned", "second_step", "second_t_turned", "second_placed", "second_stored")

    with nc.Block() as block:
        steps = k.nb // KB

        @block.scalar
        def _(act):
            with act.Fori(0, steps) as i:
                stage_acc(nc, k, 64, i).then_inc(staged, 1)
                act.wait_ge(t_turned, i + 1)
                act.sem_inc(k.paced, 1)
                place(nc, k, i).then_inc(placed, 1)
                act.wait_ge(placed, i + 1)

        @block.tensor
        def _(pe):
            with pe.Fori(0, steps) as i:
                pe.wait_ge(staged, i + 1)
                pe.sem_inc(k.paced, 1)
                turn_out(nc, k, 64).then_inc(turned, 1)
                pe.wait_ge(step, 5 * i + 4)
                pe.sem_inc(k.paced, 1)
                turn_back(nc, k, 4, k.t_rows, 64).then_inc(t_turned, 1)

        @block.vector
        def _(dve):
            with dve.Fori(0, steps) as i:
                then, at = Chain(dve, step, i, 5), bass.ds(i * KB, KB)
                dve.wait_ge(turned, i + 1)
                then(nc.vector.tensor_tensor(k.t_rows[:, :, :], node_psum(k)[:, :, 0:64], blocks(k.inv_d, at, k.m, 64), ALU.mult))
                then(nc.vector.tensor_tensor(k.t_rows[:, :, :], k.t_rows[:, :, :], rows_of(k.b2, k.m, 64), ALU.add))
                then(nc.vector.tensor_scalar(k.t_rows[:, :, :], k.t_rows[:, :, :], 0.0, None, ALU.max))
                then(nc.vector.tensor_tensor(k.t_rows[:, :, :], k.t_rows[:, :, :], blocks(k.inv_d, at, k.m, 64), ALU.mult))
                then(nc.vector.tensor_copy(k.t[:, at, :], k.t_rows[:, :, :]))
                then.end()
                dve.wait_ge(t_turned, i + 1)

        @block.sync
        def _(sp):
            sp.wait_ge(step, 5 * steps)
            sp.dma_start(k.table_rows, k.t[:, :, :]).then_inc(stored, 16)
            sp.wait_ge(stored, 16)


def add_fourth(nc, k):
    staged, turned, step = phase_sems(nc, k, "fourth_staged", "fourth_turned", "fourth_step")

    with nc.Block() as block:
        steps = k.nb // KB
        per = 4

        @block.scalar
        def _(act):
            stage_acc(nc, k, 64, 0).then_inc(staged, 1)
            with act.Fori(1, steps) as i:
                act.wait_ge(turned, i)
                stage_acc(nc, k, 64, i).then_inc(staged, 1)

        @block.tensor
        def _(pe):
            def body(i):
                pe.wait_ge(staged, i + 1)
                pe.sem_inc(k.paced, 1)
                turn_out(nc, k, 64).then_inc(turned, 1)

            body(0)
            with pe.Fori(1, steps) as i:
                pe.wait_ge(step, per * i)
                body(i)

        @block.vector
        def _(dve):
            with dve.Fori(0, steps) as i:
                then, at = Chain(dve, step, i, per), bass.ds(i * KB, KB)
                dve.wait_ge(turned, i + 1)
                rows = k.t_rows[:, :, :]
                then(nc.vector.tensor_tensor(rows, node_psum(k)[:, :, 0:64], blocks(k.inv_d, at, k.m, 64), ALU.mult))
                then(nc.vector.tensor_tensor(rows, rows, rows_of(k.b4, k.m, 64), ALU.add))
                then(nc.vector.tensor_scalar(rows, rows, 0.0, None, ALU.max))
                then(nc.vector.tensor_tensor(k.x[:, at, :], k.x[:, at, :], rows, ALU.add))
                then.end()


def scatter_to_src(nc, k):
    clear(nc, k)
    typed_in = k.gather_sems.pop()
    N = k.n
    ps = k.ps
    with nc.Block() as block:

        def later(i, r, s, by):
            return i + (s + by) // SLOTS, r + (s + by) // SLOTS, (s + by) % SLOTS

        def last(i, s, by):
            return isinstance(i, int) and i == k.rounds - 1 and s + by >= SLOTS

        @block.sync
        def _(sp):
            sp.dma_start(k.s_src_f.bitcast(I32).rearrange("p (g u) -> p g u", u=U),
                         k.edge_pad[0].rearrange("(g p u) -> p g u", p=P, u=U)).then_inc(k.loaded_rest, 16)

            def body(i, r):
                for s in range(SLOTS):
                    o, g = s % 2, SLOTS * i + s
                    sp.wait_ge(k.from_dst[(s + 2) % SLOTS], r + s // 2 + 1)
                    sp.wait_ge(k.same_ready[(s + 2) % SLOTS], r + s // 2 + 1)
                    sp.sem_inc(k.paced, 1)
                    base = sp.value_load(k.base_i[0:1, bass.ds(g, 1)], min_val=0, max_val=N - 1)
                    for to, of in ((k.s_dst[:, o, :], k.edge_pad[1][bass.ds(g * GE, GE)].rearrange("(a n) -> a n", a=1).to_broadcast([P, GE])),
                                   (k.s_src[:, o, :, :].rearrange("p e u -> p (e u)"),
                                    k.edge_pad[0][bass.ds(g * GE, GE)].rearrange("(a n) -> a n", a=1).to_broadcast([P, GE])),
                                   (k.s_win[:, o, :], k.table[bass.ds(base, P), :])):
                        sp.dma_start(to, of).then_inc(k.loaded[s], 16)

            def window(w):
                over_groups(sp, k, w, body)
                sp.sem_inc(k.loads_issued, 1)

            def between(w):
                sp.wait_ge(k.tables_ready, w)
                sp.sem_inc(k.paced, 1)

            over_windows(sp, k, window, between)

        @block.gpsimd
        def _(pool):
            for j in range(SCATTERS):
                pool.dma_start(k.scattered[j][0:N, :].rearrange("(p b) f -> p (b f)", b=k.nb), k.acc[0:k.m, 0:k.nb * 64]).then_inc(k.scattered_in[j], 16)
                pool.dma_start(k.scattered[j][N:N + P, :], k.acc[:, 0:64]).then_inc(k.scattered_in[j], 16)
                pool.dma_start(k.scattered[j][N + P:N + P + 1, :], k.acc[0:1, 0:64]).then_inc(k.scattered_in[j], 16)
            for s in range(SLOTS - 1):
                pool.sem_inc(k.out_free[s], 1)

            def gather(i, r, s):
                pool.wait_ge(k.idx_ready[s], r + 1)
                pool.sem_inc(k.paced, 1)
                for u in range(U):
                    nc.gpsimd.indirect_dma_start(k.rel_rows[:, s, u, :], None, k.rel_embed,
                                                 bass.IndirectOffsetOnAxis(k.typ_slot[:, s, u:u + 1], 0)).then_inc(typed_in[s], 16)

            def scatter(i, r, s):
                pool.wait_ge(k.idx_out[s], r + 1)
                pool.wait_ge(k.out_ready[s], r + 2)
                pool.sem_inc(k.paced, 1)
                for u in range(U):
                    j = u % SCATTERS
                    pool.wait_ge(k.scattered_in[j], 48 + 16 * ((SLOTS * r + s) * (U // SCATTERS) + u // SCATTERS))
                    pool.sem_inc(k.paced, 1)
                    if u == SCATTERS - 1:
                        pool.sem_inc(k.out_free[(s + SLOTS - 1) % SLOTS], 1)
                    nc.gpsimd.indirect_dma_start(k.scattered[j][:, :], bass.IndirectOffsetOnAxis(k.s_idx[:, s, u:u + 1], 0),
                                                 k.s_out[:, s, u, :], None, compute_op=ALU.add).then_inc(k.scattered_in[j], 16)

            def body(i, r):
                for s in range(SLOTS):
                    if not last(i, s, 1):
                        gather(*later(i, r, s, 1))
                    scatter(i, r, s)

            def window(w):
                gather(0, w * k.rounds, 0)
                over_groups(pool, k, w, body)
                for j in range(SCATTERS):
                    pool.wait_ge(k.scattered_in[j], 48 + 16 * (U // SCATTERS) * k.groups * (w + 1))
                pool.sem_inc(k.paced, 1)

            over_windows(pool, k, window)

        @block.scalar
        def _(act):
            for s in range(SLOTS):
                act.sem_inc(k.out_ready[s], 1)

            def index(i, r, s):
                act.wait_ge(k.merged[s], r + 1)
                nc.scalar.copy(k.typ_slot[:, s, :], k.typ[:, bass.ds((SLOTS * i + s) * U, U)]).then_inc(k.idx_ready[s], 1)

            def body(i, r):
                for s in range(SLOTS):
                    if not last(i, s, 2):
                        index(*later(i, r, s, 2))
                    act.wait_ge(k.merged[s], r + 2)
                    act.wait_ge(k.out_free[s], r + 1)
                    nc.scalar.copy(k.s_out[:, s, :, :].rearrange("p u f -> p (u f)"), ps[:, 2 + s % 2, :]).then_inc(k.out_ready[s], 1)

            def window(w):
                index(0, w * k.rounds, 0)
                index(0, w * k.rounds, 1)
                over_groups(act, k, w, body)

            over_windows(act, k, window)

        @block.tensor
        def _(pe):
            for s in range(SLOTS):
                pe.sem_inc(k.merged[s], 1)
                pe.sem_inc(k.from_dst[s], 1)

            def features(i, r, s):
                o = s % 2
                pe.wait_ge(k.loaded[s], 48 * (r + 1))
                pe.wait_ge(k.hot_t_ready[s], r + 1)
                pe.wait_ge(k.msg_done[(s + 2) % SLOTS], r + s // 2 + 1)
                for u in range(U):
                    ins = nc.tensor.matmul(ps[:, o, 64 * u:64 * u + 64], k.s_hot_t[:, o, :, u], k.s_win[:, o, :], start=True, stop=True)
                ins.then_inc(k.from_dst[s], 1)

            def merge(i, r, s):
                o = s % 2
                pe.wait_ge(k.msg_done[s], r + 2)
                pe.wait_ge(k.out_ready[(s + 2) % SLOTS], r + s // 2 + 1)
                for u in range(U):
                    ins = nc.tensor.matmul(ps[:, 2 + o, 64 * u:64 * u + 64], k.s_same[:, o, u, :], k.rel_rows[:, s, u, :], start=True, stop=True)
                ins.then_inc(k.merged[s], 1)

            def body(i, r):
                for s in range(SLOTS):
                    if not last(i, s, 1):
                        features(*later(i, r, s, 1))
                    merge(i, r, s)

            def window(w):
                features(0, w * k.rounds, 0)
                over_groups(pe, k, w, body)

            over_windows(pe, k, window)

        @block.vector
        def _(dve):
            for s in range(SLOTS):
                dve.sem_inc(k.msg_done[s], 1)
                dve.sem_inc(k.same_ready[s], 1)

            dve.wait_ge(k.loaded_rest, 16)
            nc.vector.tensor_copy(k.s_src_f, k.s_src_f.bitcast(I32)).then_inc(k.dve_step, 1)
            nc.vector.tensor_scalar(k.s_before, k.row_f[:, :], k.part_f[:, 0:1], None, ALU.is_lt).then_inc(k.dve_step, 1)
            dve.wait_ge(k.dve_step, 2)
            nc.vector.tensor_scalar(k.s_to, k.s_src_f, float(N + P), float(N), ALU.min, ALU.subtract).then_inc(k.dve_step, 1)
            dve.wait_ge(k.dve_step, 3)
            nc.vector.tensor_scalar(k.s_to, k.s_to, k.part_f[:, 0:1], None, ALU.subtract).then_inc(k.dve_step, 1)
            dve.wait_ge(k.dve_step, 4)

            def prepare(i, r, s):
                o, g = s % 2, SLOTS * i + s
                tiles = bass.ds(g * U, U)
                count = 3 * (SLOTS * r + s)
                dve.wait_ge(k.loaded[s], 48 * (r + 1))
                dve.wait_ge(k.from_dst[(s + 2) % SLOTS], r + s // 2 + 1)
                nc.vector.tensor_scalar(k.s_hot_t[:, o, :, :].rearrange("p e u -> p (e u)"), k.s_dst[:, o, :], k.pos[:, bass.ds(g, 1)], None,
                                        ALU.is_equal).then_inc(k.hot_t_ready[s], 1)
                dve.wait_ge(k.merged[(s + 2) % SLOTS], r + s // 2 + 1)
                nc.vector.tensor_tensor(k.s_same[:, o, :, :], k.s_src[:, o, :, :].rearrange("p e u -> p u e"),
                                        k.s_src_f[:, tiles].unsqueeze(2).to_broadcast([P, U, P]), ALU.is_equal).then_inc(k.same_ready[s], 1)
                dve.wait_ge(k.same_ready[s], r + 2)
                nc.vector.tensor_tensor(k.s_earlier[:, :, :], k.s_same[:, o, :, :], k.s_before.unsqueeze(1).to_broadcast([P, U, P]),
                                        ALU.mult).then_inc(k.repeat_step, 1)
                dve.wait_ge(k.repeat_step, count + 1)
                nc.vector.tensor_reduce(k.s_repeat, k.s_earlier[:, :, :], AX.X, ALU.max).then_inc(k.repeat_step, 1)
                dve.wait_ge(k.repeat_step, count + 2)
                nc.vector.scalar_tensor_tensor(k.s_at, k.s_repeat, 0.0, k.s_to[:, tiles], ALU.is_equal, ALU.mult).then_inc(k.repeat_step, 1)
                dve.wait_ge(k.repeat_step, count + 3)
                dve.wait_ge(k.out_free[s], r + 1)
                nc.vector.tensor_scalar(k.s_idx[:, s, :], k.s_at, k.part_f[:, 0:1], float(N), ALU.add, ALU.add).then_inc(k.idx_out[s], 1)
                dve.wait_ge(k.idx_out[s], r + 1)

            def message(i, r, s):
                o = s % 2
                rows = k.rel_rows[:, s, :, :]
                dve.wait_ge(typed_in[s], 16 * U * (r + 1))
                dve.wait_ge(k.from_dst[s], r + 2)
                nc.vector.tensor_tensor(rows, ps[:, o, :].rearrange("p (u f) -> p u f", u=U), rows, ALU.add).then_inc(k.msg_ready[s], 1)
                dve.wait_ge(k.msg_ready[s], r + 1)
                nc.vector.tensor_tensor(rows, rows, k.s_weight[:, bass.ds((SLOTS * i + s) * U, U)].unsqueeze(2).to_broadcast([P, U, 64]),
                                        ALU.mult).then_inc(k.msg_done[s], 1)

            def body(i, r):
                for s in range(SLOTS):
                    message(i, r, s)
                    if not last(i, s, 1):
                        prepare(*later(i, r, s, 1))

            def window(w):
                nc.vector.scalar_tensor_tensor(k.s_weight, k.rel[:, :], 0.0, k.wgt[:, :], ALU.is_ge, ALU.mult).then_inc(k.dve_step, 1)
                dve.wait_ge(k.dve_step, 2 * w + 5)
                nc.vector.scalar_tensor_tensor(k.s_weight, k.rel[:, :], float(P), k.s_weight, ALU.is_lt, ALU.mult).then_inc(k.dve_step, 1)
                dve.wait_ge(k.dve_step, 2 * w + 6)
                prepare(0, w * k.rounds, 0)
                dve.sem_inc(k.paced, 1)
                over_groups(dve, k, w, body)

            walk_windows(nc, k, dve, window, tables_ready=k.tables_ready, used_up=k.msg_done[SLOTS - 1])


def add_scattered(nc, k):
    loaded, added = phase_sems(nc, k, "tables_loaded", "tables_added")
    halves = k.t[:, :, :], k.acc[0:k.m, 0:k.nb * 64].rearrange("p (b f) -> p b f", b=k.nb)
    with nc.Block() as block:
        @block.sync
        def _(sp):
            for j in range(SCATTERS):
                if j >= 2:
                    sp.wait_ge(added, j - 1)
                if j:
                    sp.wait_ge(loaded, 16 * j)
                sp.dma_start(halves[j % 2], k.scattered[j][0:k.n, :].rearrange("(p b) f -> p b f", b=k.nb)).then_inc(loaded, 16)

        @block.vector
        def _(dve):
            for j in range(SCATTERS):
                dve.wait_ge(loaded, 16 * (j + 1))
                nc.vector.tensor_tensor(k.x[:, :, :], k.x[:, :, :], halves[j % 2], ALU.add).then_inc(added, 1)
                dve.wait_ge(added, j + 1)


def message_tables(nc, k):
    copied, turned, back_copied, multiplied, u_ready, v_ready = phase_sems(nc, k, "tables_copied", "tables_turned", "tables_back_copied", "tables_multiplied", "tables_u_ready", "tables_v_ready")
    u_stored, v_stored, zeroed, zeros_stored = phase_sems(nc, k, "tables_u_stored", "tables_v_stored", "tables_zeroed", "tables_zeros_stored")

    with nc.Block() as block:
        M, C, steps = k.m, KB * k.m, k.nb // KB
        u_psum, v_psum = (k.ps[0:M, bank, :].rearrange("p (b f) -> p b f", b=KB) for bank in (2, 3))

        @block.vector
        def _(dve):
            nc.vector.memset(k.x1[:, 0:P], 0.0).then_inc(zeroed, 1)

            def body(i, first):
                nc.vector.tensor_copy(k.t_rows[:, :, :], k.t[:, bass.ds(i * KB, KB), :]).then_inc(copied, 1)
                dve.wait_ge(multiplied, i + 1)
                if not first:
                    dve.wait_ge(v_stored, 16 * i)
                nc.vector.tensor_tensor(k.v_rows[:, :, :], v_psum, rows_of(k.mb1, M, 128), ALU.add).then_inc(v_ready, 1)

            body(0, True)
            with dve.Fori(1, steps) as i:
                body(i, False)

        @block.tensor
        def _(pe):
            def body(i):
                pe.wait_ge(copied, i + 1)
                pe.sem_inc(k.paced, 1)
                turn_back(nc, k, 1, k.t_rows, 64).then_inc(turned, 1)
                pe.wait_ge(back_copied, i + 1)
                for half, to in enumerate((u_psum, v_psum)):
                    for b in range(KB):
                        ins = nc.tensor.matmul(to[:, b, :], k.back[0:64, M * b:M * b + M], k.w_uv[:, P * half:P * half + P], start=True, stop=True)
                ins.then_inc(multiplied, 1)

            body(0)
            with pe.Fori(1, steps) as i:
                pe.wait_ge(u_ready, i)
                pe.wait_ge(v_ready, i)
                body(i)

        @block.scalar
        def _(act):
            def body(i, first):
                act.wait_ge(turned, i + 1)
                nc.scalar.copy(k.back[0:64, :], k.ps[0:64, 1, 0:C]).then_inc(back_copied, 1)
                act.wait_ge(multiplied, i + 1)
                if not first:
                    act.wait_ge(u_stored, 16 * i)
                nc.scalar.copy(k.u_rows[:, :, :], u_psum).then_inc(u_ready, 1)

            body(0, True)
            with act.Fori(1, steps) as i:
                body(i, False)

        @block.sync
        def _(sp):
            sp.wait_ge(zeroed, 1)
            sp.dma_start(k.v_table[k.n:k.n + P, :], k.x1[:, 0:P]).then_inc(zeros_stored, 16)
            with sp.Fori(0, steps) as i:
                for table, rows, ready, stored in ((k.u_table, k.u_rows, u_ready, u_stored), (k.v_table, k.v_rows, v_ready, v_stored)):
                    sp.wait_ge(ready, i + 1)
                    sp.dma_start(table[0:k.n, :].rearrange("(p b) f -> p b f", b=k.nb)[:, bass.ds(i * KB, KB), :],
                                 rows[:, :, :]).then_inc(stored, 16)
            sp.wait_ge(u_stored, 16 * steps)
            sp.wait_ge(v_stored, 16 * steps)
            sp.wait_ge(zeros_stored, 16)


def sum_messages(nc, k, edge_attr, dst):
    clear(nc, k)
    gathered = k.gather_sems.pop()
    with nc.Block() as block:
        u_rows, dst_b, ea, ea_t, v_win, hot_t, relu, ps = k.m_u, k.m_dst, k.m_ea, k.m_ea_t, k.m_v, k.m_hot_t, k.m_relu, k.ps
        pre = lambda o, h: ps[:, 2 * o + h, :]
        full = (k.groups - 1) * GE
        H = U // 2

        def later(i, r, s, by):
            return i + (s + by) // SLOTS, r + (s + by) // SLOTS, (s + by) % SLOTS

        def last(i, s, by):
            return isinstance(i, int) and i == k.rounds - 1 and s + by >= SLOTS

        @block.sync
        def _(sp):
            def body(i, r, w=None):
                for s in range(SLOTS):
                    o = s % 2
                    g = SLOTS * i + s
                    sp.wait_ge(k.pre_done[(s + 2) % SLOTS], r + s // 2 + 1)
                    sp.sem_inc(k.paced, 1)
                    base = sp.value_load(k.base_i[0:1, bass.ds(g, 1)], min_val=0, max_val=k.n - 1)
                    if s == SLOTS - 1 and isinstance(i, int) and i == k.rounds - 1:
                        rest = k.e - full
                        parts = [(dst_b[:, o, 0:rest], dst[full:k.e].rearrange("(a n) -> a n", a=1).to_broadcast([P, rest]))]
                        whole, odd = divmod(rest, U)
                        if whole:
                            parts.append((ea[0:whole, o, :], edge_attr[full:full + whole * U, :].rearrange("(p u) f -> p (u f)", u=U)))
                        if odd:
                            parts.append((ea[whole:whole + 1, o, 0:odd * 32], edge_attr[k.e - odd:k.e, :].rearrange("(a u) f -> a (u f)", a=1)))
                        else:
                            parts.append((ea[0:1, o, 0:32], edge_attr[full:full + 1, :]))
                        assert len(parts) == 3
                        first, more = parts[0:2], parts[2]
                    else:
                        first = [(dst_b[:, o, :], dst[bass.ds(g * GE, GE)].rearrange("(a n) -> a n", a=1).to_broadcast([P, GE])),
                                 (ea[:, o, :], edge_attr[bass.ds(g * GE, GE), :].rearrange("(p u) f -> p (u f)", u=U))]
                        more = None
                    for to, of in first + [(v_win[:, o, :], k.v_table[bass.ds(base, P), :])]:
                        sp.dma_start(to, of).then_inc(k.loaded[s], 16)
                    if more:
                        sp.dma_start(*more).then_inc(k.loaded_rest, 16)

            def window(w):
                over_groups(sp, k, w, body)
                sp.wait_ge(k.loaded_rest, 16 * (w + 1))
                sp.sem_inc(k.loads_issued, 1)

            def between(w):
                sp.wait_ge(k.tables_ready, w)
                sp.sem_inc(k.paced, 1)

            over_windows(sp, k, window, between)

        @block.gpsimd
        def _(pool):
            def body(i, r):
                for s in range(SLOTS):
                    pool.wait_ge(k.idx_ready[s], r + 1)
                    pool.sem_inc(k.paced, 1)
                    for u in range(U):
                        nc.gpsimd.indirect_dma_start(u_rows[:, s, u, :], None, k.u_table[:, :],
                                                     bass.IndirectOffsetOnAxis(k.idx_slot[:, s, u:u + 1], 0)).then_inc(gathered[s], 16)

            over_windows(pool, k, lambda w: over_groups(pool, k, w, body))

        @block.scalar
        def _(act):
            def index(i, r, s):
                act.wait_ge(k.summed_half[s], 2 * r + 2)
                nc.scalar.copy(k.idx_slot[:, s, :], k.idx[:, bass.ds((SLOTS * i + s) * U, U)]).then_inc(k.idx_ready[s], 1)

            def features(i, r, s):
                act.wait_ge(k.ea_turned[s], r + 1)
                nc.scalar.copy(ea_t[:, s % 2, :], ps[:, 6, 0:2 * P]).then_inc(k.ea_ready[s], 1)

            def body(i, r):
                for s in range(SLOTS):
                    if not last(i, s, 1):
                        features(*later(i, r, s, 1))
                    for h in range(2):
                        act.wait_ge(k.summed_half[s], 2 * r + 3 + h)
                        half = relu[:, s % 2, h * H:h * H + H, :]
                        nc.scalar.activation(half, half, ACT.Relu).then_inc(k.relued[s], 1)
                    if not last(i, s, 2):
                        index(*later(i, r, s, 2))

            def window(w):
                index(0, w * k.rounds, 0)
                index(0, w * k.rounds, 1)
                features(0, w * k.rounds, 0)
                over_groups(act, k, w, body)

            over_windows(act, k, window)

        @block.tensor
        def _(pe):
            for s in range(SLOTS):
                pe.sem_inc(k.group_done[s], 1)
                pe.sem_inc(k.pre_done[s], 1)

            def before_relu(i, r, s):
                o = s % 2
                pe.wait_ge(k.loaded[s], 48 * (r + 1))
                if last(i, s, 1):
                    pe.wait_ge(k.loaded_rest, 16 * (pe_window[0] + 1))
                for h in range(2):
                    ins = nc.tensor.transpose(ps[:, 6, P * h:P * h + P], ea[:, o, P * h:P * h + P], k.ident[:, :])
                ins.then_inc(k.ea_turned[s], 1)
                pe.wait_ge(k.ea_ready[s], r + 1)
                pe.wait_ge(k.summed_half[(s + 2) % SLOTS], 2 * (r + s // 2) + 2)
                pe.wait_ge(k.hot_t_ready[s], r + 1)
                for h in range(2):
                    nc.tensor.matmul(pre(o, h), ea_t[:, o, P * h:P * h + P], k.we[:, :], start=True, stop=False, skip_group_check=True)
                    for q in range(H):
                        ins = nc.tensor.matmul(pre(o, h)[:, P * q:P * q + P], hot_t[:, o, :, h * H + q], v_win[:, o, :],
                                               start=False, stop=q == H - 1, skip_group_check=True)
                    ins.then_inc(k.pre_half[s] if h == 0 else k.pre_done[s], 1)

            def sums(i, r, s):
                o = s % 2
                pe.wait_ge(k.relued[s], 2 * (r + 1))
                pe.wait_ge(k.hot_ready[s], r + 1)
                pe.wait_ge(k.summed[(s + 2) % SLOTS], r + s // 2 + 1)
                for u in range(U):
                    ins = nc.tensor.matmul(ps[:, 4 + o, 0:P], relu[:, o, u, :], k.one_hot[:, o, u, :], start=u == 0, stop=u == U - 1)
                ins.then_inc(k.group_done[s], 1)

            def body(i, r):
                for s in range(SLOTS):
                    if not last(i, s, 1):
                        before_relu(*later(i, r, s, 1))
                    sums(i, r, s)

            pe_window = [0]

            def window(w):
                pe_window[0] = w
                before_relu(0, w * k.rounds, 0)
                over_groups(pe, k, w, body)

            over_windows(pe, k, window)

        @block.vector
        def _(dve):
            for s in range(SLOTS):
                dve.sem_inc(k.summed[s], 1)
                dve.sem_inc(k.summed_half[s], 2)

            def one_hots(i, r, s):
                o, g = s % 2, SLOTS * i + s
                dve.wait_ge(k.loaded[s], 48 * (r + 1))
                dve.wait_ge(k.pre_done[(s + 2) % SLOTS], r + s // 2 + 1)
                dve.wait_ge(k.group_done[(s + 2) % SLOTS], r + s // 2 + 1)
                nc.vector.tensor_scalar(hot_t[:, o, :, :].rearrange("p e u -> p (e u)"), dst_b[:, o, :], k.pos[:, bass.ds(g, 1)], None,
                                        ALU.is_equal).then_inc(k.hot_t_ready[s], 1)
                one_hot(nc, k, g, o).then_inc(k.hot_ready[s], 1)

            def add_up(i, r, s):
                o = s % 2
                dve.wait_ge(gathered[s], 16 * U * (r + 1))
                dve.wait_ge(k.group_done[(s + 2) % SLOTS], r + s // 2 + 1)
                for h in range(2):
                    dve.wait_ge(k.pre_half[s] if h == 0 else k.pre_done[s], r + 1 + h)
                    nc.vector.tensor_tensor(relu[:, o, h * H:h * H + H, :], pre(o, h).rearrange("p (q f) -> p q f", q=H),
                                            u_rows[:, s, h * H:h * H + H, :], ALU.add).then_inc(k.summed_half[s], 1)

            def add_sums(i, r, s):
                base = dve.value_load(k.base_i[0:1, bass.ds(SLOTS * i + s, 1)], min_val=0, max_val=k.n - 1)
                dve.wait_ge(k.group_done[s], r + 2)
                dve.wait_ge(k.summed[(s + 3) % SLOTS], r + (s > 0) + 1)
                at = k.acc[:, bass.ds(base, P)]
                nc.vector.tensor_tensor(at, at, ps[:, 4 + s % 2, 0:P], ALU.add).then_inc(k.summed[s], 1)

            def body(i, r):
                for s in range(SLOTS):
                    add_up(i, r, s)
                    if s > 0:
                        add_sums(i, r, s - 1)
                    if not last(i, s, 1):
                        one_hots(*later(i, r, s, 1))
                add_sums(i, r, SLOTS - 1)

            def window(w):
                one_hots(0, w * k.rounds, 0)
                over_groups(dve, k, w, body)

            walk_windows(nc, k, dve, window, tables_ready=k.tables_ready)


def update_nodes(nc, k, out):
    staged, mixed, turned, back_copied = phase_sems(nc, k, "update_staged", "update_mixed", "update_turned", "update_back_copied")
    hidden, relued, out_ready, step, stored = phase_sems(nc, k, "update_hidden", "update_relued", "update_out_ready", "update_step", "update_stored")

    with nc.Block() as block:
        M, C, steps = k.m, KB * k.m, k.nb // KB
        agg = k.ps[0:M, 0, 0:KB * 64].rearrange("p (b f) -> p b f", b=KB)
        out_psum = k.ps[0:M, 3, 0:KB * 64].rearrange("p (b f) -> p b f", b=KB)
        per = 5

        @block.scalar
        def _(act):
            with act.Fori(0, steps) as i:
                stage_acc(nc, k, P, i).then_inc(staged, 1)
                act.wait_ge(turned, i + 1)
                nc.scalar.copy(k.back[:, :], k.ps[:, 1, 0:C]).then_inc(back_copied, 1)
                act.wait_ge(hidden, i + 1)
                nc.scalar.activation(k.hid[:, :], k.ps[:, 2, 0:C], ACT.Relu, bias=k.ub1[:, 0:1]).then_inc(relued, 1)

        @block.tensor
        def _(pe):
            def body(i):
                pe.wait_ge(staged, i + 1)
                for b in range(KB):
                    ins = nc.tensor.matmul(agg[:, b, :], k.stage[:, b, :], k.mw2[:, :], start=True, stop=True)
                ins.then_inc(mixed, 1)
                pe.wait_ge(step, per * i + 3)
                pe.sem_inc(k.paced, 1)
                turn_back(nc, k, 1, k.v_rows, P).then_inc(turned, 1)
                pe.wait_ge(back_copied, i + 1)
                nc.tensor.matmul(k.ps[:, 2, 0:C], k.uw1[:, :], k.back[:, :], start=True, stop=True).then_inc(hidden, 1)
                pe.wait_ge(relued, i + 1)
                for b in range(KB):
                    ins = nc.tensor.matmul(out_psum[:, b, :], k.hid[:, M * b:M * b + M], k.uw2[:, :], start=True, stop=True)
                ins.then_inc(out_ready, 1)

            body(0)
            with pe.Fori(1, steps) as i:
                pe.wait_ge(step, per * i)
                body(i)

        @block.vector
        def _(dve):
            with dve.Fori(0, steps) as i:
                then, at = Chain(dve, step, i, per), bass.ds(i * KB, KB)
                then(nc.vector.tensor_tensor(k.v_rows[:, :, 64:128], rows_of(k.mb2, M, 64), blocks(k.deg_d, at, M, 64), ALU.mult))
                then(nc.vector.tensor_copy(k.v_rows[:, :, 0:64], k.t[:, at, :]))
                dve.wait_ge(mixed, i + 1)
                then(nc.vector.tensor_tensor(k.v_rows[:, :, 64:128], k.v_rows[:, :, 64:128], agg, ALU.add))
                then(nc.vector.tensor_tensor(k.x[:, at, :], k.x[:, at, :], rows_of(k.ub2, M, 64), ALU.add))
                dve.wait_ge(out_ready, i + 1)
                then(nc.vector.tensor_tensor(k.x[:, at, :], k.x[:, at, :], out_psum, ALU.add))
                then.end()

        @block.sync
        def _(sp):
            sp.wait_ge(step, per * steps)
            sp.dma_start(out.rearrange("(p b) f -> p b f", b=k.nb), k.x[:, :, :]).then_inc(stored, 16)
            sp.wait_ge(stored, 16)


def bass_four_graph_layers(
        nc, x, src, dst, edge_attr_32, edge_type_500, edge_weight, L0_gnn_adaptive_weight,
        L1_gnn_W1, L1_gnn_b1, L1_gnn_W2, L1_gnn_b2, L1_gnn_W3, L1_gnn_b3, L1_gnn_W4, L1_gnn_b4,
        L2_gnn_rel_embed, L3_gnn_mW1, L3_gnn_mb1, L3_gnn_mW2, L3_gnn_mb2,
        L3_gnn_uW1, L3_gnn_ub1, L3_gnn_uW2, L3_gnn_ub2, out):
    a = Names()
    a.x = x
    a.src = src
    a.dst = dst
    a.edge_attr_32 = edge_attr_32
    a.edge_type_500 = edge_type_500
    a.edge_weight = edge_weight
    a.L0_gnn_adaptive_weight = L0_gnn_adaptive_weight
    a.L1_gnn_W1 = L1_gnn_W1
    a.L1_gnn_b1 = L1_gnn_b1
    a.L1_gnn_W2 = L1_gnn_W2
    a.L1_gnn_b2 = L1_gnn_b2
    a.L1_gnn_W3 = L1_gnn_W3
    a.L1_gnn_b3 = L1_gnn_b3
    a.L1_gnn_W4 = L1_gnn_W4
    a.L1_gnn_b4 = L1_gnn_b4
    a.L2_gnn_rel_embed = L2_gnn_rel_embed
    a.L3_gnn_mW1 = L3_gnn_mW1
    a.L3_gnn_mb1 = L3_gnn_mb1
    a.L3_gnn_mW2 = L3_gnn_mW2
    a.L3_gnn_mb2 = L3_gnn_mb2
    a.L3_gnn_uW1 = L3_gnn_uW1
    a.L3_gnn_ub1 = L3_gnn_ub1
    a.L3_gnn_uW2 = L3_gnn_uW2
    a.L3_gnn_ub2 = L3_gnn_ub2
    n = a.x.shape[0]
    e = a.src.shape[0]
    m = 125
    nb = n // m
    groups = -(-e // GE)
    assert n % m == 0 and nb % KB == 0 and groups % SLOTS == 0 and m <= P and nb <= P
    tiles = groups * U
    k = Names()
    k.n, k.e, k.m, k.nb, k.groups, k.rounds, k.windows = n, e, m, nb, groups, groups // SLOTS, -(-n // P)

    k.table = nc.dram_tensor("table", [n + P, 64], F32)
    k.edge_pad = [nc.dram_tensor(name, [groups * GE], I32) for name in ("src_pad", "dst_pad")]
    k.scattered = [nc.dram_tensor(f"scattered_{j}", [n + P + 1, 64], F32) for j in range(SCATTERS)]
    k.table_rows = k.table[0:n, :].rearrange("(p b) f -> p b f", b=nb)
    k.u_table = nc.dram_tensor("u_table", [n, P], F32)
    k.v_table = nc.dram_tensor("v_table", [n + P, P], F32)
    k.rel_embed = a.L2_gnn_rel_embed

    with ExitStack() as ctx:
        sb = lambda name, shape, dt=F32: ctx.enter_context(nc.sbuf_tensor(name, shape, dt))
        k.x, k.t = sb("x", [m, nb, 64]), sb("t", [m, nb, 64])
        k.acc = sb("acc", [P, max(n + P, 2 * P * U, nb * 64 + 3 * tiles + P)])
        k.x1 = sb("x1", [P, max(n, 12288, 6 * tiles)])
        k.idx, k.typ = sb("idx", [P, tiles], I32), sb("typ", [P, tiles], I32)
        k.wgt, k.rel = sb("wgt", [P, tiles]), sb("rel", [P, tiles])
        k.base, k.pos = sb("base", [P, 2 * groups]), sb("pos", [P, groups])
        k.base_i = sb("base_i", [P, groups], I32)
        k.spread_f, k.spread_i = sb("spread_f", [P, 1]), sb("spread_i", [P, 1], I32)
        k.row_f, k.part_f, k.ident = sb("row_f", [P, P]), sb("part_f", [P, 1]), sb("ident", [P, P])
        k.part_i = sb("part_i", [P, 1], I32)
        k.deg_s, k.deg_d, k.inv_s, k.inv_d = (sb(s, [m, nb]) for s in ("deg_s", "deg_d", "inv_s", "inv_d"))
        k.mean, k.var = sb("mean", [m, nb]), sb("var", [m, nb])
        k.w1, k.w2, k.w3, k.w4 = sb("w1", [64, P]), sb("w2", [P, 64]), sb("w3", [64, P]), sb("w4", [P, 64])
        k.b1, k.b2, k.b3, k.b4 = sb("b1", [P, 1]), sb("b2", [P, 64]), sb("b3", [P, 1]), sb("b4", [P, 64])
        k.w_uv, k.we, k.mb1 = sb("w_uv", [64, 2 * P]), sb("we", [P, 4 * P]), sb("mb1", [P, P])
        k.mw2, k.mb2 = sb("mw2", [P, 64]), sb("mb2", [P, 64])
        k.uw1, k.ub1, k.uw2, k.ub2 = sb("uw1", [P, P]), sb("ub1", [P, 1]), sb("uw2", [P, 64]), sb("ub2", [P, 64])
        k.adapt = sb("adapt", [P, 1])
        k.idx_slot, k.typ_slot = sb("idx_slot", [P, SLOTS, U], I32), sb("typ_slot", [P, SLOTS, U], I32)
        work = sb("work", [P, max(2 * U * P, 4 * KB * P)])
        k.one_hot = work[:, 0:2 * U * P].rearrange("p (o u n) -> p o u n", o=2, u=U)
        cut = lambda v, at, size: v[:, at:at + size]
        k.stage = cut(work, 0, KB * m).rearrange("p (b n) -> p b n", b=KB)
        k.back = cut(work, KB * P, KB * m)
        k.hid = cut(work, 2 * KB * P, KB * m)
        k.kept = cut(work, 3 * KB * P, KB * m)
        more = sb("more", [P, SLOTS * U * 65])
        k.rows = more[:, :].rearrange("p (s u f) -> p s u f", s=SLOTS, u=U)
        k.t_rows = more[0:m, 0:KB * 64].rearrange("p (b f) -> p b f", b=KB)
        k.sums = more[0:m, 256:256 + KB * 64].rearrange("p (b f) -> p b f", b=KB)
        k.u_rows = more[0:m, 512:512 + KB * P].rearrange("p (b f) -> p b f", b=KB)
        k.v_rows = more[0:m, 1024:1024 + KB * P].rearrange("p (b f) -> p b f", b=KB)
        k.ends = more[:, 0:2 * groups]
        k.row_i = more[:, 2 * groups:2 * groups + P].bitcast(I32)
        k.fill = work[:, 0:GE].bitcast(I32)
        k.src_i, k.dst_i = cut(k.x1, 0, tiles).bitcast(I32), cut(k.x1, tiles, tiles).bitcast(I32)
        k.src_f, k.dst_f, k.src_hi, k.src_lo = (cut(k.x1, j * tiles, tiles) for j in range(2, 6))
        k.rel_rows = cut(k.x1, 0, SLOTS * U * 64).rearrange("p (s u f) -> p s u f", s=SLOTS, u=U)
        k.s_src = cut(k.x1, 2048, 2048).bitcast(I32).rearrange("p (o e u) -> p o e u", o=2, u=U)
        k.s_dst = cut(k.x1, 4096, 2048).bitcast(I32).rearrange("p (o e) -> p o e", o=2)
        k.s_hot_t = cut(k.x1, 6144, 2048).rearrange("p (o e u) -> p o e u", o=2, u=U)
        k.s_same = cut(k.x1, 8192, 2048).rearrange("p (o u e) -> p o u e", o=2, u=U)
        k.s_earlier = cut(k.x1, 10240, 1024).rearrange("p (u e) -> p u e", u=U)
        k.s_win = cut(k.x1, 11264, 128).rearrange("p (o f) -> p o f", o=2)
        k.s_repeat, k.s_at = cut(k.x1, 11392, U), cut(k.x1, 11392 + U, U)
        k.s_idx = cut(k.x1, 11392 + 2 * U, SLOTS * U).bitcast(I32).rearrange("p (s u) -> p s u", s=SLOTS)
        k.s_out = work[:, 0:SLOTS * U * 64].rearrange("p (s u f) -> p s u f", s=SLOTS, u=U)
        k.s_src_f, k.s_to, k.s_weight = (cut(k.acc, nb * 64 + j * tiles, tiles) for j in range(3))
        k.s_before = cut(k.acc, nb * 64 + 3 * tiles, P)
        k.m_u = cut(k.x1, 0, 4096).rearrange("p (s u f) -> p s u f", s=SLOTS, u=U)
        k.m_hot_t = cut(k.x1, 4096, 2048).rearrange("p (o e u) -> p o e u", o=2, u=U)
        k.m_dst = cut(k.x1, 6144, 2048).bitcast(I32).rearrange("p (o e) -> p o e", o=2)
        k.m_ea = cut(k.x1, 8192, 512).rearrange("p (o c) -> p o c", o=2)
        k.m_ea_t = cut(k.x1, 8704, 512).rearrange("p (o c) -> p o c", o=2)
        k.m_v = cut(k.x1, 9216, 256).rearrange("p (o c) -> p o c", o=2)
        k.m_relu = cut(k.x1, 9472, 2048).rearrange("p (o u f) -> p o u f", o=2, u=U)
        k.ps = ctx.enter_context(nc.psum_tensor("ps", [P, 8, 512], F32))

        k.gather_sems = [[ctx.enter_context(nc.semaphore(f"gathered_{j}_{s}")) for s in range(SLOTS)] for j in range(7)]
        k.scattered_in = [ctx.enter_context(nc.semaphore(f"scattered_in_{j}")) for j in range(SCATTERS)]
        k.pass_sems, k.phase_sems, k.open_phases = [], [], ctx.enter_context(ExitStack())

        def sem(name):
            k.pass_sems.append(ctx.enter_context(nc.semaphore(name)))
            return k.pass_sems[-1]

        slots = lambda name: [sem(f"{name}_{s}") for s in range(SLOTS)]
        k.same_ready = slots("same_ready")
        k.idx_out = slots("idx_out")
        k.msg_done = slots("msg_done")
        k.from_dst = slots("from_dst")
        k.merged = slots("merged")
        k.out_ready = slots("out_ready")
        k.out_free = slots("out_free")
        k.idx_ready = slots("idx_ready")
        k.group_done = slots("group_done")
        k.summed = slots("summed")
        k.hot_ready = slots("hot_ready")
        k.msg_ready = slots("msg_ready")
        k.loaded = slots("loaded")
        k.pre_half = slots("pre_half")
        k.pre_done = slots("pre_done")
        k.ea_turned = slots("ea_turned")
        k.ea_ready = slots("ea_ready")
        k.hot_t_ready = slots("hot_t_ready")
        k.summed_half = slots("summed_half")
        k.relued = slots("relued")
        k.paced = sem("paced")
        k.dve_step = sem("dve_step")
        k.repeat_step = sem("repeat_step")
        k.table_step = sem("table_step")
        k.tables_ready = sem("tables_ready")
        k.loads_issued = sem("loads_issued")
        k.loaded_rest = sem("loaded_rest")

        load_and_index(nc, k, a)
        count_src(nc, k)
        norm_relu(nc, k, "norm0", scale=k.inv_s, add_to_x=True, clear_acc=True, ones=True)
        sum_by_dst(nc, k, k.table[0:n, :], 65)
        add_adaptive_sum(nc, k)
        norm_relu(nc, k, "norm1", scale=k.inv_d, add_to_x=True, inv_from=k.deg_d)
        start_acc(nc, k)
        sum_by_dst(nc, k, k.table[0:n, :], 64)
        convolve_wide(nc, k, "first", k.w1, k.b1, k.w2, residual=False)
        sum_by_dst(nc, k, k.table[0:n, :], 64)
        convolve_second(nc, k)
        sum_by_dst(nc, k, k.table[0:n, :], 64)
        convolve_wide(nc, k, "third", k.w3, k.b3, k.w4, residual=True)
        sum_by_dst(nc, k, k.table[0:n, :], 64)
        add_fourth(nc, k)
        norm_relu(nc, k, "norm2", clear_acc=True)
        scatter_to_src(nc, k)
        add_scattered(nc, k)
        norm_relu(nc, k, "norm3", clear_acc=True)
        message_tables(nc, k)
        sum_messages(nc, k, a.edge_attr_32, a.dst)
        update_nodes(nc, k, out)


_INS = ["x", "src", "dst", "edge_attr_32", "edge_type_500", "edge_weight", "L0_gnn_adaptive_weight",
        "L1_gnn_W1", "L1_gnn_b1", "L1_gnn_W2", "L1_gnn_b2", "L1_gnn_W3", "L1_gnn_b3", "L1_gnn_W4", "L1_gnn_b4",
        "L2_gnn_rel_embed", "L3_gnn_mW1", "L3_gnn_mb1", "L3_gnn_mW2", "L3_gnn_mb2",
        "L3_gnn_uW1", "L3_gnn_ub1", "L3_gnn_uW2", "L3_gnn_ub2"]


def kernel(**inputs):
    import numpy as _np
    import concourse.bacc as _bacc
    from concourse import mybir as _mybir
    from concourse.bass_utils import run_bass_kernel_spmd as _run

    nc = _bacc.Bacc("TRN2", target_bir_lowering=False, num_devices=1)
    arrays, args = {}, []
    for name in _INS:
        v = _np.ascontiguousarray(inputs[name])
        arrays[f"in_{name}"] = v
        args.append(nc.dram_tensor(f"in_{name}", v.shape, _mybir.dt.from_np(v.dtype), kind="ExternalInput").ap())
    out = nc.dram_tensor("out_x", arrays["in_x"].shape, _mybir.dt.float32, kind="ExternalOutput").ap()
    bass_four_graph_layers(nc, *args, out)
    return _run(nc, [arrays], core_ids=[0]).results[0]["out_x"]
```

```python
from contextlib import ExitStack

import concourse.bass as bass
from concourse import mybir

F32, I32, BF16, F16 = mybir.dt.float32, mybir.dt.int32, mybir.dt.bfloat16, mybir.dt.float16
ALU = mybir.AluOpType
ACT = mybir.ActivationFunctionType
AX = mybir.AxisListType

P = 128
U = 8
GE = P * U
SLOTS = 4
PADDED = 65536
ROUND = 12582912.0
EPS = 1e-5
SCATTERS = U
KB = 4


class Names:
    pass


def feature_major(acc, rows, n, nb):
    return acc[0:rows, 0:n].rearrange("f (p b) -> f b p", b=nb)




def over_windows(eng, k, window, between=None):
    window(0)
    spread = eng.value_load(k.spread_i[0:1, 0:1], min_val=0, max_val=1)
    with eng.If(spread):
        with eng.Fori(1, k.windows) as w:
            if between:
                between(w)
            window(w)


def over_groups(eng, k, w, body):
    if k.rounds > 1:
        with eng.Fori(0, k.rounds - 1) as i:
            body(i, w * k.rounds + i)
    body(k.rounds - 1, w * k.rounds + (k.rounds - 1))


def phase_sems(nc, k, *names):
    made = [k.open_phases.enter_context(nc.semaphore(name)) for name in names]
    k.phase_sems += made
    return made


def clear(nc, k):
    nc.all_engine_barrier()
    first = None
    nums = sorted(s.num for s in k.pass_sems + k.phase_sems)
    for at, num in enumerate(nums):
        first = num if first is None else first
        if at == len(nums) - 1 or nums[at + 1] != num + 1:
            nc.gpsimd.sem_clear(range(first, num + 1))
            first = None
    nc.all_engine_barrier()
    k.open_phases.close()
    k.phase_sems = []


def edge_parts(k, tile, dram):
    full = (k.groups - 1) * GE
    whole, rest = divmod(k.e - full, U)
    parts = [(tile[:, 0:(k.groups - 1) * U].rearrange("p (g u) -> p g u", u=U),
              dram[0:full].rearrange("(g p u) -> p g u", p=P, u=U))]
    last = tile[:, (k.groups - 1) * U:k.groups * U]
    if whole:
        parts.append((last[0:whole, :], dram[full:full + whole * U].rearrange("(p u) -> p u", u=U)))
    if rest:
        parts.append((last[whole:whole + 1, 0:rest], dram[k.e - rest:k.e].rearrange("(a u) -> a u", a=1)))
    return parts


def load_and_index(nc, k, a):
    pads_set, edges_loaded, rest_loaded = phase_sems(nc, k, "pads_set", "edges_loaded", "rest_loaded")
    iota_made, extremes, reduced, step = phase_sems(nc, k, "iota_made", "extremes", "reduced", "index_step")
    zeroed, pads_ready = phase_sems(nc, k, "we_zeroed", "pads_ready")

    with nc.Block() as block:
        src_i, dst_i, src_f, dst_f = k.src_i, k.dst_i, k.src_f, k.dst_f
        G = k.groups

        edge = [(t, d) for tile, dram in ((src_i, a.src), (dst_i, a.dst), (k.wgt, a.edge_weight))
                for t, d in edge_parts(k, tile, dram)]
        row = lambda v, n: v.rearrange("(a n) -> a n", a=1).to_broadcast([n, v.shape[0]])
        col = lambda v: v.rearrange("(n a) -> n a", a=1)
        rest = [(k.x[:, :, :], a.x.rearrange("(p b) f -> p b f", b=k.nb)),
                (k.w1[:, :], a.L1_gnn_W1), (k.w2[:, :], a.L1_gnn_W2), (k.w3[:, :], a.L1_gnn_W3), (k.w4[:, :], a.L1_gnn_W4),
                (k.b1[:, :], col(a.L1_gnn_b1)), (k.b3[:, :], col(a.L1_gnn_b3)),
                (k.b2[:, :], row(a.L1_gnn_b2, P)), (k.b4[:, :], row(a.L1_gnn_b4, P)),
                (k.w_uv[:, 0:128], a.L3_gnn_mW1[0:64, :]), (k.w_uv[:, 128:256], a.L3_gnn_mW1[64:128, :]),
                (k.mb1[:, :], row(a.L3_gnn_mb1, P)), (k.mw2[:, :], a.L3_gnn_mW2), (k.mb2[:, :], row(a.L3_gnn_mb2, P)),
                (k.uw1[:, :], a.L3_gnn_uW1), (k.ub1[:, :], col(a.L3_gnn_ub1)), (k.uw2[:, :], a.L3_gnn_uW2),
                (k.ub2[:, :], row(a.L3_gnn_ub2, P)),
                (k.adapt[:, :], row(a.L0_gnn_adaptive_weight, P))]
        diag = [(k.we[32 * q:32 * q + 32, 128 * q:128 * q + 128], a.L3_gnn_mW1[128:160, :]) for q in range(4)]

        @block.sync
        def _(sp):
            sp.wait_ge(pads_set, 1)
            for to, of in edge:
                sp.dma_start(to, of).then_inc(edges_loaded, 16)
            for to, of in rest:
                sp.dma_start(to, of).then_inc(rest_loaded, 16)
            sp.wait_ge(pads_ready, 1)
            fill = k.groups * GE - k.e
            stored = 7 + 3 * SCATTERS
            sp.wait_ge(zeroed, 3)
            fills = k.fill[0:1, 0:fill], k.fill[0:1, 0:fill], k.acc[0:1, 0:fill].bitcast(I32)
            for pad, of, with_ in zip(k.edge_pad, (a.src, a.dst, a.edge_type_500), fills):
                sp.dma_start(pad[0:k.e].rearrange("(p n) -> p n", p=4), of.rearrange("(p n) -> p n", p=4)).then_inc(rest_loaded, 16)
                sp.dma_start(pad[k.e:k.e + fill].rearrange("(a n) -> a n", a=1), with_).then_inc(rest_loaded, 16)
            sp.dma_start(k.table[k.n:k.n + P, :], k.zeros[:, :]).then_inc(rest_loaded, 16)
            for j in range(SCATTERS):
                sp.dma_start(k.scattered[j][0:k.n, :].rearrange("(p b) f -> p (b f)", b=k.nb), k.acc[0:k.m, 0:k.nb * 64]).then_inc(rest_loaded, 16)
                sp.dma_start(k.scattered[j][k.n:k.n + P, :], k.zeros[:, :]).then_inc(rest_loaded, 16)
                sp.dma_start(k.scattered[j][k.n + P:k.n + P + 1, :], k.zeros[0:1, :]).then_inc(rest_loaded, 16)
            sp.wait_ge(rest_loaded, 16 * (len(rest) + stored))
            for to, of in diag:
                sp.dma_start(to, of).then_inc(rest_loaded, 16)
            sp.wait_ge(rest_loaded, 16 * (len(rest) + stored + len(diag)))

        @block.gpsimd
        def _(pool):
            nc.gpsimd.iota(k.row_i[:, :], pattern=[[1, P]], base=0, channel_multiplier=0).then_inc(iota_made, 1)
            nc.gpsimd.iota(k.part_i[:, :], pattern=[[0, 1]], base=0, channel_multiplier=1).then_inc(iota_made, 1)
            pool.wait_ge(extremes, 1)
            nc.gpsimd.partition_all_reduce(k.base[:, 0:2 * G], k.ends[:, 0:2 * G], P, bass.bass_isa.ReduceOp.max).then_inc(reduced, 1)

        @block.vector
        def _(dve):
            done = [0]

            def then(ins):
                done[0] += 1
                ins.then_inc(step, 1)
                dve.wait_ge(step, done[0])

            last = slice((G - 1) * U, G * U)
            then(nc.vector.memset(src_i[:, last], PADDED))
            then(nc.vector.memset(dst_i[:, last], PADDED))
            nc.vector.memset(k.wgt[:, last], 0.0).then_inc(pads_set, 1)
            nc.vector.memset(k.fill[0:1, :], PADDED).then_inc(pads_ready, 1)
            nc.vector.memset(k.we[:, :], 0.0).then_inc(zeroed, 1)
            nc.vector.memset(k.zeros[:, :], 0.0).then_inc(zeroed, 1)
            nc.vector.memset(k.acc[0:k.m, 0:max(k.nb * 64, GE)], 0.0).then_inc(zeroed, 1)
            dve.wait_ge(iota_made, 2)
            then(nc.vector.tensor_copy(k.row_f[:, :], k.row_i[:, :]))
            then(nc.vector.tensor_copy(k.part_f[:, :], k.part_i[:, :]))
            then(nc.vector.tensor_scalar(k.ident[:, :], k.row_f[:, :], k.part_f[:, 0:1], None, ALU.is_equal))
            dve.wait_ge(edges_loaded, 16 * len(edge))
            then(nc.vector.tensor_copy(src_f[:, :], src_i[:, :]))
            then(nc.vector.tensor_copy(dst_f[:, :], dst_i[:, :]))
            then(nc.vector.scalar_tensor_tensor(k.idx[:, :], src_f[:, :], float(PADDED), src_f[:, :], ALU.is_lt, ALU.mult))
            then(nc.vector.tensor_reduce(k.ends[:, 0:G], dst_f.rearrange("p (g u) -> p g u", u=U), AX.X, ALU.min, negate=True))
            then(nc.vector.scalar_tensor_tensor(k.src_hi[:, :], dst_f[:, :], float(PADDED), dst_f[:, :], ALU.is_lt, ALU.mult))
            nc.vector.tensor_reduce(k.ends[:, G:2 * G], k.src_hi.rearrange("p (g u) -> p g u", u=U), AX.X, ALU.max).then_inc(extremes, 1)
            dve.wait_ge(reduced, 1)
            then(nc.vector.tensor_tensor(k.base[:, G:2 * G], k.base[:, G:2 * G], k.base[:, 0:G], ALU.add))
            then(nc.vector.tensor_reduce(k.spread_f[:, 0:1], k.base[:, G:2 * G], AX.X, ALU.max))
            then(nc.vector.tensor_scalar(k.spread_f[:, 0:1], k.spread_f[:, 0:1], float(P), None, ALU.is_ge))
            then(nc.vector.tensor_copy(k.spread_i[:, :], k.spread_f[:, 0:1]))
            then(nc.vector.tensor_scalar(k.spread_f[:, 0:1], k.spread_f[:, 0:1], 1.0, None, ALU.subtract))
            then(nc.vector.tensor_scalar(k.base[:, 0:G], k.base[:, 0:G], k.spread_f[:, 0:1], None, ALU.mult))
            then(nc.vector.tensor_copy(k.base_i[:, :], k.base[:, 0:G]))
            then(nc.vector.tensor_scalar(k.pos[:, :], k.base[:, 0:G], k.part_f[:, 0:1], None, ALU.add))
            then(nc.vector.tensor_tensor(k.rel.rearrange("p (g u) -> p g u", u=U), dst_f.rearrange("p (g u) -> p g u", u=U),
                                         k.base[:, 0:G].unsqueeze(2).to_broadcast([P, G, U]), ALU.subtract))
            then(nc.vector.tensor_scalar(k.src_hi[:, :], src_f[:, :], 1.0 / k.nb, -(k.nb - 1) / (2.0 * k.nb), ALU.mult, ALU.add))
            then(nc.vector.tensor_scalar(k.src_hi[:, :], k.src_hi[:, :], ROUND, None, ALU.add))
            then(nc.vector.tensor_scalar(k.src_hi[:, :], k.src_hi[:, :], ROUND, None, ALU.subtract))
            then(nc.vector.scalar_tensor_tensor(k.src_lo[:, :], k.src_hi[:, :], -float(k.nb), src_f[:, :], ALU.mult, ALU.add))


def count_src(nc, k):
    digits, counted, added, step, rooted = phase_sems(nc, k, "digits_ready", "counted", "counts_added", "degree_step", "rooted")
    hi = k.acc[:, 0:P * U].bitcast(BF16).rearrange("p (s u n) -> p s u n", s=2, u=U)
    lo = k.acc[:, P * U:2 * P * U].bitcast(BF16).rearrange("p (s u n) -> p s u n", s=2, u=U)

    with nc.Block() as block:
        M, NB = k.m, k.nb

        @block.vector
        def _(dve):
            def one_hots(g, s):
                for out, digit, n in ((hi, k.src_hi, M), (lo, k.src_lo, NB)):
                    ins = nc.vector.tensor_tensor(out[:, s, :, 0:n], k.row_f[:, 0:n].unsqueeze(1).to_broadcast([P, U, n]),
                                                  digit[:, bass.ds(g * U, U)].unsqueeze(2).to_broadcast([P, U, n]), ALU.is_equal)
                ins.then_inc(digits, 1)

            nc.vector.memset(k.deg_s[:, :], 0.0).then_inc(added, 1)
            with dve.Fori(0, k.groups // 2) as i:
                for s in range(2):
                    g = 2 * i + s
                    dve.wait_ge(added, g + 1)
                    one_hots(g, s)
                    dve.wait_ge(counted, g + 1)
                    nc.vector.tensor_tensor(k.deg_s[:, :], k.deg_s[:, :], k.ps[0:M, s, 0:NB], ALU.add).then_inc(added, 1)
            dve.wait_ge(added, k.groups + 1)
            nc.vector.tensor_scalar(k.inv_s[:, :], k.deg_s[:, :], 1.0, None, ALU.max).then_inc(step, 1)
            dve.wait_ge(rooted, 1)
            nc.vector.reciprocal(k.inv_s[:, :], k.inv_s[:, :]).then_inc(step, 1)
            nc.vector.tensor_scalar(k.deg_s[:, :], k.deg_s[:, :], 0.0, None, ALU.is_gt).then_inc(step, 1)
            dve.wait_ge(step, 3)
            nc.vector.tensor_tensor(k.inv_s[:, :], k.inv_s[:, :], k.deg_s[:, :], ALU.mult).then_inc(step, 1)

        @block.tensor
        def _(pe):
            with pe.Fori(0, k.groups // 2) as i:
                for s in range(2):
                    g = 2 * i + s
                    pe.wait_ge(digits, g + 1)
                    for u in range(U):
                        ins = nc.tensor.matmul(k.ps[0:M, s, 0:NB], hi[:, s, u, 0:M], lo[:, s, u, 0:NB], start=u == 0, stop=u == U - 1)
                    ins.then_inc(counted, 1)

        @block.scalar
        def _(act):
            act.wait_ge(step, 1)
            nc.scalar.activation(k.inv_s[:, :], k.inv_s[:, :], ACT.Sqrt).then_inc(rooted, 1)


def norm_relu(nc, k, name, scale=None, add_to_x=False, inv_from=None, clear_acc=False, ones=False):
    step, var_ready, std_ready, stored, acc_clear = phase_sems(nc, k, f"{name}_step", f"{name}_var_ready", f"{name}_std_ready", f"{name}_stored", f"{name}_acc_clear")
    M, NB = k.m, k.nb
    sq = k.acc[0:M, 0:NB * 64].rearrange("p (b f) -> p b f", f=64)
    wide = lambda v: v[:, :].unsqueeze(2).to_broadcast([M, NB, 64])

    with nc.Block() as block:

        @block.vector
        def _(dve):
            done = [0]

            def then(ins):
                done[0] += 1
                ins.then_inc(step, 1)
                dve.wait_ge(step, done[0])

            if inv_from is not None:
                nc.vector.tensor_scalar(k.inv_d[:, :], inv_from[:, :], 1.0, None, ALU.add).then_inc(var_ready, 1)
                dve.wait_ge(std_ready, 1)
                then(nc.vector.reciprocal(k.inv_d[:, :], k.inv_d[:, :]))
            then(nc.vector.tensor_reduce(k.mean[:, :], k.x[:, :, :], AX.X, ALU.add))
            then(nc.vector.tensor_scalar(k.mean[:, :], k.mean[:, :], 1.0 / 64, None, ALU.mult))
            then(nc.vector.tensor_tensor(k.t[:, :, :], k.x[:, :, :], wide(k.mean), ALU.subtract))
            then(nc.vector.tensor_tensor(sq, k.t[:, :, :], k.t[:, :, :], ALU.mult))
            then(nc.vector.tensor_reduce(k.var[:, :], sq, AX.X, ALU.add))
            n = 1 + (inv_from is not None)
            nc.vector.tensor_scalar(k.var[:, :], k.var[:, :], 1.0 / 64, EPS, ALU.mult, ALU.add).then_inc(var_ready, 1)
            dve.wait_ge(std_ready, n)
            then(nc.vector.reciprocal(k.var[:, :], k.var[:, :]))
            then(nc.vector.tensor_tensor(k.t[:, :, :], k.t[:, :, :], wide(k.var), ALU.mult))
            then(nc.vector.tensor_scalar(k.t[:, :, :], k.t[:, :, :], 0.0, None, ALU.max))
            if add_to_x:
                then(nc.vector.tensor_tensor(k.x[:, :, :], k.x[:, :, :], k.t[:, :, :], ALU.add))
            if scale is not None:
                then(nc.vector.tensor_tensor(k.t[:, :, :], k.t[:, :, :], wide(scale), ALU.mult))
            if ones:
                nc.vector.memset(k.rows[:, :, :, 64], 1.0).then_inc(acc_clear, 1)
            if clear_acc:
                nc.vector.memset(k.acc[:, :], 0.0).then_inc(acc_clear, 1)
            k.last_step = done[0]

        @block.scalar
        def _(act):
            n = 0
            if inv_from is not None:
                n = 1
                act.wait_ge(var_ready, 1)
                nc.scalar.activation(k.inv_d[:, :], k.inv_d[:, :], ACT.Sqrt).then_inc(std_ready, 1)
            act.wait_ge(var_ready, n + 1)
            nc.scalar.activation(k.var[:, :], k.var[:, :], ACT.Sqrt).then_inc(std_ready, 1)

        @block.sync
        def _(sp):
            sp.wait_ge(step, k.last_step)
            sp.dma_start(k.table_rows, k.t[:, :, :]).then_inc(stored, 16)
            sp.wait_ge(stored, 16)


def sum_by_dst(nc, k, table, width):
    clear(nc, k)
    gathered = k.gather_sems.pop()
    with nc.Block() as block:
        rows, oh, ps = k.rows, k.one_hot, k.ps

        @block.gpsimd
        def _(pool):
            def body(i, r):
                for s in range(SLOTS):
                    pool.wait_ge(k.idx_ready[s], r + 1)
                    pool.sem_inc(k.paced, 1)
                    for u in range(U):
                        nc.gpsimd.indirect_dma_start(rows[:, s, u, 0:64], None, table,
                                                     bass.IndirectOffsetOnAxis(k.idx_slot[:, s, u:u + 1], 0)).then_inc(gathered[s], 16)

            over_windows(pool, k, lambda w: over_groups(pool, k, w, body))

        @block.scalar
        def _(act):
            def body(i, r):
                for s in range(SLOTS):
                    at = bass.ds((SLOTS * i + s) * U, U)
                    act.wait_ge(k.group_done[s], r + 1)
                    nc.scalar.copy(k.idx_slot[:, s, :], k.idx[:, at]).then_inc(k.idx_ready[s], 1)

            over_windows(act, k, lambda w: over_groups(act, k, w, body))

        @block.tensor
        def _(pe):
            for s in range(SLOTS):
                pe.sem_inc(k.group_done[s], 1)

            def body(i, r):
                for s in range(SLOTS):
                    pe.wait_ge(gathered[s], 16 * U * (r + 1))
                    pe.wait_ge(k.hot_ready[s], r + 1)
                    pe.wait_ge(k.summed[s], r + 1)
                    for u in range(U):
                        ins = nc.tensor.matmul(ps[0:width, s, 0:P], rows[:, s, u, 0:width], oh[:, s % 2, u, :], start=u == 0, stop=u == U - 1)
                    ins.then_inc(k.group_done[s], 1)

            over_windows(pe, k, lambda w: over_groups(pe, k, w, body))

        @block.vector
        def _(dve):
            for s in range(SLOTS):
                dve.sem_inc(k.summed[s], 1)

            def body(i, r):
                for s in range(SLOTS):
                    g = SLOTS * i + s
                    dve.wait_ge(k.group_done[(s + 2) % SLOTS], r + s // 2 + 1)
                    one_hot(nc, k, g, s % 2).then_inc(k.hot_ready[s], 1)
                    base = dve.value_load(k.base_i[0:1, bass.ds(g, 1)], min_val=0, max_val=k.n - 1)
                    dve.wait_ge(k.group_done[s], r + 2)
                    dve.wait_ge(k.summed[(s + 3) % SLOTS], r + (s > 0) + 1)
                    at = k.acc[0:width, bass.ds(base, P)]
                    nc.vector.tensor_tensor(at, at, ps[0:width, s, 0:P], ALU.add).then_inc(k.summed[s], 1)

            walk_windows(nc, k, dve, lambda w: over_groups(dve, k, w, body))


def one_hot(nc, k, g, slot):
    return nc.vector.tensor_tensor(k.one_hot[:, slot, :, :], k.row_f[:, :].unsqueeze(1).to_broadcast([P, U, P]),
                                   k.rel[:, bass.ds(g * U, U)].unsqueeze(2).to_broadcast([P, U, P]), ALU.is_equal)


def walk_windows(nc, k, dve, window, tables_ready=None, used_up=None):
    def move(by, at):
        for n, (table, op) in enumerate(((k.rel, -by), (k.pos, by), (k.base, by))):
            table = table[:, 0:k.groups] if table is k.base else table[:, :]
            nc.vector.tensor_scalar(table, table, float(op), None, ALU.add).then_inc(k.table_step, 1)
        dve.wait_ge(k.table_step, 4 * at - 1)
        nc.vector.tensor_copy(k.base_i[:, :], k.base[:, 0:k.groups]).then_inc(k.table_step, 1)
        dve.wait_ge(k.table_step, 4 * at)
        dve.sem_inc(k.paced, 1)

    used_up = used_up or k.summed[SLOTS - 1]

    def between(w):
        dve.wait_ge(used_up, w * k.rounds + 1)
        if tables_ready is not None:
            dve.wait_ge(k.loads_issued, w)
        move(P, w)
        if tables_ready is not None:
            dve.sem_inc(tables_ready, 1)

    window(0)
    spread = dve.value_load(k.spread_i[0:1, 0:1], min_val=0, max_val=1)
    with dve.If(spread):
        with dve.Fori(1, k.windows) as w:
            between(w)
            window(w)
        dve.wait_ge(used_up, k.windows * k.rounds + 1)
        if tables_ready is not None:
            dve.wait_ge(k.loads_issued, k.windows)
        move(-P * (k.windows - 1), k.windows)


class Chain:

    def __init__(self, dve, sem, i, per):
        self.dve, self.sem, self.at, self.left = dve, sem, i * per, per

    def __call__(self, ins):
        ins.then_inc(self.sem, 1)
        self.at, self.left = self.at + 1, self.left - 1
        self.dve.wait_ge(self.sem, self.at)

    def end(self):
        assert self.left == 0


def blocks(v, at, m, width):
    return v[:, at].unsqueeze(2).to_broadcast([m, KB, width])


def rows_of(v, m, width):
    return v[0:m, 0:width].unsqueeze(1).to_broadcast([m, KB, width])


def in_pairs(eng, k, body):
    steps = k.nb // KB
    if steps > 1:
        with eng.Fori(0, steps // 2) as i:
            body([(2 * i, 0), (2 * i + 1, 1)])
    if steps % 2:
        body([(steps - 1, 0)])


def stage_acc(nc, k, rows, i, slot=0):
    return nc.scalar.copy(k.stage[0:rows, slot, :, :], feature_major(k.acc, rows, k.n, k.nb)[:, bass.ds(i * KB, KB), :])


def turn_out(nc, k, rows, slot=0):
    for b in range(KB):
        ins = nc.tensor.transpose(node_psum(k, slot)[:, b, 0:rows], k.stage[0:rows, slot, b, :], k.ident[0:rows, 0:rows])
    return ins


def turn_back(nc, k, bank, rows, width):
    for b in range(KB):
        ins = nc.tensor.transpose(k.ps[0:width, bank, k.m * b:k.m * b + k.m], rows[:, b, :], k.ident[0:k.m, 0:k.m])
    return ins


def node_psum(k, slot=0):
    return k.ps[0:k.m, 3 * slot, :].rearrange("p (b f) -> p b f", b=KB)


def place(nc, k, i, slot=0):
    return nc.scalar.copy(feature_major(k.acc, 64, k.n, k.nb)[:, bass.ds(i * KB, KB), :],
                          k.ps[0:64, 3 * slot + 1, 0:KB * k.m].rearrange("f (b p) -> f b p", b=KB))


def add_adaptive_sum(nc, k):
    staged, turned, added, step = phase_sems(nc, k, "adaptive_staged", "adaptive_turned", "adaptive_added", "adaptive_step")

    with nc.Block() as block:
        steps = k.nb // KB

        @block.scalar
        def _(act):
            stage_acc(nc, k, 65, 0).then_inc(staged, 1)
            with act.Fori(1, steps) as i:
                act.wait_ge(turned, i)
                stage_acc(nc, k, 65, i).then_inc(staged, 1)

        @block.tensor
        def _(pe):
            def body(i):
                pe.wait_ge(staged, i + 1)
                pe.sem_inc(k.paced, 1)
                turn_out(nc, k, 65).then_inc(turned, 1)

            body(0)
            with pe.Fori(1, steps) as i:
                pe.wait_ge(added, i)
                body(i)

        @block.vector
        def _(dve):
            nc.vector.tensor_scalar(k.inv_s[:, :], k.inv_s[:, :], k.adapt[0:k.m, 0:1], None, ALU.mult).then_inc(step, 1)
            dve.wait_ge(step, 1)
            with dve.Fori(0, steps) as i:
                at = bass.ds(i * KB, KB)
                dve.wait_ge(turned, i + 1)
                nc.vector.tensor_copy(k.deg_d[:, at], node_psum(k)[:, :, 64]).then_inc(step, 1)
                nc.vector.tensor_tensor(k.t_rows[:, 0, :, :], node_psum(k)[:, :, 0:64], blocks(k.inv_s, at, k.m, 64), ALU.mult).then_inc(step, 1)
                dve.wait_ge(step, 2 * i + 3)
                nc.vector.tensor_tensor(k.x[:, at, :], k.x[:, at, :], k.t_rows[:, 0, :, :], ALU.add).then_inc(added, 1)
                dve.wait_ge(added, i + 1)


def start_acc(nc, k):
    copied, turned, placed = phase_sems(nc, k, "start_copied", "start_turned", "start_placed")

    with nc.Block() as block:
        steps = k.nb // KB

        @block.vector
        def _(dve):
            def body(i):
                nc.vector.tensor_copy(k.t_rows[:, 0, :, :], k.t[:, bass.ds(i * KB, KB), :]).then_inc(copied, 1)

            body(0)
            with dve.Fori(1, steps) as i:
                dve.wait_ge(turned, i)
                body(i)

        @block.tensor
        def _(pe):
            def body(i):
                pe.wait_ge(copied, i + 1)
                pe.sem_inc(k.paced, 1)
                turn_back(nc, k, 1, k.t_rows[:, 0, :, :], 64).then_inc(turned, 1)

            body(0)
            with pe.Fori(1, steps) as i:
                pe.wait_ge(placed, i)
                body(i)

        @block.scalar
        def _(act):
            with act.Fori(0, steps) as i:
                act.wait_ge(turned, i + 1)
                act.sem_inc(k.paced, 1)
                place(nc, k, i).then_inc(placed, 1)


def convolve_wide(nc, k, name, w_in, bias, w_out, residual):
    staged, turned, scaled, back, back_copied = phase_sems(nc, k, f"{name}_staged", f"{name}_turned", f"{name}_scaled", f"{name}_back", f"{name}_back_copied")
    hidden, relued, kept, out, t_ready = phase_sems(nc, k, f"{name}_hidden", f"{name}_relued", f"{name}_kept", f"{name}_out", f"{name}_t_ready")
    t_turned, placed, saved, stored = phase_sems(nc, k, f"{name}_t_turned", f"{name}_placed", f"{name}_saved", f"{name}_stored")

    M, C, steps = k.m, KB * k.m, k.nb // KB
    out_psum = lambda slot: k.ps[0:M, 3 * slot, 0:KB * 64].rearrange("p (b f) -> p b f", b=KB)
    with nc.Block() as block:

        @block.scalar
        def _(act):
            def body(pair):
                for q, o in pair:
                    stage_acc(nc, k, 64, q, o).then_inc(staged, 1)
                for q, o in pair:
                    act.wait_ge(back, q + 1)
                    nc.scalar.copy(k.back[0:64, o, :], k.ps[0:64, 3 * o + 1, 0:C]).then_inc(back_copied, 1)
                for q, o in pair:
                    act.wait_ge(hidden, q + 1)
                    nc.scalar.activation(k.hid[:, o, :], k.ps[:, 3 * o + 2, 0:C], ACT.Relu, bias=bias[:, 0:1]).then_inc(relued, 1)
                for q, o in pair:
                    act.wait_ge(t_turned, q + 1)
                    act.sem_inc(k.paced, 1)
                    place(nc, k, q, o).then_inc(placed, 1)
                act.wait_ge(placed, pair[-1][0] + 1)
                act.sem_inc(k.paced, 1)

            in_pairs(act, k, body)

        @block.tensor
        def _(pe):
            def body(pair):
                for q, o in pair:
                    pe.wait_ge(staged, q + 1)
                    pe.sem_inc(k.paced, 1)
                    turn_out(nc, k, 64, o).then_inc(turned, 1)
                for q, o in pair:
                    pe.wait_ge(scaled, q + 1)
                    pe.sem_inc(k.paced, 1)
                    turn_back(nc, k, 3 * o + 1, k.sums[:, o, :, :], 64).then_inc(back, 1)
                for q, o in pair:
                    pe.wait_ge(back_copied, q + 1)
                    nc.tensor.matmul(k.ps[:, 3 * o + 2, 0:C], w_in[:, :], k.back[0:64, o, :], start=True, stop=True).then_inc(hidden, 1)
                for q, o in pair:
                    pe.wait_ge(kept, q + 1)
                    for b in range(KB):
                        ins = nc.tensor.matmul(out_psum(o)[:, b, :], k.kept[:, o, M * b:M * b + M], w_out[:, :], start=True, stop=True)
                    ins.then_inc(out, 1)
                for q, o in pair:
                    pe.wait_ge(t_ready, q + 1)
                    pe.sem_inc(k.paced, 1)
                    turn_back(nc, k, 3 * o + 1, k.t_rows[:, o, :, :], 64).then_inc(t_turned, 1)

            in_pairs(pe, k, body)

        @block.vector
        def _(dve):
            def body(pair):
                for q, o in pair:
                    dve.wait_ge(turned, q + 1)
                    nc.vector.tensor_tensor(k.sums[:, o, :, :], node_psum(k, o)[:, :, 0:64], blocks(k.inv_d, bass.ds(q * KB, KB), M, 64),
                                            ALU.mult).then_inc(scaled, 1)
                for q, o in pair:
                    x1 = k.x1[:, bass.ds(q * C, C)]
                    dve.wait_ge(relued, q + 1)
                    if residual:
                        nc.vector.tensor_tensor(k.kept[:, o, :], k.hid[:, o, :], x1, ALU.add).then_inc(kept, 1)
                    else:
                        nc.vector.tensor_copy(k.kept[:, o, :], k.hid[:, o, :]).then_inc(kept, 1)
                        nc.vector.tensor_copy(x1, k.hid[:, o, :]).then_inc(saved, 1)
                for q, o in pair:
                    at = bass.ds(q * KB, KB)
                    dve.wait_ge(out, q + 1)
                    nc.vector.tensor_tensor(k.t_rows[:, o, :, :], out_psum(o), blocks(k.inv_d, at, M, 64), ALU.mult).then_inc(t_ready, 1)
                    dve.wait_ge(t_ready, q + 1)
                    nc.vector.tensor_copy(k.t[:, at, :], k.t_rows[:, o, :, :]).then_inc(saved, 1)
                last = pair[-1][0] + 1
                dve.wait_ge(saved, last * (1 if residual else 2))
                dve.wait_ge(t_turned, last)
                dve.sem_inc(k.paced, 1)

            in_pairs(dve, k, body)

        @block.sync
        def _(sp):
            sp.wait_ge(saved, steps * (1 if residual else 2))
            sp.dma_start(k.table_rows, k.t[:, :, :]).then_inc(stored, 16)
            sp.wait_ge(stored, 16)


def convolve_second(nc, k):
    staged, turned, step, t_turned, placed, stored = phase_sems(nc, k, "second_staged", "second_turned", "second_step", "second_t_turned", "second_placed", "second_stored")

    with nc.Block() as block:
        steps = k.nb // KB

        @block.scalar
        def _(act):
            with act.Fori(0, steps) as i:
                stage_acc(nc, k, 64, i).then_inc(staged, 1)
                act.wait_ge(t_turned, i + 1)
                act.sem_inc(k.paced, 1)
                place(nc, k, i).then_inc(placed, 1)
                act.wait_ge(placed, i + 1)

        @block.tensor
        def _(pe):
            with pe.Fori(0, steps) as i:
                pe.wait_ge(staged, i + 1)
                pe.sem_inc(k.paced, 1)
                turn_out(nc, k, 64).then_inc(turned, 1)
                pe.wait_ge(step, 5 * i + 4)
                pe.sem_inc(k.paced, 1)
                turn_back(nc, k, 1, k.t_rows[:, 0, :, :], 64).then_inc(t_turned, 1)

        @block.vector
        def _(dve):
            with dve.Fori(0, steps) as i:
                then, at = Chain(dve, step, i, 5), bass.ds(i * KB, KB)
                dve.wait_ge(turned, i + 1)
                then(nc.vector.tensor_tensor(k.t_rows[:, 0, :, :], node_psum(k)[:, :, 0:64], blocks(k.inv_d, at, k.m, 64), ALU.mult))
                then(nc.vector.tensor_tensor(k.t_rows[:, 0, :, :], k.t_rows[:, 0, :, :], rows_of(k.b2, k.m, 64), ALU.add))
                then(nc.vector.tensor_scalar(k.t_rows[:, 0, :, :], k.t_rows[:, 0, :, :], 0.0, None, ALU.max))
                then(nc.vector.tensor_tensor(k.t_rows[:, 0, :, :], k.t_rows[:, 0, :, :], blocks(k.inv_d, at, k.m, 64), ALU.mult))
                then(nc.vector.tensor_copy(k.t[:, at, :], k.t_rows[:, 0, :, :]))
                then.end()
                dve.wait_ge(t_turned, i + 1)

        @block.sync
        def _(sp):
            sp.wait_ge(step, 5 * steps)
            sp.dma_start(k.table_rows, k.t[:, :, :]).then_inc(stored, 16)
            sp.wait_ge(stored, 16)


def add_fourth(nc, k):
    staged, turned, step = phase_sems(nc, k, "fourth_staged", "fourth_turned", "fourth_step")

    with nc.Block() as block:
        steps = k.nb // KB
        per = 4

        @block.scalar
        def _(act):
            stage_acc(nc, k, 64, 0).then_inc(staged, 1)
            with act.Fori(1, steps) as i:
                act.wait_ge(turned, i)
                stage_acc(nc, k, 64, i).then_inc(staged, 1)

        @block.tensor
        def _(pe):
            def body(i):
                pe.wait_ge(staged, i + 1)
                pe.sem_inc(k.paced, 1)
                turn_out(nc, k, 64).then_inc(turned, 1)

            body(0)
            with pe.Fori(1, steps) as i:
                pe.wait_ge(step, per * i)
                body(i)

        @block.vector
        def _(dve):
            with dve.Fori(0, steps) as i:
                then, at = Chain(dve, step, i, per), bass.ds(i * KB, KB)
                dve.wait_ge(turned, i + 1)
                rows = k.t_rows[:, 0, :, :]
                then(nc.vector.tensor_tensor(rows, node_psum(k)[:, :, 0:64], blocks(k.inv_d, at, k.m, 64), ALU.mult))
                then(nc.vector.tensor_tensor(rows, rows, rows_of(k.b4, k.m, 64), ALU.add))
                then(nc.vector.tensor_scalar(rows, rows, 0.0, None, ALU.max))
                then(nc.vector.tensor_tensor(k.x[:, at, :], k.x[:, at, :], rows, ALU.add))
                then.end()


def scatter_to_src(nc, k):
    clear(nc, k)
    N = k.n
    ps = k.ps
    with nc.Block() as block:

        def later(i, r, s, by):
            return i + (s + by) // SLOTS, r + (s + by) // SLOTS, (s + by) % SLOTS

        def last(i, s, by):
            return isinstance(i, int) and i == k.rounds - 1 and s + by >= SLOTS

        @block.sync
        def _(sp):
            sp.dma_start(k.s_src_f.bitcast(I32).rearrange("p (g u) -> p g u", u=U),
                         k.edge_pad[0].rearrange("(g p u) -> p g u", p=P, u=U)).then_inc(k.loaded_rest, 16)

            sp.dma_start(k.s_rel[:, :, :], k.rel_embed.rearrange("(c p) f -> p c f", p=k.relations)).then_inc(k.loaded_rest, 16)

            def body(i, r):
                for s in range(SLOTS):
                    o, g = s % 2, SLOTS * i + s
                    sp.wait_ge(k.types_ready[(s + 2) % SLOTS], r + s // 2 + 1)
                    sp.wait_ge(k.hot_t_ready[(s + 2) % SLOTS], r + s // 2 + 1)
                    sp.wait_ge(k.same_ready[(s + 2) % SLOTS], r + s // 2 + 1)
                    sp.sem_inc(k.paced, 1)
                    base = sp.value_load(k.base_i[0:1, bass.ds(g, 1)], min_val=0, max_val=N - 1)
                    for to, of in ((k.s_dst[:, o, :], k.edge_pad[1][bass.ds(g * GE, GE)].rearrange("(a n) -> a n", a=1).to_broadcast([P, GE])),
                                   (k.s_src[:, o, :, :].rearrange("p e u -> p (e u)"),
                                    k.edge_pad[0][bass.ds(g * GE, GE)].rearrange("(a n) -> a n", a=1).to_broadcast([P, GE])),
                                   (k.s_types[:, o, :], k.edge_pad[2][bass.ds(g * GE, GE)].rearrange("(a n) -> a n", a=1).to_broadcast([P, GE]))):
                        sp.dma_start(to, of).then_inc(k.loaded[s], 16)
                    sp.wait_ge(k.from_dst[(s + 2) % SLOTS], r + s // 2 + 1)
                    sp.dma_start(k.s_win[:, o, :], k.table[bass.ds(base, P), :]).then_inc(k.window_loaded[s], 16)

            def window(w):
                over_groups(sp, k, w, body)
                sp.sem_inc(k.loads_issued, 1)

            def between(w):
                sp.wait_ge(k.tables_ready, w)
                sp.sem_inc(k.paced, 1)

            over_windows(sp, k, window, between)

        @block.gpsimd
        def _(pool):
            for j in range(SCATTERS):
                pool.dma_start(k.scattered[j][N + P:N + P + 1, :], k.zeros[0:1, :]).then_inc(k.scattered_in[j], 16)
            for s in range(SLOTS - 1):
                pool.sem_inc(k.out_free[s], 1)

            def scatter(i, r, s):
                pool.wait_ge(k.idx_out[s], r + 1)
                pool.wait_ge(k.out_ready[s], r + 2)
                for u in range(U):
                    if u % 2 == 0:
                        for j in range(u, u + 2):
                            pool.wait_ge(k.scattered_in[j], 16 + 16 * (SLOTS * r + s))
                        pool.sem_inc(k.paced, 1)
                    if u == U - 1:
                        pool.sem_inc(k.out_free[(s + SLOTS - 1) % SLOTS], 1)
                    nc.gpsimd.indirect_dma_start(k.scattered[u][:, :], bass.IndirectOffsetOnAxis(k.s_idx[:, s, u:u + 1], 0),
                                                 k.s_out[:, s, u, :], None, compute_op=ALU.add).then_inc(k.scattered_in[u], 16)

            def body(i, r):
                for s in range(SLOTS):
                    scatter(i, r, s)

            def window(w):
                over_groups(pool, k, w, body)
                for j in range(SCATTERS):
                    pool.wait_ge(k.scattered_in[j], 16 + 16 * k.groups * (w + 1))
                pool.sem_inc(k.paced, 1)

            over_windows(pool, k, window)

        @block.scalar
        def _(act):
            for s in range(SLOTS):
                act.sem_inc(k.out_ready[s], 1)
                act.sem_inc(k.types_ready[s], 1)

            def types(i, r, s):
                act.wait_ge(k.loaded[s], 48 * (r + 1))
                act.wait_ge(k.hot_t_ready[(s + 2) % SLOTS], r + s // 2 + 1)
                nc.scalar.copy(k.s_types_h[:, s % 2, :], k.s_types[:, s % 2, :]).then_inc(k.types_ready[s], 1)

            def body(i, r):
                for s in range(SLOTS):
                    if not last(i, s, 2):
                        types(*later(i, r, s, 2))
                    act.wait_ge(k.merged[s], r + 2)
                    act.wait_ge(k.out_free[s], r + 1)
                    nc.scalar.copy(k.s_out[:, s, :, :].rearrange("p u f -> p (u f)"), ps[:, 4 + s % 2, :]).then_inc(k.out_ready[s], 1)

            def window(w):
                types(0, w * k.rounds, 0)
                types(0, w * k.rounds, 1)
                over_groups(act, k, w, body)

            over_windows(act, k, window)

        @block.tensor
        def _(pe):
            for s in range(SLOTS):
                pe.sem_inc(k.merged[s], 1)
                pe.sem_inc(k.from_dst[s], 1)

            def features(i, r, s):
                o = s % 2
                pe.wait_ge(k.window_loaded[s], 16 * (r + 1))
                pe.wait_ge(k.hot_t_ready[s], r + 2)
                pe.wait_ge(k.msg_done[(s + 2) % SLOTS], r + s // 2 + 1)
                for u in range(U):
                    out = ps[:, o, 64 * u:64 * u + 64]
                    for c in range(4):
                        for q in range(3):
                            nc.tensor.matmul(out, k.s_hot_type[:, o, c, :, u], k.rel_parts[:, c, 64 * q:64 * q + 64], start=c + q == 0, stop=False,
                                             skip_group_check=True)
                    ins = nc.tensor.matmul(out, k.s_hot_t[:, o, :, u], k.s_win[:, o, :], start=False, stop=True, skip_group_check=True)
                ins.then_inc(k.from_dst[s], 1)

            def merge(i, r, s):
                o = s % 2
                pe.wait_ge(k.msg_done[s], r + 2)
                pe.wait_ge(k.out_ready[(s + 2) % SLOTS], r + s // 2 + 1)
                for u in range(U):
                    ins = nc.tensor.matmul(ps[:, 4 + o, 64 * u:64 * u + 64], k.s_same[:, o, u, :], k.s_msg[:, o, u, :], start=True, stop=True)
                ins.then_inc(k.merged[s], 1)

            def body(i, r):
                for s in range(SLOTS):
                    if not last(i, s, 1):
                        features(*later(i, r, s, 1))
                    merge(i, r, s)

            def window(w):
                features(0, w * k.rounds, 0)
                over_groups(pe, k, w, body)

            over_windows(pe, k, window)

        @block.vector
        def _(dve):
            for s in range(SLOTS):
                dve.sem_inc(k.msg_done[s], 1)
                dve.sem_inc(k.same_ready[s], 1)
                dve.sem_inc(k.hot_t_ready[s], 1)

            dve.wait_ge(k.loaded_rest, 32)
            high, middle, low = (k.rel_parts[:, :, 64 * q:64 * q + 64] for q in range(3))
            nc.vector.tensor_copy(high, k.s_rel[:, :, :]).then_inc(k.repeat_step, 1)
            dve.wait_ge(k.repeat_step, 1)
            nc.vector.tensor_tensor(k.s_rel[:, :, :], k.s_rel[:, :, :], high, ALU.subtract).then_inc(k.repeat_step, 1)
            dve.wait_ge(k.repeat_step, 2)
            nc.vector.tensor_copy(middle, k.s_rel[:, :, :]).then_inc(k.repeat_step, 1)
            dve.wait_ge(k.repeat_step, 3)
            nc.vector.tensor_tensor(low, k.s_rel[:, :, :], middle, ALU.subtract).then_inc(k.repeat_step, 1)
            for c in range(4):
                nc.vector.tensor_scalar(k.s_type_at[:, c:c + 1], k.part_f[:, :], float(c * k.relations), None, ALU.add).then_inc(k.repeat_step, 1)
            dve.wait_ge(k.repeat_step, 8)
            nc.vector.tensor_copy(k.s_src_f, k.s_src_f.bitcast(I32)).then_inc(k.dve_step, 1)
            nc.vector.tensor_scalar(k.s_before, k.row_f[:, :], k.part_f[:, 0:1], None, ALU.is_lt).then_inc(k.dve_step, 1)
            dve.wait_ge(k.dve_step, 2)
            nc.vector.tensor_scalar(k.s_to, k.s_src_f, float(N + P), float(N), ALU.min, ALU.subtract).then_inc(k.dve_step, 1)
            dve.wait_ge(k.dve_step, 3)
            nc.vector.tensor_scalar(k.s_to, k.s_to, k.part_f[:, 0:1], None, ALU.subtract).then_inc(k.dve_step, 1)
            dve.wait_ge(k.dve_step, 4)

            def one_hots(i, r, s):
                o, g = s % 2, SLOTS * i + s
                dve.wait_ge(k.loaded[s], 48 * (r + 1))
                dve.wait_ge(k.from_dst[(s + 2) % SLOTS], r + s // 2 + 1)
                nc.vector.tensor_scalar(k.s_hot_t[:, o, :, :].rearrange("p e u -> p (e u)"), k.s_dst[:, o, :], k.pos[:, bass.ds(g, 1)], None,
                                        ALU.is_equal)
                dve.wait_ge(k.types_ready[s], r + 2)
                for c in range(4):
                    ins = nc.vector.tensor_scalar(k.s_hot_type[:, o, c, :, :].rearrange("p e u -> p (e u)"), k.s_types_h[0:k.relations, o, :],
                                                  k.s_type_at[0:k.relations, c:c + 1], None, ALU.is_equal)
                ins.then_inc(k.hot_t_ready[s], 1)

            def indices(i, r, s):
                o = s % 2
                tiles = bass.ds((SLOTS * i + s) * U, U)
                count = 8 + 3 * (SLOTS * r + s)
                dve.wait_ge(k.merged[(s + 2) % SLOTS], r + s // 2 + 1)
                nc.vector.tensor_tensor(k.s_same[:, o, :, :], k.s_src[:, o, :, :].rearrange("p e u -> p u e"),
                                        k.s_src_f[:, tiles].unsqueeze(2).to_broadcast([P, U, P]), ALU.is_equal).then_inc(k.same_ready[s], 1)
                dve.wait_ge(k.same_ready[s], r + 2)
                nc.vector.tensor_tensor(k.s_earlier[:, :, :], k.s_same[:, o, :, :], k.s_before.unsqueeze(1).to_broadcast([P, U, P]),
                                        ALU.mult).then_inc(k.repeat_step, 1)
                dve.wait_ge(k.repeat_step, count + 1)
                nc.vector.tensor_reduce(k.s_repeat, k.s_earlier[:, :, :], AX.X, ALU.max).then_inc(k.repeat_step, 1)
                dve.wait_ge(k.repeat_step, count + 2)
                nc.vector.scalar_tensor_tensor(k.s_at, k.s_repeat, 0.0, k.s_to[:, tiles], ALU.is_equal, ALU.mult).then_inc(k.repeat_step, 1)
                dve.wait_ge(k.repeat_step, count + 3)
                dve.wait_ge(k.out_free[s], r + 1)
                nc.vector.tensor_scalar(k.s_idx[:, s, :], k.s_at, k.part_f[:, 0:1], float(N), ALU.add, ALU.add).then_inc(k.idx_out[s], 1)
                dve.wait_ge(k.idx_out[s], r + 1)

            def message(i, r, s):
                o = s % 2
                dve.wait_ge(k.from_dst[s], r + 2)
                dve.wait_ge(k.merged[(s + 2) % SLOTS], r + s // 2 + 1)
                nc.vector.tensor_tensor(k.s_msg[:, o, :, :], ps[:, o, :].rearrange("p (u f) -> p u f", u=U),
                                        k.s_weight[:, bass.ds((SLOTS * i + s) * U, U)].unsqueeze(2).to_broadcast([P, U, 64]),
                                        ALU.mult).then_inc(k.msg_done[s], 1)

            def body(i, r):
                for s in range(SLOTS):
                    if not last(i, s, 1):
                        one_hots(*later(i, r, s, 1))
                    message(i, r, s)
                    if not last(i, s, 1):
                        indices(*later(i, r, s, 1))

            def window(w):
                nc.vector.scalar_tensor_tensor(k.s_weight, k.rel[:, :], 0.0, k.wgt[:, :], ALU.is_ge, ALU.mult).then_inc(k.dve_step, 1)
                dve.wait_ge(k.dve_step, 2 * w + 5)
                nc.vector.scalar_tensor_tensor(k.s_weight, k.rel[:, :], float(P), k.s_weight, ALU.is_lt, ALU.mult).then_inc(k.dve_step, 1)
                dve.wait_ge(k.dve_step, 2 * w + 6)
                one_hots(0, w * k.rounds, 0)
                indices(0, w * k.rounds, 0)
                dve.sem_inc(k.paced, 1)
                over_groups(dve, k, w, body)

            walk_windows(nc, k, dve, window, tables_ready=k.tables_ready, used_up=k.msg_done[SLOTS - 1])


def add_scattered(nc, k):
    loaded, added = phase_sems(nc, k, "tables_loaded", "tables_added")
    halves = k.t[:, :, :], k.acc[0:k.m, 0:k.nb * 64].rearrange("p (b f) -> p b f", b=k.nb)
    with nc.Block() as block:
        @block.sync
        def _(sp):
            for j in range(SCATTERS):
                if j >= 2:
                    sp.wait_ge(added, j - 1)
                if j:
                    sp.wait_ge(loaded, 16 * j)
                sp.dma_start(halves[j % 2], k.scattered[j][0:k.n, :].rearrange("(p b) f -> p b f", b=k.nb)).then_inc(loaded, 16)

        @block.vector
        def _(dve):
            for j in range(SCATTERS):
                dve.wait_ge(loaded, 16 * (j + 1))
                nc.vector.tensor_tensor(k.x[:, :, :], k.x[:, :, :], halves[j % 2], ALU.add).then_inc(added, 1)
                dve.wait_ge(added, j + 1)


def message_tables(nc, k):
    copied, turned, back_copied, multiplied, u_ready, v_ready = phase_sems(nc, k, "tables_copied", "tables_turned", "tables_back_copied", "tables_multiplied", "tables_u_ready", "tables_v_ready")
    u_stored, v_stored, zeroed, zeros_stored = phase_sems(nc, k, "tables_u_stored", "tables_v_stored", "tables_zeroed", "tables_zeros_stored")

    with nc.Block() as block:
        M, C, steps = k.m, KB * k.m, k.nb // KB
        u_psum, v_psum = (k.ps[0:M, bank, :].rearrange("p (b f) -> p b f", b=KB) for bank in (2, 3))

        @block.vector
        def _(dve):
            nc.vector.memset(k.x1[:, 0:P], 0.0).then_inc(zeroed, 1)

            def body(i, first):
                nc.vector.tensor_copy(k.t_rows[:, 0, :, :], k.t[:, bass.ds(i * KB, KB), :]).then_inc(copied, 1)
                dve.wait_ge(multiplied, i + 1)
                if not first:
                    dve.wait_ge(v_stored, 16 * i)
                nc.vector.tensor_tensor(k.v_rows[:, :, :], v_psum, rows_of(k.mb1, M, 128), ALU.add).then_inc(v_ready, 1)

            body(0, True)
            with dve.Fori(1, steps) as i:
                body(i, False)

        @block.tensor
        def _(pe):
            def body(i):
                pe.wait_ge(copied, i + 1)
                pe.sem_inc(k.paced, 1)
                turn_back(nc, k, 1, k.t_rows[:, 0, :, :], 64).then_inc(turned, 1)
                pe.wait_ge(back_copied, i + 1)
                for half, to in enumerate((u_psum, v_psum)):
                    for b in range(KB):
                        ins = nc.tensor.matmul(to[:, b, :], k.back[0:64, 0, M * b:M * b + M], k.w_uv[:, P * half:P * half + P], start=True, stop=True)
                ins.then_inc(multiplied, 1)

            body(0)
            with pe.Fori(1, steps) as i:
                pe.wait_ge(u_ready, i)
                pe.wait_ge(v_ready, i)
                body(i)

        @block.scalar
        def _(act):
            def body(i, first):
                act.wait_ge(turned, i + 1)
                nc.scalar.copy(k.back[0:64, 0, :], k.ps[0:64, 1, 0:C]).then_inc(back_copied, 1)
                act.wait_ge(multiplied, i + 1)
                if not first:
                    act.wait_ge(u_stored, 16 * i)
                nc.scalar.copy(k.u_rows[:, :, :], u_psum).then_inc(u_ready, 1)

            body(0, True)
            with act.Fori(1, steps) as i:
                body(i, False)

        @block.sync
        def _(sp):
            sp.wait_ge(zeroed, 1)
            sp.dma_start(k.v_table[k.n:k.n + P, :], k.x1[:, 0:P]).then_inc(zeros_stored, 16)
            with sp.Fori(0, steps) as i:
                for table, rows, ready, stored in ((k.u_table, k.u_rows, u_ready, u_stored), (k.v_table, k.v_rows, v_ready, v_stored)):
                    sp.wait_ge(ready, i + 1)
                    sp.dma_start(table[0:k.n, :].rearrange("(p b) f -> p b f", b=k.nb)[:, bass.ds(i * KB, KB), :],
                                 rows[:, :, :]).then_inc(stored, 16)
            sp.wait_ge(u_stored, 16 * steps)
            sp.wait_ge(v_stored, 16 * steps)
            sp.wait_ge(zeros_stored, 16)


def sum_messages(nc, k, edge_attr, dst):
    clear(nc, k)
    gathered = k.gather_sems.pop()
    with nc.Block() as block:
        u_rows, dst_b, ea, ea_t, v_win, hot_t, relu, ps = k.m_u, k.m_dst, k.m_ea, k.m_ea_t, k.m_v, k.m_hot_t, k.m_relu, k.ps
        pre = lambda o, h: ps[:, 2 * o + h, :]
        full = (k.groups - 1) * GE
        H = U // 2

        def later(i, r, s, by):
            return i + (s + by) // SLOTS, r + (s + by) // SLOTS, (s + by) % SLOTS

        def last(i, s, by):
            return isinstance(i, int) and i == k.rounds - 1 and s + by >= SLOTS

        @block.sync
        def _(sp):
            def body(i, r, w=None):
                for s in range(SLOTS):
                    o = s % 2
                    g = SLOTS * i + s
                    sp.wait_ge(k.pre_done[(s + 2) % SLOTS], r + s // 2 + 1)
                    sp.sem_inc(k.paced, 1)
                    base = sp.value_load(k.base_i[0:1, bass.ds(g, 1)], min_val=0, max_val=k.n - 1)
                    if s == SLOTS - 1 and isinstance(i, int) and i == k.rounds - 1:
                        rest = k.e - full
                        parts = [(dst_b[:, o, 0:rest], dst[full:k.e].rearrange("(a n) -> a n", a=1).to_broadcast([P, rest]))]
                        whole, odd = divmod(rest, U)
                        if whole:
                            parts.append((ea[0:whole, o, :], edge_attr[full:full + whole * U, :].rearrange("(p u) f -> p (u f)", u=U)))
                        if odd:
                            parts.append((ea[whole:whole + 1, o, 0:odd * 32], edge_attr[k.e - odd:k.e, :].rearrange("(a u) f -> a (u f)", a=1)))
                        else:
                            parts.append((ea[0:1, o, 0:32], edge_attr[full:full + 1, :]))
                        assert len(parts) == 3
                        first, more = parts[0:2], parts[2]
                    else:
                        first = [(dst_b[:, o, :], dst[bass.ds(g * GE, GE)].rearrange("(a n) -> a n", a=1).to_broadcast([P, GE])),
                                 (ea[:, o, :], edge_attr[bass.ds(g * GE, GE), :].rearrange("(p u) f -> p (u f)", u=U))]
                        more = None
                    for to, of in first + [(v_win[:, o, :], k.v_table[bass.ds(base, P), :])]:
                        sp.dma_start(to, of).then_inc(k.loaded[s], 16)
                    if more:
                        sp.dma_start(*more).then_inc(k.loaded_rest, 16)

            def window(w):
                over_groups(sp, k, w, body)
                sp.wait_ge(k.loaded_rest, 16 * (w + 1))
                sp.sem_inc(k.loads_issued, 1)

            def between(w):
                sp.wait_ge(k.tables_ready, w)
                sp.sem_inc(k.paced, 1)

            over_windows(sp, k, window, between)

        @block.gpsimd
        def _(pool):
            def body(i, r):
                for s in range(SLOTS):
                    pool.wait_ge(k.idx_ready[s], r + 1)
                    pool.sem_inc(k.paced, 1)
                    for u in range(U):
                        nc.gpsimd.indirect_dma_start(u_rows[:, s, u, :], None, k.u_table[:, :],
                                                     bass.IndirectOffsetOnAxis(k.idx_slot[:, s, u:u + 1], 0)).then_inc(gathered[s], 16)

            over_windows(pool, k, lambda w: over_groups(pool, k, w, body))

        @block.scalar
        def _(act):
            def index(i, r, s):
                act.wait_ge(k.summed_half[s], 2 * r + 2)
                nc.scalar.copy(k.idx_slot[:, s, :], k.idx[:, bass.ds((SLOTS * i + s) * U, U)]).then_inc(k.idx_ready[s], 1)

            def features(i, r, s):
                act.wait_ge(k.ea_turned[s], r + 1)
                nc.scalar.copy(ea_t[:, s % 2, :], ps[:, 6, 0:2 * P]).then_inc(k.ea_ready[s], 1)

            def body(i, r):
                for s in range(SLOTS):
                    if not last(i, s, 1):
                        features(*later(i, r, s, 1))
                    for h in range(2):
                        act.wait_ge(k.summed_half[s], 2 * r + 3 + h)
                        half = relu[:, s % 2, h * H:h * H + H, :]
                        nc.scalar.activation(half, half, ACT.Relu).then_inc(k.relued[s], 1)
                    if not last(i, s, 2):
                        index(*later(i, r, s, 2))

            def window(w):
                index(0, w * k.rounds, 0)
                index(0, w * k.rounds, 1)
                features(0, w * k.rounds, 0)
                over_groups(act, k, w, body)

            over_windows(act, k, window)

        @block.tensor
        def _(pe):
            for s in range(SLOTS):
                pe.sem_inc(k.group_done[s], 1)
                pe.sem_inc(k.pre_done[s], 1)

            def before_relu(i, r, s):
                o = s % 2
                pe.wait_ge(k.loaded[s], 48 * (r + 1))
                if last(i, s, 1):
                    pe.wait_ge(k.loaded_rest, 16 * (pe_window[0] + 1))
                for h in range(2):
                    ins = nc.tensor.transpose(ps[:, 6, P * h:P * h + P], ea[:, o, P * h:P * h + P], k.ident[:, :])
                ins.then_inc(k.ea_turned[s], 1)
                pe.wait_ge(k.ea_ready[s], r + 1)
                pe.wait_ge(k.summed_half[(s + 2) % SLOTS], 2 * (r + s // 2) + 2)
                pe.wait_ge(k.hot_t_ready[s], r + 1)
                for h in range(2):
                    nc.tensor.matmul(pre(o, h), ea_t[:, o, P * h:P * h + P], k.we[:, :], start=True, stop=False, skip_group_check=True)
                    for q in range(H):
                        ins = nc.tensor.matmul(pre(o, h)[:, P * q:P * q + P], hot_t[:, o, :, h * H + q], v_win[:, o, :],
                                               start=False, stop=q == H - 1, skip_group_check=True)
                    ins.then_inc(k.pre_half[s] if h == 0 else k.pre_done[s], 1)

            def sums(i, r, s):
                o = s % 2
                pe.wait_ge(k.relued[s], 2 * (r + 1))
                pe.wait_ge(k.hot_ready[s], r + 1)
                pe.wait_ge(k.summed[(s + 2) % SLOTS], r + s // 2 + 1)
                for u in range(U):
                    ins = nc.tensor.matmul(ps[:, 4 + o, 0:P], relu[:, o, u, :], k.one_hot[:, o, u, :], start=u == 0, stop=u == U - 1)
                ins.then_inc(k.group_done[s], 1)

            def body(i, r):
                for s in range(SLOTS):
                    if not last(i, s, 1):
                        before_relu(*later(i, r, s, 1))
                    sums(i, r, s)

            pe_window = [0]

            def window(w):
                pe_window[0] = w
                before_relu(0, w * k.rounds, 0)
                over_groups(pe, k, w, body)

            over_windows(pe, k, window)

        @block.vector
        def _(dve):
            for s in range(SLOTS):
                dve.sem_inc(k.summed[s], 1)
                dve.sem_inc(k.summed_half[s], 2)

            def one_hots(i, r, s):
                o, g = s % 2, SLOTS * i + s
                dve.wait_ge(k.loaded[s], 48 * (r + 1))
                dve.wait_ge(k.pre_done[(s + 2) % SLOTS], r + s // 2 + 1)
                dve.wait_ge(k.group_done[(s + 2) % SLOTS], r + s // 2 + 1)
                nc.vector.tensor_scalar(hot_t[:, o, :, :].rearrange("p e u -> p (e u)"), dst_b[:, o, :], k.pos[:, bass.ds(g, 1)], None,
                                        ALU.is_equal).then_inc(k.hot_t_ready[s], 1)
                one_hot(nc, k, g, o).then_inc(k.hot_ready[s], 1)

            def add_up(i, r, s):
                o = s % 2
                dve.wait_ge(gathered[s], 16 * U * (r + 1))
                dve.wait_ge(k.group_done[(s + 2) % SLOTS], r + s // 2 + 1)
                for h in range(2):
                    dve.wait_ge(k.pre_half[s] if h == 0 else k.pre_done[s], r + 1 + h)
                    nc.vector.tensor_tensor(relu[:, o, h * H:h * H + H, :], pre(o, h).rearrange("p (q f) -> p q f", q=H),
                                            u_rows[:, s, h * H:h * H + H, :], ALU.add).then_inc(k.summed_half[s], 1)

            def add_sums(i, r, s):
                base = dve.value_load(k.base_i[0:1, bass.ds(SLOTS * i + s, 1)], min_val=0, max_val=k.n - 1)
                dve.wait_ge(k.group_done[s], r + 2)
                dve.wait_ge(k.summed[(s + 3) % SLOTS], r + (s > 0) + 1)
                at = k.acc[:, bass.ds(base, P)]
                nc.vector.tensor_tensor(at, at, ps[:, 4 + s % 2, 0:P], ALU.add).then_inc(k.summed[s], 1)

            def body(i, r):
                for s in range(SLOTS):
                    add_up(i, r, s)
                    if s > 0:
                        add_sums(i, r, s - 1)
                    if not last(i, s, 1):
                        one_hots(*later(i, r, s, 1))
                add_sums(i, r, SLOTS - 1)

            def window(w):
                one_hots(0, w * k.rounds, 0)
                over_groups(dve, k, w, body)

            walk_windows(nc, k, dve, window, tables_ready=k.tables_ready)


def update_nodes(nc, k, out):
    staged, mixed, turned, back_copied = phase_sems(nc, k, "update_staged", "update_mixed", "update_turned", "update_back_copied")
    hidden, relued, out_ready, step, stored = phase_sems(nc, k, "update_hidden", "update_relued", "update_out_ready", "update_step", "update_stored")

    with nc.Block() as block:
        M, C, steps = k.m, KB * k.m, k.nb // KB
        agg = k.ps[0:M, 0, 0:KB * 64].rearrange("p (b f) -> p b f", b=KB)
        out_psum = k.ps[0:M, 3, 0:KB * 64].rearrange("p (b f) -> p b f", b=KB)
        per = 5

        @block.scalar
        def _(act):
            with act.Fori(0, steps) as i:
                stage_acc(nc, k, P, i).then_inc(staged, 1)
                act.wait_ge(turned, i + 1)
                nc.scalar.copy(k.back[:, 0, :], k.ps[:, 1, 0:C]).then_inc(back_copied, 1)
                act.wait_ge(hidden, i + 1)
                nc.scalar.activation(k.hid[:, 0, :], k.ps[:, 2, 0:C], ACT.Relu, bias=k.ub1[:, 0:1]).then_inc(relued, 1)

        @block.tensor
        def _(pe):
            def body(i):
                pe.wait_ge(staged, i + 1)
                for b in range(KB):
                    ins = nc.tensor.matmul(agg[:, b, :], k.stage[:, 0, b, :], k.mw2[:, :], start=True, stop=True)
                ins.then_inc(mixed, 1)
                pe.wait_ge(step, per * i + 3)
                pe.sem_inc(k.paced, 1)
                turn_back(nc, k, 1, k.v_rows, P).then_inc(turned, 1)
                pe.wait_ge(back_copied, i + 1)
                nc.tensor.matmul(k.ps[:, 2, 0:C], k.uw1[:, :], k.back[:, 0, :], start=True, stop=True).then_inc(hidden, 1)
                pe.wait_ge(relued, i + 1)
                for b in range(KB):
                    ins = nc.tensor.matmul(out_psum[:, b, :], k.hid[:, 0, M * b:M * b + M], k.uw2[:, :], start=True, stop=True)
                ins.then_inc(out_ready, 1)

            body(0)
            with pe.Fori(1, steps) as i:
                pe.wait_ge(step, per * i)
                body(i)

        @block.vector
        def _(dve):
            with dve.Fori(0, steps) as i:
                then, at = Chain(dve, step, i, per), bass.ds(i * KB, KB)
                then(nc.vector.tensor_tensor(k.v_rows[:, :, 64:128], rows_of(k.mb2, M, 64), blocks(k.deg_d, at, M, 64), ALU.mult))
                then(nc.vector.tensor_copy(k.v_rows[:, :, 0:64], k.t[:, at, :]))
                dve.wait_ge(mixed, i + 1)
                then(nc.vector.tensor_tensor(k.v_rows[:, :, 64:128], k.v_rows[:, :, 64:128], agg, ALU.add))
                then(nc.vector.tensor_tensor(k.x[:, at, :], k.x[:, at, :], rows_of(k.ub2, M, 64), ALU.add))
                dve.wait_ge(out_ready, i + 1)
                then(nc.vector.tensor_tensor(k.x[:, at, :], k.x[:, at, :], out_psum, ALU.add))
                then.end()

        @block.sync
        def _(sp):
            sp.wait_ge(step, per * steps)
            sp.dma_start(out.rearrange("(p b) f -> p b f", b=k.nb), k.x[:, :, :]).then_inc(stored, 16)
            sp.wait_ge(stored, 16)


def bass_four_graph_layers(
        nc, x, src, dst, edge_attr_32, edge_type_500, edge_weight, L0_gnn_adaptive_weight,
        L1_gnn_W1, L1_gnn_b1, L1_gnn_W2, L1_gnn_b2, L1_gnn_W3, L1_gnn_b3, L1_gnn_W4, L1_gnn_b4,
        L2_gnn_rel_embed, L3_gnn_mW1, L3_gnn_mb1, L3_gnn_mW2, L3_gnn_mb2,
        L3_gnn_uW1, L3_gnn_ub1, L3_gnn_uW2, L3_gnn_ub2, out):
    a = Names()
    a.x = x
    a.src = src
    a.dst = dst
    a.edge_attr_32 = edge_attr_32
    a.edge_type_500 = edge_type_500
    a.edge_weight = edge_weight
    a.L0_gnn_adaptive_weight = L0_gnn_adaptive_weight
    a.L1_gnn_W1 = L1_gnn_W1
    a.L1_gnn_b1 = L1_gnn_b1
    a.L1_gnn_W2 = L1_gnn_W2
    a.L1_gnn_b2 = L1_gnn_b2
    a.L1_gnn_W3 = L1_gnn_W3
    a.L1_gnn_b3 = L1_gnn_b3
    a.L1_gnn_W4 = L1_gnn_W4
    a.L1_gnn_b4 = L1_gnn_b4
    a.L2_gnn_rel_embed = L2_gnn_rel_embed
    a.L3_gnn_mW1 = L3_gnn_mW1
    a.L3_gnn_mb1 = L3_gnn_mb1
    a.L3_gnn_mW2 = L3_gnn_mW2
    a.L3_gnn_mb2 = L3_gnn_mb2
    a.L3_gnn_uW1 = L3_gnn_uW1
    a.L3_gnn_ub1 = L3_gnn_ub1
    a.L3_gnn_uW2 = L3_gnn_uW2
    a.L3_gnn_ub2 = L3_gnn_ub2
    n = a.x.shape[0]
    e = a.src.shape[0]
    m = 125
    nb = n // m
    groups = -(-e // GE)
    assert n % m == 0 and nb % KB == 0 and groups % SLOTS == 0 and m <= P and nb <= P
    tiles = groups * U
    k = Names()
    k.n, k.e, k.m, k.nb, k.groups, k.rounds, k.windows = n, e, m, nb, groups, groups // SLOTS, -(-n // P)

    k.table = nc.dram_tensor("table", [n + P, 64], F32)
    k.edge_pad = [nc.dram_tensor(name, [groups * GE], I32) for name in ("src_pad", "dst_pad", "type_pad")]
    k.scattered = [nc.dram_tensor(f"scattered_{j}", [n + P + 1, 64], F32) for j in range(SCATTERS)]
    k.table_rows = k.table[0:n, :].rearrange("(p b) f -> p b f", b=nb)
    k.u_table = nc.dram_tensor("u_table", [n, P], F32)
    k.v_table = nc.dram_tensor("v_table", [n + P, P], F32)
    k.rel_embed = a.L2_gnn_rel_embed
    k.relations = k.rel_embed.shape[0] // 4
    assert k.relations * 4 == k.rel_embed.shape[0] <= 2048 and k.relations <= P

    with ExitStack() as ctx:
        sb = lambda name, shape, dt=F32: ctx.enter_context(nc.sbuf_tensor(name, shape, dt))
        k.x, k.t = sb("x", [m, nb, 64]), sb("t", [m, nb, 64])
        behind = max(nb * 64, 5 * GE)
        k.acc = sb("acc", [P, max(n + P, 2 * P * U, behind + 3 * tiles + P)])
        k.x1 = sb("x1", [P, max(n, 12288, 6 * tiles)])
        k.idx = sb("idx", [P, tiles], I32)
        k.wgt, k.rel = sb("wgt", [P, tiles]), sb("rel", [P, tiles])
        k.base, k.pos = sb("base", [P, 2 * groups]), sb("pos", [P, groups])
        k.base_i = sb("base_i", [P, groups], I32)
        k.spread_f, k.spread_i = sb("spread_f", [P, 1]), sb("spread_i", [P, 1], I32)
        k.row_f, k.part_f, k.ident = sb("row_f", [P, P]), sb("part_f", [P, 1]), sb("ident", [P, P])
        k.part_i = sb("part_i", [P, 1], I32)
        k.deg_s, k.deg_d, k.inv_s, k.inv_d = (sb(s, [m, nb]) for s in ("deg_s", "deg_d", "inv_s", "inv_d"))
        k.mean, k.var = sb("mean", [m, nb]), sb("var", [m, nb])
        k.w1, k.w2, k.w3, k.w4 = sb("w1", [64, P]), sb("w2", [P, 64]), sb("w3", [64, P]), sb("w4", [P, 64])
        k.b1, k.b2, k.b3, k.b4 = sb("b1", [P, 1]), sb("b2", [P, 64]), sb("b3", [P, 1]), sb("b4", [P, 64])
        k.w_uv, k.we, k.mb1 = sb("w_uv", [64, 2 * P]), sb("we", [P, 4 * P]), sb("mb1", [P, P])
        k.mw2, k.mb2 = sb("mw2", [P, 64]), sb("mb2", [P, 64])
        k.uw1, k.ub1, k.uw2, k.ub2 = sb("uw1", [P, P]), sb("ub1", [P, 1]), sb("uw2", [P, 64]), sb("ub2", [P, 64])
        k.zeros = sb("zeros", [P, 64])
        k.adapt = sb("adapt", [P, 1])
        k.idx_slot = sb("idx_slot", [P, SLOTS, U], I32)
        k.rel_parts = sb("rel_parts", [k.relations, 4, 3 * 64], BF16)
        work = sb("work", [P, max(2 * U * P, 6 * KB * P)])
        k.one_hot = work[:, 0:2 * U * P].rearrange("p (o u n) -> p o u n", o=2, u=U)
        cut = lambda v, at, size: v[:, at:at + size]
        two = lambda at: cut(work, at * KB * P, 2 * KB * m).rearrange("p (o c) -> p o c", o=2)
        k.stage = two(0).rearrange("p o (b n) -> p o b n", b=KB)
        k.kept = two(0)
        k.back, k.hid = two(2), two(4)
        more = sb("more", [P, SLOTS * U * 65])
        k.rows = more[:, :].rearrange("p (s u f) -> p s u f", s=SLOTS, u=U)
        k.t_rows = more[0:m, 0:2 * KB * 64].rearrange("p (o b f) -> p o b f", o=2, b=KB)
        k.sums = more[0:m, 512:512 + 2 * KB * 64].rearrange("p (o b f) -> p o b f", o=2, b=KB)
        k.u_rows = more[0:m, 512:512 + KB * P].rearrange("p (b f) -> p b f", b=KB)
        k.v_rows = more[0:m, 1024:1024 + KB * P].rearrange("p (b f) -> p b f", b=KB)
        k.ends = more[:, 0:2 * groups]
        k.row_i = more[:, 2 * groups:2 * groups + P].bitcast(I32)
        k.fill = work[:, 0:GE].bitcast(I32)
        k.src_i, k.dst_i = cut(k.x1, 0, tiles).bitcast(I32), cut(k.x1, tiles, tiles).bitcast(I32)
        k.src_f, k.dst_f, k.src_hi, k.src_lo = (cut(k.x1, j * tiles, tiles) for j in range(2, 6))
        k.s_msg = cut(k.x1, 0, 1024).rearrange("p (o u f) -> p o u f", o=2, u=U)
        k.s_rel = cut(k.x1, 1024, 256)[0:k.relations, :].rearrange("p (c f) -> p c f", c=4)
        k.s_type_at = cut(k.x1, 1280, 4)
        k.s_hot_type = cut(k.acc, 0, 4 * GE)[0:k.relations, :].bitcast(BF16).rearrange("p (o c e u) -> p o c e u", o=2, c=4, u=U)
        k.s_types_h = cut(k.acc, 4 * GE, GE).bitcast(F16).rearrange("p (o e) -> p o e", o=2)
        k.s_types = more[:, 0:2 * GE].bitcast(I32).rearrange("p (o e) -> p o e", o=2)
        k.s_src = cut(k.x1, 2048, 2048).bitcast(I32).rearrange("p (o e u) -> p o e u", o=2, u=U)
        k.s_dst = cut(k.x1, 4096, 2048).bitcast(I32).rearrange("p (o e) -> p o e", o=2)
        k.s_hot_t = cut(k.x1, 6144, 2048).rearrange("p (o e u) -> p o e u", o=2, u=U)
        k.s_same = cut(k.x1, 8192, 2048).rearrange("p (o u e) -> p o u e", o=2, u=U)
        k.s_earlier = cut(k.x1, 10240, 1024).rearrange("p (u e) -> p u e", u=U)
        k.s_win = cut(k.x1, 11264, 128).rearrange("p (o f) -> p o f", o=2)
        k.s_repeat, k.s_at = cut(k.x1, 11392, U), cut(k.x1, 11392 + U, U)
        k.s_idx = cut(k.x1, 11392 + 2 * U, SLOTS * U).bitcast(I32).rearrange("p (s u) -> p s u", s=SLOTS)
        k.s_out = work[:, 0:SLOTS * U * 64].rearrange("p (s u f) -> p s u f", s=SLOTS, u=U)
        k.s_src_f, k.s_to, k.s_weight = (cut(k.acc, behind + j * tiles, tiles) for j in range(3))
        k.s_before = cut(k.acc, behind + 3 * tiles, P)
        k.m_u = cut(k.x1, 0, 4096).rearrange("p (s u f) -> p s u f", s=SLOTS, u=U)
        k.m_hot_t = cut(k.x1, 4096, 2048).rearrange("p (o e u) -> p o e u", o=2, u=U)
        k.m_dst = cut(k.x1, 6144, 2048).bitcast(I32).rearrange("p (o e) -> p o e", o=2)
        k.m_ea = cut(k.x1, 8192, 512).rearrange("p (o c) -> p o c", o=2)
        k.m_ea_t = cut(k.x1, 8704, 512).rearrange("p (o c) -> p o c", o=2)
        k.m_v = cut(k.x1, 9216, 256).rearrange("p (o c) -> p o c", o=2)
        k.m_relu = cut(k.x1, 9472, 2048).rearrange("p (o u f) -> p o u f", o=2, u=U)
        k.ps = ctx.enter_context(nc.psum_tensor("ps", [P, 8, 512], F32))

        k.gather_sems = [[ctx.enter_context(nc.semaphore(f"gathered_{j}_{s}")) for s in range(SLOTS)] for j in range(6)]
        k.scattered_in = [ctx.enter_context(nc.semaphore(f"scattered_in_{j}")) for j in range(SCATTERS)]
        k.pass_sems, k.phase_sems, k.open_phases = [], [], ctx.enter_context(ExitStack())

        def sem(name):
            k.pass_sems.append(ctx.enter_context(nc.semaphore(name)))
            return k.pass_sems[-1]

        slots = lambda name: [sem(f"{name}_{s}") for s in range(SLOTS)]
        k.same_ready = slots("same_ready")
        k.types_ready = slots("types_ready")
        k.idx_out = slots("idx_out")
        k.msg_done = slots("msg_done")
        k.from_dst = slots("from_dst")
        k.merged = slots("merged")
        k.out_ready = slots("out_ready")
        k.out_free = slots("out_free")
        k.idx_ready = slots("idx_ready")
        k.group_done = slots("group_done")
        k.summed = slots("summed")
        k.hot_ready = slots("hot_ready")
        k.msg_ready = slots("msg_ready")
        k.loaded = slots("loaded")
        k.window_loaded = slots("window_loaded")
        k.pre_half = slots("pre_half")
        k.pre_done = slots("pre_done")
        k.ea_turned = slots("ea_turned")
        k.ea_ready = slots("ea_ready")
        k.hot_t_ready = slots("hot_t_ready")
        k.summed_half = slots("summed_half")
        k.relued = slots("relued")
        k.paced = sem("paced")
        k.dve_step = sem("dve_step")
        k.repeat_step = sem("repeat_step")
        k.table_step = sem("table_step")
        k.tables_ready = sem("tables_ready")
        k.loads_issued = sem("loads_issued")
        k.loaded_rest = sem("loaded_rest")

        load_and_index(nc, k, a)
        count_src(nc, k)
        norm_relu(nc, k, "norm0", scale=k.inv_s, add_to_x=True, clear_acc=True, ones=True)
        sum_by_dst(nc, k, k.table[0:n, :], 65)
        add_adaptive_sum(nc, k)
        norm_relu(nc, k, "norm1", scale=k.inv_d, add_to_x=True, inv_from=k.deg_d)
        start_acc(nc, k)
        sum_by_dst(nc, k, k.table[0:n, :], 64)
        convolve_wide(nc, k, "first", k.w1, k.b1, k.w2, residual=False)
        sum_by_dst(nc, k, k.table[0:n, :], 64)
        convolve_second(nc, k)
        sum_by_dst(nc, k, k.table[0:n, :], 64)
        convolve_wide(nc, k, "third", k.w3, k.b3, k.w4, residual=True)
        sum_by_dst(nc, k, k.table[0:n, :], 64)
        add_fourth(nc, k)
        norm_relu(nc, k, "norm2", clear_acc=True)
        scatter_to_src(nc, k)
        add_scattered(nc, k)
        norm_relu(nc, k, "norm3", clear_acc=True)
        message_tables(nc, k)
        sum_messages(nc, k, a.edge_attr_32, a.dst)
        update_nodes(nc, k, out)


_INS = ["x", "src", "dst", "edge_attr_32", "edge_type_500", "edge_weight", "L0_gnn_adaptive_weight",
        "L1_gnn_W1", "L1_gnn_b1", "L1_gnn_W2", "L1_gnn_b2", "L1_gnn_W3", "L1_gnn_b3", "L1_gnn_W4", "L1_gnn_b4",
        "L2_gnn_rel_embed", "L3_gnn_mW1", "L3_gnn_mb1", "L3_gnn_mW2", "L3_gnn_mb2",
        "L3_gnn_uW1", "L3_gnn_ub1", "L3_gnn_uW2", "L3_gnn_ub2"]


def kernel(**inputs):
    import numpy as _np
    import concourse.bacc as _bacc
    from concourse import mybir as _mybir
    from concourse.bass_utils import run_bass_kernel_spmd as _run

    nc = _bacc.Bacc("TRN2", target_bir_lowering=False, num_devices=1)
    arrays, args = {}, []
    for name in _INS:
        v = _np.ascontiguousarray(inputs[name])
        arrays[f"in_{name}"] = v
        args.append(nc.dram_tensor(f"in_{name}", v.shape, _mybir.dt.from_np(v.dtype), kind="ExternalInput").ap())
    out = nc.dram_tensor("out_x", arrays["in_x"].shape, _mybir.dt.float32, kind="ExternalOutput").ap()
    bass_four_graph_layers(nc, *args, out)
    return _run(nc, [arrays], core_ids=[0]).results[0]["out_x"]
```

```python
from contextlib import ExitStack

import concourse.bass as bass
from concourse import mybir

F32, I32, BF16, F16 = mybir.dt.float32, mybir.dt.int32, mybir.dt.bfloat16, mybir.dt.float16
ALU = mybir.AluOpType
ACT = mybir.ActivationFunctionType
AX = mybir.AxisListType

P = 128
U = 8
GE = P * U
SLOTS = 4
PADDED = 65536
ROUND = 12582912.0
EPS = 1e-5
SCATTERS = U
KB = 4


class Names:
    pass


def feature_major(acc, rows, n, nb):
    return acc[0:rows, 0:n].rearrange("f (p b) -> f b p", b=nb)




def over_windows(eng, k, window, between=None):
    window(0)
    spread = eng.value_load(k.spread_i[0:1, 0:1], min_val=0, max_val=1)
    with eng.If(spread):
        with eng.Fori(1, k.windows) as w:
            if between:
                between(w)
            window(w)


def over_groups(eng, k, w, body):
    if k.rounds > 1:
        with eng.Fori(0, k.rounds - 1) as i:
            body(i, w * k.rounds + i)
    body(k.rounds - 1, w * k.rounds + (k.rounds - 1))


def phase_sems(nc, k, *names):
    made = [k.open_phases.enter_context(nc.semaphore(name)) for name in names]
    k.phase_sems += made
    return made


def clear(nc, k):
    nc.all_engine_barrier()
    first = None
    nums = sorted(s.num for s in k.pass_sems + k.phase_sems)
    for at, num in enumerate(nums):
        first = num if first is None else first
        if at == len(nums) - 1 or nums[at + 1] != num + 1:
            nc.gpsimd.sem_clear(range(first, num + 1))
            first = None
    nc.all_engine_barrier()
    k.open_phases.close()
    k.phase_sems = []


def edge_parts(k, tile, dram):
    full = (k.groups - 1) * GE
    whole, rest = divmod(k.e - full, U)
    parts = [(tile[:, 0:(k.groups - 1) * U].rearrange("p (g u) -> p g u", u=U),
              dram[0:full].rearrange("(g p u) -> p g u", p=P, u=U))]
    last = tile[:, (k.groups - 1) * U:k.groups * U]
    if whole:
        parts.append((last[0:whole, :], dram[full:full + whole * U].rearrange("(p u) -> p u", u=U)))
    if rest:
        parts.append((last[whole:whole + 1, 0:rest], dram[k.e - rest:k.e].rearrange("(a u) -> a u", a=1)))
    return parts


def load_and_index(nc, k, a):
    pads_set, edges_loaded, rest_loaded = phase_sems(nc, k, "pads_set", "edges_loaded", "rest_loaded")
    iota_made, extremes, reduced, step = phase_sems(nc, k, "iota_made", "extremes", "reduced", "index_step")
    zeroed, pads_ready = phase_sems(nc, k, "zeroed", "pads_ready")

    with nc.Block() as block:
        src_i, dst_i, src_f, dst_f = k.src_i, k.dst_i, k.src_f, k.dst_f
        G = k.groups

        edge = [part for tile, dram in ((src_i, a.src), (dst_i, a.dst)) for part in edge_parts(k, tile, dram)]
        late = edge_parts(k, k.wgt, a.edge_weight)
        late += [(pad[0:k.e].rearrange("(p n) -> p n", p=4), of.rearrange("(p n) -> p n", p=4))
                 for pad, of in zip(k.edge_pad, (a.src, a.dst, a.edge_type_500))]
        for table in k.scattered:
            late += [(table[0:k.n, :].rearrange("(p b) f -> p b f", b=k.nb), k.zeros[0:k.m, :].unsqueeze(1).to_broadcast([k.m, k.nb, 64])),
                     (table[k.n:k.n + P, :], k.zeros[:, :]), (table[k.n + P:k.n + P + 1, :], k.zeros[0:1, :])]
        k.late_loads = len(late)
        row = lambda v, n: v.rearrange("(a n) -> a n", a=1).to_broadcast([n, v.shape[0]])
        col = lambda v: v.rearrange("(n a) -> n a", a=1)
        rest = [(k.x[:, :, :], a.x.rearrange("(p b) f -> p b f", b=k.nb)),
                (k.w1[:, :], a.L1_gnn_W1), (k.w2[:, :], a.L1_gnn_W2), (k.w3[:, :], a.L1_gnn_W3), (k.w4[:, :], a.L1_gnn_W4),
                (k.b1[:, :], col(a.L1_gnn_b1)), (k.b3[:, :], col(a.L1_gnn_b3)),
                (k.b2[:, :], col(a.L1_gnn_b2)), (k.b4[:, :], col(a.L1_gnn_b4)),
                (k.w_uv[:, 0:128], a.L3_gnn_mW1[0:64, :]), (k.w_uv[:, 128:256], a.L3_gnn_mW1[64:128, :]),
                (k.mb1[:, :], row(a.L3_gnn_mb1, P)), (k.mw2[:, :], a.L3_gnn_mW2), (k.mb2[:, :], row(a.L3_gnn_mb2, P)),
                (k.uw1[:, :], a.L3_gnn_uW1), (k.ub1[:, :], col(a.L3_gnn_ub1)), (k.uw2[:, :], a.L3_gnn_uW2),
                (k.ub2[:, :], row(a.L3_gnn_ub2, P)),
                (k.adapt[:, :], row(a.L0_gnn_adaptive_weight, P))]
        diag = [(k.we[32 * q:32 * q + 32, 128 * q:128 * q + 128], a.L3_gnn_mW1[128:160, :]) for q in range(4)]

        @block.sync
        def _(sp):
            sp.wait_ge(pads_set, 1)
            for to, of in edge:
                sp.dma_start(to, of).then_inc(edges_loaded, 16)
            for to, of in rest:
                sp.dma_start(to, of).then_inc(rest_loaded, 16)
            sp.wait_ge(pads_ready, 1)
            sp.wait_ge(zeroed, 3)
            fill = k.groups * GE - k.e
            fills = k.fill[0:1, 0:fill], k.fill[0:1, 0:fill], k.acc[0:1, 0:fill].bitcast(I32)
            stored = len(fills) + 1
            for pad, with_ in zip(k.edge_pad, fills):
                sp.dma_start(pad[k.e:k.e + fill].rearrange("(a n) -> a n", a=1), with_).then_inc(rest_loaded, 16)
            sp.dma_start(k.table[k.n:k.n + P, :], k.zeros[:, :]).then_inc(rest_loaded, 16)
            for to, of in diag:
                sp.dma_start(to, of).then_inc(rest_loaded, 16)
            for to, of in late:
                sp.dma_start(to, of).then_inc(k.late_loaded, 16)
            sp.wait_ge(rest_loaded, 16 * (len(rest) + stored + len(diag)))

        @block.gpsimd
        def _(pool):
            nc.gpsimd.iota(k.row_i[:, :], pattern=[[1, P]], base=0, channel_multiplier=0).then_inc(iota_made, 1)
            nc.gpsimd.iota(k.part_i[:, :], pattern=[[0, 1]], base=0, channel_multiplier=1).then_inc(iota_made, 1)
            pool.wait_ge(extremes, 1)
            nc.gpsimd.partition_all_reduce(k.base[:, 0:2 * G], k.ends[:, 0:2 * G], P, bass.bass_isa.ReduceOp.max).then_inc(reduced, 1)

        @block.vector
        def _(dve):
            done = [0]

            def then(ins):
                done[0] += 1
                ins.then_inc(step, 1)
                dve.wait_ge(step, done[0])

            last = slice((G - 1) * U, G * U)
            then(nc.vector.memset(src_i[:, last], PADDED))
            then(nc.vector.memset(dst_i[:, last], PADDED))
            nc.vector.memset(k.wgt[:, last], 0.0).then_inc(pads_set, 1)
            nc.vector.memset(k.fill[0:1, :], PADDED).then_inc(pads_ready, 1)
            nc.vector.memset(k.we[:, :], 0.0).then_inc(zeroed, 1)
            nc.vector.memset(k.zeros[:, :], 0.0).then_inc(zeroed, 1)
            nc.vector.memset(k.acc[0:1, 0:GE], 0.0).then_inc(zeroed, 1)
            dve.wait_ge(iota_made, 2)
            then(nc.vector.tensor_copy(k.row_f[:, :], k.row_i[:, :]))
            then(nc.vector.tensor_copy(k.part_f[:, :], k.part_i[:, :]))
            then(nc.vector.tensor_scalar(k.ident[:, :], k.row_f[:, :], k.part_f[:, 0:1], None, ALU.is_equal))
            dve.wait_ge(edges_loaded, 16 * len(edge))
            then(nc.vector.tensor_copy(src_f[:, :], src_i[:, :]))
            then(nc.vector.tensor_copy(dst_f[:, :], dst_i[:, :]))
            then(nc.vector.scalar_tensor_tensor(k.idx[:, :], src_f[:, :], float(PADDED), src_f[:, :], ALU.is_lt, ALU.mult))
            then(nc.vector.tensor_reduce(k.ends[:, 0:G], dst_f.rearrange("p (g u) -> p g u", u=U), AX.X, ALU.min, negate=True))
            then(nc.vector.scalar_tensor_tensor(k.src_hi[:, :], dst_f[:, :], float(PADDED), dst_f[:, :], ALU.is_lt, ALU.mult))
            nc.vector.tensor_reduce(k.ends[:, G:2 * G], k.src_hi.rearrange("p (g u) -> p g u", u=U), AX.X, ALU.max).then_inc(extremes, 1)
            dve.wait_ge(reduced, 1)
            then(nc.vector.tensor_tensor(k.base[:, G:2 * G], k.base[:, G:2 * G], k.base[:, 0:G], ALU.add))
            then(nc.vector.tensor_reduce(k.spread_f[:, 0:1], k.base[:, G:2 * G], AX.X, ALU.max))
            then(nc.vector.tensor_scalar(k.spread_f[:, 0:1], k.spread_f[:, 0:1], float(P), None, ALU.is_ge))
            then(nc.vector.tensor_copy(k.spread_i[:, :], k.spread_f[:, 0:1]))
            then(nc.vector.tensor_scalar(k.spread_f[:, 0:1], k.spread_f[:, 0:1], 1.0, None, ALU.subtract))
            then(nc.vector.tensor_scalar(k.base[:, 0:G], k.base[:, 0:G], k.spread_f[:, 0:1], None, ALU.mult))
            then(nc.vector.tensor_copy(k.base_i[:, :], k.base[:, 0:G]))
            then(nc.vector.tensor_scalar(k.pos[:, :], k.base[:, 0:G], k.part_f[:, 0:1], None, ALU.add))
            then(nc.vector.tensor_tensor(k.rel.rearrange("p (g u) -> p g u", u=U), dst_f.rearrange("p (g u) -> p g u", u=U),
                                         k.base[:, 0:G].unsqueeze(2).to_broadcast([P, G, U]), ALU.subtract))
            then(nc.vector.tensor_scalar(k.src_hi[:, :], src_f[:, :], 1.0 / k.nb, -(k.nb - 1) / (2.0 * k.nb), ALU.mult, ALU.add))
            then(nc.vector.tensor_scalar(k.src_hi[:, :], k.src_hi[:, :], ROUND, None, ALU.add))
            then(nc.vector.tensor_scalar(k.src_hi[:, :], k.src_hi[:, :], ROUND, None, ALU.subtract))
            then(nc.vector.scalar_tensor_tensor(k.src_lo[:, :], k.src_hi[:, :], -float(k.nb), src_f[:, :], ALU.mult, ALU.add))


def count_src(nc, k):
    digits, counted, copied, step, rooted = phase_sems(nc, k, "digits_ready", "counted", "digits_copied", "degree_step", "rooted")
    slot = lambda at: k.acc[:, at * P * U:(at + 1) * P * U].bitcast(F16).rearrange("p (s n u) -> p s n u", s=2, u=U)
    hi, lo = slot(0), slot(1)
    column = k.acc[:, 2 * P * U:2 * P * U + P * U // 2].bitcast(F16).rearrange("p (n u) -> p n u", u=U)
    hi_digit, lo_digit = (digit.bitcast(F16)[:, 0:k.groups * U] for digit in (k.src_i, k.dst_i))

    with nc.Block() as block:
        M, NB = k.m, k.nb

        @block.vector
        def _(dve):
            def one_hots(g, s):
                for out, digit, n in ((hi, hi_digit, M), (lo, lo_digit, NB)):
                    ins = nc.vector.tensor_tensor(out[:, s, 0:n, :], column[:, 0:n, :], digit[:, bass.ds(g * U, U)].unsqueeze(1).to_broadcast([P, n, U]),
                                                  ALU.is_equal)
                ins.then_inc(digits, 1)

            nc.vector.tensor_copy(column, k.row_f[:, :].unsqueeze(2).to_broadcast([P, P, U])).then_inc(copied, 1)
            nc.vector.tensor_copy(hi_digit, k.src_hi[:, :]).then_inc(copied, 1)
            nc.vector.tensor_copy(lo_digit, k.src_lo[:, :]).then_inc(copied, 1)
            dve.wait_ge(copied, 3)
            one_hots(0, 0)
            one_hots(1, 1)
            with dve.Fori(1, k.groups // 2) as i:
                for s in range(2):
                    g = 2 * i + s
                    dve.wait_ge(counted, g - 1)
                    one_hots(g, s)
            dve.wait_ge(counted, k.groups)
            nc.vector.tensor_scalar(k.inv_s[:, :], k.ps[0:M, 0, 0:NB], 1.0, None, ALU.max).then_inc(step, 1)
            nc.vector.tensor_scalar(k.deg_s[:, :], k.ps[0:M, 0, 0:NB], 0.0, None, ALU.is_gt).then_inc(step, 1)
            dve.wait_ge(rooted, 1)
            nc.vector.reciprocal(k.inv_s[:, :], k.inv_s[:, :]).then_inc(step, 1)
            dve.wait_ge(step, 3)
            nc.vector.tensor_tensor(k.inv_s[:, :], k.inv_s[:, :], k.deg_s[:, :], ALU.mult).then_inc(step, 1)

        @block.tensor
        def _(pe):
            def count(g, s, first=False, last=False):
                pe.wait_ge(digits, g + 1)
                for u in range(U):
                    ins = nc.tensor.matmul(k.ps[0:M, 0, 0:NB], hi[:, s, 0:M, u], lo[:, s, 0:NB, u], start=first and u == 0, stop=last and u == U - 1,
                                           skip_group_check=True)
                ins.then_inc(counted, 1)

            count(0, 0, first=True)
            count(1, 1)
            with pe.Fori(1, k.groups // 2 - 1) as i:
                for s in range(2):
                    count(2 * i + s, s)
            count(k.groups - 2, 0)
            count(k.groups - 1, 1, last=True)

        @block.scalar
        def _(act):
            act.wait_ge(step, 1)
            nc.scalar.activation(k.inv_s[:, :], k.inv_s[:, :], ACT.Sqrt).then_inc(rooted, 1)


def norm_relu(nc, k, name, scale=None, add_to_x=False, inv_from=None, clear_acc=False, ones=False, store=True, late=False):
    centered, squared, summed, t_ready = phase_sems(nc, k, f"{name}_centered", f"{name}_squared", f"{name}_summed", f"{name}_t_ready")
    step, rooting, rooted, stored, acc_clear = phase_sems(nc, k, f"{name}_step", f"{name}_rooting", f"{name}_rooted", f"{name}_stored", f"{name}_acc_clear")
    ones_set, = phase_sems(nc, k, f"{name}_ones_set")
    inv_turned, inv_copied, inv_stored = phase_sems(nc, k, f"{name}_inv_turned", f"{name}_inv_copied", f"{name}_inv_stored")
    M, NB = k.m, k.nb
    sq = k.x1[0:M, 0:NB * 64].rearrange("p (b f) -> p b f", f=64)
    quarter = NB // 4
    parts = [slice(q * quarter, (q + 1) * quarter if q < 3 else NB) for q in range(4)]
    wide = lambda v, part: v[:, part].unsqueeze(2).to_broadcast([M, part.stop - part.start, 64])

    with nc.Block() as block:

        @block.vector
        def _(dve):
            done = [0]

            def then(ins):
                done[0] += 1
                ins.then_inc(step, 1)
                dve.wait_ge(step, done[0])

            if inv_from is not None:
                nc.vector.tensor_scalar(k.inv_d[:, :], inv_from[:, :], 1.0, None, ALU.add).then_inc(rooting, 1)
                dve.wait_ge(rooted, 1)
                then(nc.vector.reciprocal(k.inv_d[:, :], k.inv_d[:, :]))
            then(nc.vector.tensor_reduce(k.mean[:, :], k.x[:, :, :], AX.X, ALU.add))
            then(nc.vector.tensor_scalar(k.mean[:, :], k.mean[:, :], 1.0 / 64, None, ALU.mult))
            for part in parts:
                nc.vector.tensor_tensor(k.t[:, part, :], k.x[:, part, :], wide(k.mean, part), ALU.subtract).then_inc(centered, 1)
            for q, part in enumerate(parts):
                dve.wait_ge(squared, q + 1)
                nc.vector.tensor_reduce(k.var[:, part], sq[:, part, :], AX.X, ALU.add).then_inc(summed, 1)
            dve.wait_ge(summed, 4)
            n = 1 + (inv_from is not None)
            nc.vector.tensor_scalar(k.var[:, :], k.var[:, :], 1.0 / 64, EPS, ALU.mult, ALU.add).then_inc(rooting, 1)
            dve.wait_ge(rooted, n)
            then(nc.vector.reciprocal(k.var[:, :], k.var[:, :]))
            for q, part in enumerate(parts):
                t, x = k.t[:, part, :], k.x[:, part, :]
                then(nc.vector.tensor_tensor(t, t, wide(k.var, part), ALU.mult))
                if add_to_x:
                    then(nc.vector.scalar_tensor_tensor(x, t, 0.0, x, ALU.max, ALU.add))
                if scale is not None:
                    nc.vector.scalar_tensor_tensor(t, t, 0.0, wide(scale, part), ALU.max, ALU.mult).then_inc(t_ready, 1)
                else:
                    nc.vector.tensor_scalar(t, t, 0.0, None, ALU.max).then_inc(t_ready, 1)
            if ones:
                nc.vector.memset(k.rows[:, :, :, 64], 1.0).then_inc(ones_set, 1)

        @block.gpsimd
        def _(pool):
            if clear_acc:
                nc.gpsimd.memset(k.acc[:, :], 0.0).then_inc(acc_clear, 1)

        if inv_from is not None:
            @block.tensor
            def _(pe):
                pe.wait_ge(step, 1)
                nc.tensor.transpose(k.ps[0:NB, 0, 0:M], k.inv_d[:, :], k.ident[0:M, 0:M]).then_inc(inv_turned, 1)

        @block.scalar
        def _(act):
            n = 0
            if inv_from is not None:
                n = 1
                act.wait_ge(rooting, 1)
                nc.scalar.activation(k.inv_d[:, :], k.inv_d[:, :], ACT.Sqrt).then_inc(rooted, 1)
                act.wait_ge(inv_turned, 1)
                nc.scalar.copy(k.inv_turned, k.ps[0:NB, 0, 0:M]).then_inc(inv_copied, 1)
            for q, part in enumerate(parts):
                act.wait_ge(centered, q + 1)
                nc.scalar.activation(sq[:, part, :], k.t[:, part, :], ACT.Square).then_inc(squared, 1)
            act.wait_ge(rooting, n + 1)
            nc.scalar.activation(k.var[:, :], k.var[:, :], ACT.Sqrt).then_inc(rooted, 1)

        @block.sync
        def _(sp):
            if late:
                sp.wait_ge(k.late_loaded, 16 * k.late_loads)
            if inv_from is not None:
                sp.wait_ge(inv_copied, 1)
                sp.dma_start(k.inv_row.rearrange("(b p) -> b p", p=M), k.inv_turned).then_inc(inv_stored, 16)
                sp.wait_ge(inv_stored, 16)
            if store:
                for q, part in enumerate(parts):
                    sp.wait_ge(t_ready, q + 1)
                    sp.dma_start(k.table_rows[:, part, :], k.t[:, part, :]).then_inc(stored, 16)
                sp.wait_ge(stored, 64)


def sum_by_dst(nc, k, table, width):
    clear(nc, k)
    gathered = k.gather_sems.pop()
    with nc.Block() as block:
        rows, oh, ps = k.rows, k.one_hot, k.ps

        @block.gpsimd
        def _(pool):
            def body(i, r):
                for s in range(SLOTS):
                    pool.wait_ge(k.idx_ready[s], r + 1)
                    pool.sem_inc(k.paced, 1)
                    for u in range(U):
                        nc.gpsimd.indirect_dma_start(rows[:, s, u, 0:64], None, table,
                                                     bass.IndirectOffsetOnAxis(k.idx_slot[:, s, u:u + 1], 0)).then_inc(gathered[s], 16)

            over_windows(pool, k, lambda w: over_groups(pool, k, w, body))

        @block.scalar
        def _(act):
            def body(i, r):
                for s in range(SLOTS):
                    at = bass.ds((SLOTS * i + s) * U, U)
                    act.wait_ge(k.group_done[s], r + 1)
                    nc.scalar.copy(k.idx_slot[:, s, :], k.idx[:, at]).then_inc(k.idx_ready[s], 1)

            over_windows(act, k, lambda w: over_groups(act, k, w, body))

        @block.tensor
        def _(pe):
            for s in range(SLOTS):
                pe.sem_inc(k.group_done[s], 1)

            def body(i, r):
                for s in range(SLOTS):
                    pe.wait_ge(gathered[s], 16 * U * (r + 1))
                    pe.wait_ge(k.hot_ready[s], r + 1)
                    pe.wait_ge(k.summed[s], r + 1)
                    for u in range(U):
                        ins = nc.tensor.matmul(ps[0:width, s, 0:P], rows[:, s, u, 0:width], oh[:, s % 2, u, :], start=u == 0, stop=u == U - 1)
                    ins.then_inc(k.group_done[s], 1)

            over_windows(pe, k, lambda w: over_groups(pe, k, w, body))

        @block.vector
        def _(dve):
            for s in range(SLOTS):
                dve.sem_inc(k.summed[s], 1)

            def body(i, r):
                for s in range(SLOTS):
                    g = SLOTS * i + s
                    dve.wait_ge(k.group_done[(s + 2) % SLOTS], r + s // 2 + 1)
                    one_hot(nc, k, g, s % 2).then_inc(k.hot_ready[s], 1)
                    base = dve.value_load(k.base_i[0:1, bass.ds(g, 1)], min_val=0, max_val=k.n - 1)
                    dve.wait_ge(k.group_done[s], r + 2)
                    dve.wait_ge(k.summed[(s + 3) % SLOTS], r + (s > 0) + 1)
                    at = k.acc[0:width, bass.ds(base, P)]
                    nc.vector.tensor_tensor(at, at, ps[0:width, s, 0:P], ALU.add).then_inc(k.summed[s], 1)

            walk_windows(nc, k, dve, lambda w: over_groups(dve, k, w, body))


def one_hot(nc, k, g, slot):
    return nc.vector.tensor_tensor(k.one_hot[:, slot, :, :], k.row_f[:, :].unsqueeze(1).to_broadcast([P, U, P]),
                                   k.rel[:, bass.ds(g * U, U)].unsqueeze(2).to_broadcast([P, U, P]), ALU.is_equal)


def walk_windows(nc, k, dve, window, tables_ready=None, used_up=None):
    def move(by, at):
        for table, op in ((k.rel, -by), (k.pos, by), (k.base, by)):
            table = table[:, 0:k.groups] if table is k.base else table[:, :]
            nc.vector.tensor_scalar(table, table, float(op), None, ALU.add).then_inc(k.table_step, 1)
        dve.wait_ge(k.table_step, 4 * at - 1)
        nc.vector.tensor_copy(k.base_i[:, :], k.base[:, 0:k.groups]).then_inc(k.table_step, 1)
        dve.wait_ge(k.table_step, 4 * at)
        dve.sem_inc(k.paced, 1)

    used_up = used_up or k.summed[SLOTS - 1]

    def between(w):
        dve.wait_ge(used_up, w * k.rounds + 1)
        if tables_ready is not None:
            dve.wait_ge(k.loads_issued, w)
        move(P, w)
        if tables_ready is not None:
            dve.sem_inc(tables_ready, 1)

    window(0)
    spread = dve.value_load(k.spread_i[0:1, 0:1], min_val=0, max_val=1)
    with dve.If(spread):
        with dve.Fori(1, k.windows) as w:
            between(w)
            window(w)
        dve.wait_ge(used_up, k.windows * k.rounds + 1)
        if tables_ready is not None:
            dve.wait_ge(k.loads_issued, k.windows)
        move(-P * (k.windows - 1), k.windows)


def blocks(v, at, m, width):
    return v[:, at].unsqueeze(2).to_broadcast([m, KB, width])


def rows_of(v, m, width):
    return v[0:m, 0:width].unsqueeze(1).to_broadcast([m, KB, width])


def staggered(eng, k, *stages):
    steps = k.nb // KB

    def turn(q, i, s):
        for d, stage in reversed(list(enumerate(stages))):
            if stage and (not isinstance(q, int) or 0 <= q - d < steps):
                stage(q - d, i + (s - d) // 4, (s - d) % 4)

    for q in range(4):
        turn(q, q // 4, q % 4)
    whole = max(1, steps // 4)
    if whole > 1:
        with eng.Fori(1, whole) as i:
            for s in range(4):
                turn(4 * i + s, i, s)
    for q in range(4 * whole, steps + len(stages) - 1):
        turn(q, q // 4, q % 4)


def credit(eng, *sems):
    for sem in sems:
        eng.sem_inc(sem, 2)


def acc_step(k, q, rows=64):
    return feature_major(k.acc, rows, k.n, k.nb)[:, bass.ds(q * KB, KB), :]


def columns(v):
    return v.rearrange("f (b p) -> f b p", b=KB)


def stage_acc(nc, k, rows, i, slot=0):
    return nc.scalar.copy(k.stage[0:rows, slot, :, :], feature_major(k.acc, rows, k.n, k.nb)[:, bass.ds(i * KB, KB), :])


def turn_out(nc, k, rows, slot=0):
    for b in range(KB):
        ins = nc.tensor.transpose(node_psum(k, slot)[:, b, 0:rows], k.stage[0:rows, slot, b, :], k.ident[0:rows, 0:rows])
    return ins


def turn_back(nc, k, bank, rows, width):
    for b in range(KB):
        ins = nc.tensor.transpose(k.ps[0:width, bank, k.m * b:k.m * b + k.m], rows[:, b, :], k.ident[0:k.m, 0:k.m])
    return ins


def node_psum(k, slot=0):
    return k.ps[0:k.m, 3 * slot, :].rearrange("p (b f) -> p b f", b=KB)


def add_adaptive_sum(nc, k):
    staged, turned, used, step = phase_sems(nc, k, "adaptive_staged", "adaptive_turned", "adaptive_used", "adaptive_step")

    with nc.Block() as block:
        @block.scalar
        def _(act):
            def stage(q, i, o):
                act.wait_ge(turned, q + 1)
                act.sem_inc(k.paced, 1)
                stage_acc(nc, k, 65, q, o % 2).then_inc(staged, 1)

            staggered(act, k, stage)

        @block.tensor
        def _(pe):
            credit(pe, turned)

            def turn(q, i, o):
                pe.wait_ge(staged, q + 1)
                pe.wait_ge(used, 2 * q + 2)
                pe.sem_inc(k.paced, 1)
                turn_out(nc, k, 65, o % 2).then_inc(turned, 1)

            staggered(pe, k, turn)

        @block.vector
        def _(dve):
            credit(dve, used, used)
            nc.vector.tensor_scalar(k.inv_s[:, :], k.inv_s[:, :], k.adapt[0:k.m, 0:1], None, ALU.mult).then_inc(step, 1)
            dve.wait_ge(step, 1)

            def take(q, i, o):
                at = bass.ds(q * KB, KB)
                rows = k.t_rows[:, o % 2, :, :]
                dve.wait_ge(turned, q + 3)
                nc.vector.tensor_copy(k.deg_d[:, at], node_psum(k, o % 2)[:, :, 64]).then_inc(used, 1)
                nc.vector.tensor_tensor(rows, node_psum(k, o % 2)[:, :, 0:64], blocks(k.inv_s, at, k.m, 64), ALU.mult).then_inc(used, 1)
                dve.wait_ge(used, 2 * q + 6)
                nc.vector.tensor_tensor(k.x[:, at, :], k.x[:, at, :], rows, ALU.add).then_inc(step, 1)
                dve.wait_ge(step, q + 2)

            staggered(dve, k, take)


def start_acc(nc, k):
    copied, turned, placed = phase_sems(nc, k, "start_copied", "start_turned", "start_placed")

    with nc.Block() as block:
        @block.vector
        def _(dve):
            def copy(q, i, o):
                dve.wait_ge(turned, q + 1)
                dve.sem_inc(k.paced, 1)
                nc.vector.tensor_copy(k.plain_rows[:, o % 2, :, :], k.t[:, bass.ds(q * KB, KB), :]).then_inc(copied, 1)

            staggered(dve, k, copy)

        @block.tensor
        def _(pe):
            credit(pe, turned)

            def turn(q, i, o):
                pe.wait_ge(copied, q + 1)
                pe.wait_ge(placed, q + 1)
                pe.sem_inc(k.paced, 1)
                turn_back(nc, k, o % 2, k.plain_rows[:, o % 2, :, :], 64).then_inc(turned, 1)

            staggered(pe, k, turn)

        @block.scalar
        def _(act):
            credit(act, placed)

            def place(q, i, o):
                act.wait_ge(turned, q + 3)
                act.sem_inc(k.paced, 1)
                nc.scalar.copy(acc_step(k, q), columns(k.ps[0:64, o % 2, 0:KB * k.m])).then_inc(placed, 1)

            staggered(act, k, place)


def convolve_wide(nc, k, name, w_in, bias, w_out, residual):
    scaled, hidden, relued, kept, out = phase_sems(nc, k, f"{name}_scaled", f"{name}_hidden", f"{name}_relued", f"{name}_kept", f"{name}_out")
    t_ready, placed, turned, copied, stored = phase_sems(nc, k, f"{name}_t_ready", f"{name}_placed", f"{name}_turned", f"{name}_copied", f"{name}_stored")
    loaded = phase_sems(nc, k, *(f"{name}_scale_loaded_{o}" for o in range(4)))

    C = KB * k.m
    hid_psum = lambda o: k.ps[:, o % 2, 0:C]
    out_psum = lambda o: k.ps[0:64, 2 + o % 2, 0:C]
    h_of = lambda q, o: k.hid[:, o % 2, :] if residual else k.x1[:, bass.ds(q * C, C)]
    with nc.Block() as block:

        @block.sync
        def _(sp):
            def load(q, i, o):
                sp.wait_ge(t_ready, q + 1)
                sp.sem_inc(k.paced, 1)
                sp.dma_start(k.scale[:, o, :], k.inv_row[bass.ds(q * C, C)].rearrange("(a n) -> a n", a=1).to_broadcast([64, C])).then_inc(loaded[o], 16)

            def store(q, i, o):
                sp.wait_ge(copied, q + 3)
                sp.sem_inc(k.paced, 1)
                sp.dma_start(k.table_rows[:, bass.ds(q * KB, KB), :], k.t[:, bass.ds(q * KB, KB), :]).then_inc(stored, 16)

            staggered(sp, k, load, None, None, None, store)
            sp.wait_ge(stored, 16 * (k.nb // KB))

        @block.vector
        def _(dve):
            credit(dve, t_ready, t_ready, kept)

            def scale_sums(q, i, o):
                dve.wait_ge(loaded[o], 16 * i + 16)
                dve.wait_ge(hidden, q + 1)
                nc.vector.tensor_tensor(columns(k.back[0:64, o % 2, :]), acc_step(k, q), columns(k.scale[:, o, :]), ALU.mult).then_inc(scaled, 1)

            def keep(q, i, o):
                if residual:
                    dve.wait_ge(relued, q + 3)
                    nc.vector.tensor_tensor(k.hid[:, o % 2, :], k.hid[:, o % 2, :], k.x1[:, bass.ds(q * C, C)], ALU.add).then_inc(kept, 1)

            def scale_out(q, i, o):
                dve.wait_ge(out, q + 3)
                dve.wait_ge(turned, q + 1)
                dve.wait_ge(placed, q + 1)
                nc.vector.tensor_tensor(k.feature_t[:, o % 2, :], out_psum(o), k.scale[:, o, :], ALU.mult).then_inc(t_ready, 1)

            def finish(q, i, o):
                keep(q, i, o)
                scale_out(q, i, o)

            if residual:
                staggered(dve, k, scale_sums, None, finish)
            else:
                staggered(dve, k, scale_sums, None, scale_out)

        @block.tensor
        def _(pe):
            credit(pe, hidden, out, turned)

            def to_hidden(q, i, o):
                pe.wait_ge(scaled, q + 1)
                pe.wait_ge(relued, q + 1)
                nc.tensor.matmul(hid_psum(o), w_in[:, :], k.back[0:64, o % 2, :], start=True, stop=True).then_inc(hidden, 1)

            def to_out(q, i, o):
                pe.wait_ge(kept if residual else relued, q + 3)
                pe.wait_ge(t_ready, q + 3)
                pe.sem_inc(k.paced, 1)
                nc.tensor.matmul(out_psum(o), w_out[:, :], h_of(q, o), start=True, stop=True).then_inc(out, 1)

            def turn(q, i, o):
                pe.wait_ge(t_ready, q + 5)
                turn_t(nc, k, pe, q, o, copied, turned)

            staggered(pe, k, to_hidden, to_out, turn)

        @block.scalar
        def _(act):
            credit(act, relued, placed, copied)

            def relu(q, i, o):
                act.wait_ge(hidden, q + 3)
                act.wait_ge(out, q + 1)
                act.sem_inc(k.paced, 1)
                nc.scalar.activation(h_of(q, o), hid_psum(o), ACT.Relu, bias=bias[:, 0:1]).then_inc(relued, 1)

            def save(q, i, o):
                act.wait_ge(t_ready, q + 5)
                save_t(nc, k, act, q, o, placed, turned, copied)

            staggered(act, k, relu, None, save)


def turn_t(nc, k, pe, q, o, copied, turned):
    pe.wait_ge(copied, q + 1)
    pe.sem_inc(k.paced, 1)
    for b in range(KB):
        ins = nc.tensor.transpose(t_psum(k, o)[:, b, :], k.feature_t[:, o % 2, k.m * b:k.m * b + k.m], k.ident[0:64, 0:64])
    ins.then_inc(turned, 1)


def save_t(nc, k, act, q, o, placed, turned, copied):
    act.sem_inc(k.paced, 1)
    nc.scalar.copy(acc_step(k, q), columns(k.feature_t[:, o % 2, :])).then_inc(placed, 1)
    act.wait_ge(turned, q + 3)
    act.sem_inc(k.paced, 1)
    nc.scalar.copy(k.t[:, bass.ds(q * KB, KB), :], t_psum(k, o)).then_inc(copied, 1)


def t_psum(k, o):
    return k.ps[0:k.m, 4 + o % 2, 0:KB * 64].rearrange("p (b f) -> p b f", b=KB)


def convolve_second(nc, k):
    scaled, relued, t_ready, placed, turned, copied, stored = phase_sems(
        nc, k, "second_scaled", "second_relued", "second_t_ready", "second_placed", "second_turned", "second_copied", "second_stored")
    loaded = phase_sems(nc, k, *(f"second_scale_loaded_{o}" for o in range(4)))
    C = KB * k.m

    with nc.Block() as block:

        @block.sync
        def _(sp):
            def load(q, i, o):
                sp.wait_ge(t_ready, q + 1)
                sp.sem_inc(k.paced, 1)
                sp.dma_start(k.scale[:, o, :], k.inv_row[bass.ds(q * C, C)].rearrange("(a n) -> a n", a=1).to_broadcast([64, C])).then_inc(loaded[o], 16)

            def store(q, i, o):
                sp.wait_ge(copied, q + 3)
                sp.sem_inc(k.paced, 1)
                sp.dma_start(k.table_rows[:, bass.ds(q * KB, KB), :], k.t[:, bass.ds(q * KB, KB), :]).then_inc(stored, 16)

            staggered(sp, k, load, None, None, None, store)
            sp.wait_ge(stored, 16 * (k.nb // KB))

        @block.vector
        def _(dve):
            credit(dve, t_ready, t_ready)

            def scale_sums(q, i, o):
                dve.wait_ge(loaded[o], 16 * i + 16)
                dve.wait_ge(relued, q + 1)
                nc.vector.tensor_tensor(columns(k.back[0:64, o % 2, :]), acc_step(k, q), columns(k.scale[:, o, :]), ALU.mult).then_inc(scaled, 1)

            def scale_out(q, i, o):
                dve.wait_ge(relued, q + 3)
                dve.wait_ge(turned, q + 1)
                dve.wait_ge(placed, q + 1)
                nc.vector.tensor_tensor(k.feature_t[:, o % 2, :], k.hid[0:64, o % 2, :], k.scale[:, o, :], ALU.mult).then_inc(t_ready, 1)

            staggered(dve, k, scale_sums, scale_out)

        @block.tensor
        def _(pe):
            credit(pe, turned)

            def turn(q, i, o):
                pe.wait_ge(t_ready, q + 5)
                turn_t(nc, k, pe, q, o, copied, turned)

            staggered(pe, k, turn)

        @block.scalar
        def _(act):
            credit(act, relued, placed, copied)

            def relu(q, i, o):
                act.wait_ge(scaled, q + 1)
                act.wait_ge(t_ready, q + 3)
                nc.scalar.activation(k.hid[0:64, o % 2, :], k.back[0:64, o % 2, :], ACT.Relu, bias=k.b2[:, 0:1]).then_inc(relued, 1)

            def save(q, i, o):
                act.wait_ge(t_ready, q + 5)
                save_t(nc, k, act, q, o, placed, turned, copied)

            staggered(act, k, relu, None, save)


def add_fourth(nc, k):
    scaled, relued, turned, added = phase_sems(nc, k, "fourth_scaled", "fourth_relued", "fourth_turned", "fourth_added")
    loaded = phase_sems(nc, k, *(f"fourth_scale_loaded_{o}" for o in range(4)))
    C = KB * k.m

    with nc.Block() as block:

        @block.sync
        def _(sp):
            def load(q, i, o):
                sp.wait_ge(scaled, q + 1)
                sp.sem_inc(k.paced, 1)
                sp.dma_start(k.scale[:, o, :], k.inv_row[bass.ds(q * C, C)].rearrange("(a n) -> a n", a=1).to_broadcast([64, C])).then_inc(loaded[o], 16)

            staggered(sp, k, load)

        @block.vector
        def _(dve):
            credit(dve, scaled, scaled, added)

            def scale_sums(q, i, o):
                dve.wait_ge(loaded[o], 16 * i + 16)
                dve.wait_ge(relued, q + 1)
                nc.vector.tensor_tensor(columns(k.back[0:64, o % 2, :]), acc_step(k, q), columns(k.scale[:, o, :]), ALU.mult).then_inc(scaled, 1)

            def add(q, i, o):
                at = bass.ds(q * KB, KB)
                dve.wait_ge(turned, q + 3)
                nc.vector.tensor_tensor(k.x[:, at, :], k.x[:, at, :], t_psum(k, o), ALU.add).then_inc(added, 1)

            staggered(dve, k, scale_sums, None, add)

        @block.tensor
        def _(pe):
            credit(pe, turned)

            def turn(q, i, o):
                pe.wait_ge(relued, q + 3)
                pe.wait_ge(added, q + 1)
                pe.sem_inc(k.paced, 1)
                for b in range(KB):
                    ins = nc.tensor.transpose(t_psum(k, o)[:, b, :], k.feature_t[:, o % 2, k.m * b:k.m * b + k.m], k.ident[0:64, 0:64])
                ins.then_inc(turned, 1)

            staggered(pe, k, turn)

        @block.scalar
        def _(act):
            credit(act, relued)

            def relu(q, i, o):
                act.wait_ge(scaled, q + 5)
                act.wait_ge(turned, q + 1)
                nc.scalar.activation(k.feature_t[:, o % 2, :], k.back[0:64, o % 2, :], ACT.Relu, bias=k.b4[:, 0:1]).then_inc(relued, 1)

            staggered(act, k, relu)


def scatter_to_src(nc, k):
    clear(nc, k)
    N = k.n
    ps = k.ps
    with nc.Block() as block:

        def later(i, r, s, by):
            return i + (s + by) // SLOTS, r + (s + by) // SLOTS, (s + by) % SLOTS

        def last(i, s, by):
            return isinstance(i, int) and i == k.rounds - 1 and s + by >= SLOTS

        @block.sync
        def _(sp):
            sp.dma_start(k.s_src_f.bitcast(I32).rearrange("p (g u) -> p g u", u=U),
                         k.edge_pad[0].rearrange("(g p u) -> p g u", p=P, u=U)).then_inc(k.loaded_rest, 16)

            sp.dma_start(k.s_rel[:, :, :], k.rel_embed.rearrange("(c p) f -> p c f", p=k.relations)).then_inc(k.loaded_rest, 16)

            def body(i, r):
                for s in range(SLOTS):
                    o, g = s % 2, SLOTS * i + s
                    sp.wait_ge(k.types_ready[(s + 2) % SLOTS], r + s // 2 + 1)
                    sp.wait_ge(k.hot_t_ready[(s + 2) % SLOTS], r + s // 2 + 1)
                    sp.wait_ge(k.same_ready[(s + 2) % SLOTS], r + s // 2 + 1)
                    sp.sem_inc(k.paced, 1)
                    base = sp.value_load(k.base_i[0:1, bass.ds(g, 1)], min_val=0, max_val=N - 1)
                    for to, of in ((k.s_dst[:, o, :], k.edge_pad[1][bass.ds(g * GE, GE)].rearrange("(a n) -> a n", a=1).to_broadcast([P, GE])),
                                   (k.s_src[:, o, :, :].rearrange("p e u -> p (e u)"),
                                    k.edge_pad[0][bass.ds(g * GE, GE)].rearrange("(a n) -> a n", a=1).to_broadcast([P, GE])),
                                   (k.s_types[:, o, :], k.edge_pad[2][bass.ds(g * GE, GE)].rearrange("(a n) -> a n", a=1).to_broadcast([P, GE]))):
                        sp.dma_start(to, of).then_inc(k.loaded[s], 16)
                    sp.wait_ge(k.from_dst[(s + 2) % SLOTS], r + s // 2 + 1)
                    sp.dma_start(k.s_win[:, o, :], k.table[bass.ds(base, P), :]).then_inc(k.window_loaded[s], 16)

            def window(w):
                over_groups(sp, k, w, body)
                sp.sem_inc(k.loads_issued, 1)

            def between(w):
                sp.wait_ge(k.tables_ready, w)
                sp.sem_inc(k.paced, 1)

            over_windows(sp, k, window, between)

        @block.gpsimd
        def _(pool):
            for j in range(SCATTERS):
                pool.dma_start(k.scattered[j][N + P:N + P + 1, :], k.zeros[0:1, :]).then_inc(k.scattered_in[j], 16)
            for s in range(SLOTS - 1):
                pool.sem_inc(k.out_free[s], 1)

            def scatter(i, r, s):
                pool.wait_ge(k.idx_out[s], r + 1)
                pool.wait_ge(k.out_ready[s], r + 2)
                for u in range(U):
                    if u % 2 == 0:
                        for j in range(u, u + 2):
                            pool.wait_ge(k.scattered_in[j], 16 + 16 * (SLOTS * r + s))
                        pool.sem_inc(k.paced, 1)
                    if u == U - 1:
                        pool.sem_inc(k.out_free[(s + SLOTS - 1) % SLOTS], 1)
                    nc.gpsimd.indirect_dma_start(k.scattered[u][:, :], bass.IndirectOffsetOnAxis(k.s_idx[:, s, u:u + 1], 0),
                                                 k.s_out[:, s, u, :], None, compute_op=ALU.add).then_inc(k.scattered_in[u], 16)

            def body(i, r):
                for s in range(SLOTS):
                    scatter(i, r, s)

            def window(w):
                over_groups(pool, k, w, body)
                for j in range(SCATTERS):
                    pool.wait_ge(k.scattered_in[j], 16 + 16 * k.groups * (w + 1))
                pool.sem_inc(k.paced, 1)

            over_windows(pool, k, window)

        @block.scalar
        def _(act):
            for s in range(SLOTS):
                act.sem_inc(k.out_ready[s], 1)
                act.sem_inc(k.types_ready[s], 1)

            def types(i, r, s):
                act.wait_ge(k.loaded[s], 48 * (r + 1))
                act.wait_ge(k.hot_t_ready[(s + 2) % SLOTS], r + s // 2 + 1)
                nc.scalar.copy(k.s_types_h[:, s % 2, :], k.s_types[:, s % 2, :]).then_inc(k.types_ready[s], 1)

            def body(i, r):
                for s in range(SLOTS):
                    if not last(i, s, 2):
                        types(*later(i, r, s, 2))
                    act.wait_ge(k.merged[s], r + 2)
                    act.wait_ge(k.out_free[s], r + 1)
                    nc.scalar.copy(k.s_out[:, s, :, :].rearrange("p u f -> p (u f)"), ps[:, 4 + s % 2, :]).then_inc(k.out_ready[s], 1)

            def window(w):
                types(0, w * k.rounds, 0)
                types(0, w * k.rounds, 1)
                over_groups(act, k, w, body)

            over_windows(act, k, window)

        @block.tensor
        def _(pe):
            for s in range(SLOTS):
                pe.sem_inc(k.merged[s], 1)
                pe.sem_inc(k.from_dst[s], 1)

            def features(i, r, s):
                o = s % 2
                pe.wait_ge(k.window_loaded[s], 16 * (r + 1))
                pe.wait_ge(k.hot_t_ready[s], r + 2)
                pe.wait_ge(k.msg_done[(s + 2) % SLOTS], r + s // 2 + 1)
                for u in range(U):
                    out = ps[:, o, 64 * u:64 * u + 64]
                    for c in range(4):
                        for q in range(3):
                            nc.tensor.matmul(out, k.s_hot_type[:, o, c, :, u], k.rel_parts[:, c, 64 * q:64 * q + 64], start=c + q == 0, stop=False,
                                             skip_group_check=True)
                    ins = nc.tensor.matmul(out, k.s_hot_t[:, o, :, u], k.s_win[:, o, :], start=False, stop=True, skip_group_check=True)
                ins.then_inc(k.from_dst[s], 1)

            def merge(i, r, s):
                o = s % 2
                pe.wait_ge(k.msg_done[s], r + 2)
                pe.wait_ge(k.out_ready[(s + 2) % SLOTS], r + s // 2 + 1)
                for u in range(U):
                    ins = nc.tensor.matmul(ps[:, 4 + o, 64 * u:64 * u + 64], k.s_same[:, o, u, :], k.s_msg[:, o, u, :], start=True, stop=True)
                ins.then_inc(k.merged[s], 1)

            def body(i, r):
                for s in range(SLOTS):
                    if not last(i, s, 1):
                        features(*later(i, r, s, 1))
                    merge(i, r, s)

            def window(w):
                features(0, w * k.rounds, 0)
                over_groups(pe, k, w, body)

            over_windows(pe, k, window)

        @block.vector
        def _(dve):
            for s in range(SLOTS):
                dve.sem_inc(k.msg_done[s], 1)
                dve.sem_inc(k.same_ready[s], 1)
                dve.sem_inc(k.hot_t_ready[s], 1)

            dve.wait_ge(k.loaded_rest, 32)
            high, middle, low = (k.rel_parts[:, :, 64 * q:64 * q + 64] for q in range(3))
            nc.vector.tensor_copy(high, k.s_rel[:, :, :]).then_inc(k.repeat_step, 1)
            dve.wait_ge(k.repeat_step, 1)
            nc.vector.tensor_tensor(k.s_rel[:, :, :], k.s_rel[:, :, :], high, ALU.subtract).then_inc(k.repeat_step, 1)
            dve.wait_ge(k.repeat_step, 2)
            nc.vector.tensor_copy(middle, k.s_rel[:, :, :]).then_inc(k.repeat_step, 1)
            dve.wait_ge(k.repeat_step, 3)
            nc.vector.tensor_tensor(low, k.s_rel[:, :, :], middle, ALU.subtract).then_inc(k.repeat_step, 1)
            for c in range(4):
                nc.vector.tensor_scalar(k.s_type_at[:, c:c + 1], k.part_f[:, :], float(c * k.relations), None, ALU.add).then_inc(k.repeat_step, 1)
            dve.wait_ge(k.repeat_step, 8)
            nc.vector.tensor_copy(k.s_src_f, k.s_src_f.bitcast(I32)).then_inc(k.dve_step, 1)
            nc.vector.tensor_scalar(k.s_before, k.row_f[:, :], k.part_f[:, 0:1], None, ALU.is_lt).then_inc(k.dve_step, 1)
            dve.wait_ge(k.dve_step, 2)
            nc.vector.tensor_scalar(k.s_to, k.s_src_f, float(N + P), float(N), ALU.min, ALU.subtract).then_inc(k.dve_step, 1)
            dve.wait_ge(k.dve_step, 3)
            nc.vector.tensor_scalar(k.s_to, k.s_to, k.part_f[:, 0:1], None, ALU.subtract).then_inc(k.dve_step, 1)
            dve.wait_ge(k.dve_step, 4)

            def one_hots(i, r, s):
                o, g = s % 2, SLOTS * i + s
                dve.wait_ge(k.loaded[s], 48 * (r + 1))
                dve.wait_ge(k.from_dst[(s + 2) % SLOTS], r + s // 2 + 1)
                nc.vector.tensor_scalar(k.s_hot_t[:, o, :, :].rearrange("p e u -> p (e u)"), k.s_dst[:, o, :], k.pos[:, bass.ds(g, 1)], None,
                                        ALU.is_equal)
                dve.wait_ge(k.types_ready[s], r + 2)
                for c in range(4):
                    ins = nc.vector.tensor_scalar(k.s_hot_type[:, o, c, :, :].rearrange("p e u -> p (e u)"), k.s_types_h[0:k.relations, o, :],
                                                  k.s_type_at[0:k.relations, c:c + 1], None, ALU.is_equal)
                ins.then_inc(k.hot_t_ready[s], 1)

            def indices(i, r, s):
                o = s % 2
                tiles = bass.ds((SLOTS * i + s) * U, U)
                count = 8 + 3 * (SLOTS * r + s)
                dve.wait_ge(k.merged[(s + 2) % SLOTS], r + s // 2 + 1)
                nc.vector.tensor_tensor(k.s_same[:, o, :, :], k.s_src[:, o, :, :].rearrange("p e u -> p u e"),
                                        k.s_src_f[:, tiles].unsqueeze(2).to_broadcast([P, U, P]), ALU.is_equal).then_inc(k.same_ready[s], 1)
                dve.wait_ge(k.same_ready[s], r + 2)
                nc.vector.tensor_tensor(k.s_earlier[:, :, :], k.s_same[:, o, :, :], k.s_before.unsqueeze(1).to_broadcast([P, U, P]),
                                        ALU.mult).then_inc(k.repeat_step, 1)
                dve.wait_ge(k.repeat_step, count + 1)
                nc.vector.tensor_reduce(k.s_repeat, k.s_earlier[:, :, :], AX.X, ALU.max).then_inc(k.repeat_step, 1)
                dve.wait_ge(k.repeat_step, count + 2)
                nc.vector.scalar_tensor_tensor(k.s_at, k.s_repeat, 0.0, k.s_to[:, tiles], ALU.is_equal, ALU.mult).then_inc(k.repeat_step, 1)
                dve.wait_ge(k.repeat_step, count + 3)
                dve.wait_ge(k.out_free[s], r + 1)
                nc.vector.tensor_scalar(k.s_idx[:, s, :], k.s_at, k.part_f[:, 0:1], float(N), ALU.add, ALU.add).then_inc(k.idx_out[s], 1)
                dve.wait_ge(k.idx_out[s], r + 1)

            def message(i, r, s):
                o = s % 2
                dve.wait_ge(k.from_dst[s], r + 2)
                dve.wait_ge(k.merged[(s + 2) % SLOTS], r + s // 2 + 1)
                nc.vector.tensor_tensor(k.s_msg[:, o, :, :], ps[:, o, :].rearrange("p (u f) -> p u f", u=U),
                                        k.s_weight[:, bass.ds((SLOTS * i + s) * U, U)].unsqueeze(2).to_broadcast([P, U, 64]),
                                        ALU.mult).then_inc(k.msg_done[s], 1)

            def body(i, r):
                for s in range(SLOTS):
                    if not last(i, s, 1):
                        one_hots(*later(i, r, s, 1))
                    message(i, r, s)
                    if not last(i, s, 1):
                        indices(*later(i, r, s, 1))

            def window(w):
                nc.vector.scalar_tensor_tensor(k.s_weight, k.rel[:, :], 0.0, k.wgt[:, :], ALU.is_ge, ALU.mult).then_inc(k.dve_step, 1)
                dve.wait_ge(k.dve_step, 2 * w + 5)
                nc.vector.scalar_tensor_tensor(k.s_weight, k.rel[:, :], float(P), k.s_weight, ALU.is_lt, ALU.mult).then_inc(k.dve_step, 1)
                dve.wait_ge(k.dve_step, 2 * w + 6)
                one_hots(0, w * k.rounds, 0)
                indices(0, w * k.rounds, 0)
                dve.sem_inc(k.paced, 1)
                over_groups(dve, k, w, body)

            walk_windows(nc, k, dve, window, tables_ready=k.tables_ready, used_up=k.msg_done[SLOTS - 1])


def add_scattered(nc, k):
    loaded, added = phase_sems(nc, k, "tables_loaded", "tables_added")
    halves = k.t[:, :, :], k.acc[0:k.m, 0:k.nb * 64].rearrange("p (b f) -> p b f", b=k.nb)
    with nc.Block() as block:
        @block.sync
        def _(sp):
            for j in range(SCATTERS):
                if j >= 2:
                    sp.wait_ge(added, j - 1)
                if j:
                    sp.wait_ge(loaded, 16 * j)
                sp.dma_start(halves[j % 2], k.scattered[j][0:k.n, :].rearrange("(p b) f -> p b f", b=k.nb)).then_inc(loaded, 16)

        @block.vector
        def _(dve):
            for j in range(SCATTERS):
                dve.wait_ge(loaded, 16 * (j + 1))
                nc.vector.tensor_tensor(k.x[:, :, :], k.x[:, :, :], halves[j % 2], ALU.add).then_inc(added, 1)
                dve.wait_ge(added, j + 1)


def message_tables(nc, k):
    copied, turned, back_copied, multiplied, u_ready, v_ready = phase_sems(
        nc, k, "tables_copied", "tables_turned", "tables_back_copied", "tables_multiplied", "tables_u_ready", "tables_v_ready")
    zeroed, zeros_stored = phase_sems(nc, k, "tables_zeroed", "tables_zeros_stored")
    stored = phase_sems(nc, k, *(f"tables_stored_{o}" for o in range(2)))

    with nc.Block() as block:
        M, C = k.m, KB * k.m
        u_psum, v_psum = (lambda o, bank=bank: k.ps[0:M, bank + o % 2, :].rearrange("p (b f) -> p b f", b=KB) for bank in (2, 4))

        @block.vector
        def _(dve):
            credit(dve, v_ready)
            nc.vector.memset(k.x1[:, 0:P], 0.0).then_inc(zeroed, 1)

            def copy(q, i, o):
                dve.wait_ge(turned, q + 1)
                dve.sem_inc(k.paced, 1)
                nc.vector.tensor_copy(k.plain_rows[:, o % 2, :, :], k.t[:, bass.ds(q * KB, KB), :]).then_inc(copied, 1)

            def add_bias(q, i, o):
                dve.wait_ge(multiplied, q + 3)
                dve.wait_ge(stored[o % 2], 32 * (2 * i + o // 2) + 1)
                nc.vector.tensor_tensor(k.v_rows[:, o % 2, :, :], v_psum(o), rows_of(k.mb1, M, 128), ALU.add).then_inc(v_ready, 1)

            staggered(dve, k, copy, None, add_bias)

        @block.tensor
        def _(pe):
            credit(pe, turned, multiplied)

            def turn(q, i, o):
                pe.wait_ge(copied, q + 1)
                pe.wait_ge(back_copied, q + 1)
                pe.sem_inc(k.paced, 1)
                turn_back(nc, k, o % 2, k.plain_rows[:, o % 2, :, :], 64).then_inc(turned, 1)

            def multiply(q, i, o):
                pe.wait_ge(back_copied, q + 3)
                pe.wait_ge(u_ready, q + 1)
                pe.wait_ge(v_ready, q + 1)
                for half, to in enumerate((u_psum(o), v_psum(o))):
                    for b in range(KB):
                        ins = nc.tensor.matmul(to[:, b, :], k.back[0:64, o % 2, M * b:M * b + M], k.w_uv[:, P * half:P * half + P], start=True, stop=True)
                ins.then_inc(multiplied, 1)

            staggered(pe, k, turn, multiply)

        @block.scalar
        def _(act):
            credit(act, back_copied, u_ready)
            for sem in stored:
                act.sem_inc(sem, 1)

            def back(q, i, o):
                act.wait_ge(turned, q + 3)
                act.wait_ge(multiplied, q + 1)
                act.sem_inc(k.paced, 1)
                nc.scalar.copy(k.back[0:64, o % 2, :], k.ps[0:64, o % 2, 0:C]).then_inc(back_copied, 1)

            def copy_u(q, i, o):
                act.wait_ge(multiplied, q + 3)
                act.wait_ge(stored[o % 2], 32 * (2 * i + o // 2) + 1)
                nc.scalar.copy(k.u_rows[:, o % 2, :, :], u_psum(o)).then_inc(u_ready, 1)

            staggered(act, k, back, None, copy_u)

        @block.sync
        def _(sp):
            sp.wait_ge(zeroed, 1)
            sp.dma_start(k.v_table[k.n:k.n + P, :], k.x1[:, 0:P]).then_inc(zeros_stored, 16)

            def store(q, i, o):
                for table, rows, ready in ((k.u_table, k.u_rows, u_ready), (k.v_table, k.v_rows, v_ready)):
                    sp.wait_ge(ready, q + 3)
                    sp.sem_inc(k.paced, 1)
                    sp.dma_start(table[0:k.n, :].rearrange("(p b) f -> p b f", b=k.nb)[:, bass.ds(q * KB, KB), :],
                                 rows[:, o % 2, :, :]).then_inc(stored[o % 2], 16)

            staggered(sp, k, store)
            steps = k.nb // KB
            sp.wait_ge(stored[0], 32 * ((steps + 1) // 2) + 1)
            sp.wait_ge(stored[1], 32 * (steps // 2) + 1)
            sp.wait_ge(zeros_stored, 16)


def sum_messages(nc, k, edge_attr, dst):
    clear(nc, k)
    gathered = k.gather_sems.pop()
    with nc.Block() as block:
        u_rows, dst_b, ea, ea_t, v_win, hot_t, relu, ps = k.m_u, k.m_dst, k.m_ea, k.m_ea_t, k.m_v, k.m_hot_t, k.m_relu, k.ps
        pre = lambda o, h: ps[:, 2 * o + h, :]
        full = (k.groups - 1) * GE
        H = U // 2

        def later(i, r, s, by):
            return i + (s + by) // SLOTS, r + (s + by) // SLOTS, (s + by) % SLOTS

        def last(i, s, by):
            return isinstance(i, int) and i == k.rounds - 1 and s + by >= SLOTS

        @block.sync
        def _(sp):
            def body(i, r, w=None):
                for s in range(SLOTS):
                    o = s % 2
                    g = SLOTS * i + s
                    sp.wait_ge(k.pre_done[(s + 2) % SLOTS], r + s // 2 + 1)
                    sp.sem_inc(k.paced, 1)
                    base = sp.value_load(k.base_i[0:1, bass.ds(g, 1)], min_val=0, max_val=k.n - 1)
                    if s == SLOTS - 1 and isinstance(i, int) and i == k.rounds - 1:
                        rest = k.e - full
                        parts = [(dst_b[:, o, 0:rest], dst[full:k.e].rearrange("(a n) -> a n", a=1).to_broadcast([P, rest]))]
                        whole, odd = divmod(rest, U)
                        if whole:
                            parts.append((ea[0:whole, o, :], edge_attr[full:full + whole * U, :].rearrange("(p u) f -> p (u f)", u=U)))
                        if odd:
                            parts.append((ea[whole:whole + 1, o, 0:odd * 32], edge_attr[k.e - odd:k.e, :].rearrange("(a u) f -> a (u f)", a=1)))
                        else:
                            parts.append((ea[0:1, o, 0:32], edge_attr[full:full + 1, :]))
                        assert len(parts) == 3
                        first, more = parts[0:2], parts[2]
                    else:
                        first = [(dst_b[:, o, :], dst[bass.ds(g * GE, GE)].rearrange("(a n) -> a n", a=1).to_broadcast([P, GE])),
                                 (ea[:, o, :], edge_attr[bass.ds(g * GE, GE), :].rearrange("(p u) f -> p (u f)", u=U))]
                        more = None
                    for to, of in first + [(v_win[:, o, :], k.v_table[bass.ds(base, P), :])]:
                        sp.dma_start(to, of).then_inc(k.loaded[s], 16)
                    if more:
                        sp.dma_start(*more).then_inc(k.loaded_rest, 16)

            def window(w):
                over_groups(sp, k, w, body)
                sp.wait_ge(k.loaded_rest, 16 * (w + 1))
                sp.sem_inc(k.loads_issued, 1)

            def between(w):
                sp.wait_ge(k.tables_ready, w)
                sp.sem_inc(k.paced, 1)

            over_windows(sp, k, window, between)

        @block.gpsimd
        def _(pool):
            def body(i, r):
                for s in range(SLOTS):
                    pool.wait_ge(k.idx_ready[s], r + 1)
                    pool.sem_inc(k.paced, 1)
                    for u in range(U):
                        nc.gpsimd.indirect_dma_start(u_rows[:, s, u, :], None, k.u_table[:, :],
                                                     bass.IndirectOffsetOnAxis(k.idx_slot[:, s, u:u + 1], 0)).then_inc(gathered[s], 16)

            over_windows(pool, k, lambda w: over_groups(pool, k, w, body))

        @block.scalar
        def _(act):
            def index(i, r, s):
                act.wait_ge(k.summed_half[s], 2 * r + 2)
                nc.scalar.copy(k.idx_slot[:, s, :], k.idx[:, bass.ds((SLOTS * i + s) * U, U)]).then_inc(k.idx_ready[s], 1)

            def features(i, r, s):
                act.wait_ge(k.ea_turned[s], r + 1)
                nc.scalar.copy(ea_t[:, s % 2, :], ps[:, 6, 0:2 * P]).then_inc(k.ea_ready[s], 1)

            def body(i, r):
                for s in range(SLOTS):
                    if not last(i, s, 1):
                        features(*later(i, r, s, 1))
                    for h in range(2):
                        act.wait_ge(k.summed_half[s], 2 * r + 3 + h)
                        half = relu[:, s % 2, h * H:h * H + H, :]
                        nc.scalar.activation(half, half, ACT.Relu).then_inc(k.relued[s], 1)
                    if not last(i, s, 2):
                        index(*later(i, r, s, 2))

            def window(w):
                index(0, w * k.rounds, 0)
                index(0, w * k.rounds, 1)
                features(0, w * k.rounds, 0)
                over_groups(act, k, w, body)

            over_windows(act, k, window)

        @block.tensor
        def _(pe):
            for s in range(SLOTS):
                pe.sem_inc(k.group_done[s], 1)
                pe.sem_inc(k.pre_done[s], 1)

            def before_relu(i, r, s):
                o = s % 2
                pe.wait_ge(k.loaded[s], 48 * (r + 1))
                if last(i, s, 1):
                    pe.wait_ge(k.loaded_rest, 16 * (pe_window[0] + 1))
                for h in range(2):
                    ins = nc.tensor.transpose(ps[:, 6, P * h:P * h + P], ea[:, o, P * h:P * h + P], k.ident[:, :])
                ins.then_inc(k.ea_turned[s], 1)
                pe.wait_ge(k.ea_ready[s], r + 1)
                pe.wait_ge(k.summed_half[(s + 2) % SLOTS], 2 * (r + s // 2) + 2)
                pe.wait_ge(k.hot_t_ready[s], r + 1)
                for h in range(2):
                    nc.tensor.matmul(pre(o, h), ea_t[:, o, P * h:P * h + P], k.we[:, :], start=True, stop=False, skip_group_check=True)
                    for q in range(H):
                        ins = nc.tensor.matmul(pre(o, h)[:, P * q:P * q + P], hot_t[:, o, :, h * H + q], v_win[:, o, :],
                                               start=False, stop=q == H - 1, skip_group_check=True)
                    ins.then_inc(k.pre_half[s] if h == 0 else k.pre_done[s], 1)

            def sums(i, r, s):
                o = s % 2
                pe.wait_ge(k.relued[s], 2 * (r + 1))
                pe.wait_ge(k.hot_ready[s], r + 1)
                pe.wait_ge(k.summed[(s + 2) % SLOTS], r + s // 2 + 1)
                for u in range(U):
                    ins = nc.tensor.matmul(ps[:, 4 + o, 0:P], relu[:, o, u, :], k.one_hot[:, o, u, :], start=u == 0, stop=u == U - 1)
                ins.then_inc(k.group_done[s], 1)

            def body(i, r):
                for s in range(SLOTS):
                    if not last(i, s, 1):
                        before_relu(*later(i, r, s, 1))
                    sums(i, r, s)

            pe_window = [0]

            def window(w):
                pe_window[0] = w
                before_relu(0, w * k.rounds, 0)
                over_groups(pe, k, w, body)

            over_windows(pe, k, window)

        @block.vector
        def _(dve):
            for s in range(SLOTS):
                dve.sem_inc(k.summed[s], 1)
                dve.sem_inc(k.summed_half[s], 2)

            def one_hots(i, r, s):
                o, g = s % 2, SLOTS * i + s
                dve.wait_ge(k.loaded[s], 48 * (r + 1))
                dve.wait_ge(k.pre_done[(s + 2) % SLOTS], r + s // 2 + 1)
                dve.wait_ge(k.group_done[(s + 2) % SLOTS], r + s // 2 + 1)
                nc.vector.tensor_scalar(hot_t[:, o, :, :].rearrange("p e u -> p (e u)"), dst_b[:, o, :], k.pos[:, bass.ds(g, 1)], None,
                                        ALU.is_equal).then_inc(k.hot_t_ready[s], 1)
                one_hot(nc, k, g, o).then_inc(k.hot_ready[s], 1)

            def add_up(i, r, s):
                o = s % 2
                dve.wait_ge(gathered[s], 16 * U * (r + 1))
                dve.wait_ge(k.group_done[(s + 2) % SLOTS], r + s // 2 + 1)
                for h in range(2):
                    dve.wait_ge(k.pre_half[s] if h == 0 else k.pre_done[s], r + 1 + h)
                    nc.vector.tensor_tensor(relu[:, o, h * H:h * H + H, :], pre(o, h).rearrange("p (q f) -> p q f", q=H),
                                            u_rows[:, s, h * H:h * H + H, :], ALU.add).then_inc(k.summed_half[s], 1)

            def add_sums(i, r, s):
                base = dve.value_load(k.base_i[0:1, bass.ds(SLOTS * i + s, 1)], min_val=0, max_val=k.n - 1)
                dve.wait_ge(k.group_done[s], r + 2)
                dve.wait_ge(k.summed[(s + 3) % SLOTS], r + (s > 0) + 1)
                at = k.acc[:, bass.ds(base, P)]
                nc.vector.tensor_tensor(at, at, ps[:, 4 + s % 2, 0:P], ALU.add).then_inc(k.summed[s], 1)

            def body(i, r):
                for s in range(SLOTS):
                    add_up(i, r, s)
                    if s > 0:
                        add_sums(i, r, s - 1)
                    if not last(i, s, 1):
                        one_hots(*later(i, r, s, 1))
                add_sums(i, r, SLOTS - 1)

            def window(w):
                one_hots(0, w * k.rounds, 0)
                over_groups(dve, k, w, body)

            walk_windows(nc, k, dve, window, tables_ready=k.tables_ready)


def update_nodes(nc, k, out):
    staged, mixed, joined, turned, back_copied = phase_sems(nc, k, "update_staged", "update_mixed", "update_joined", "update_turned", "update_back_copied")
    hidden, relued, out_ready, step, added, stored = phase_sems(
        nc, k, "update_hidden", "update_relued", "update_out_ready", "update_step", "update_added", "update_stored")

    with nc.Block() as block:
        M, C = k.m, KB * k.m
        agg = lambda o: k.ps[0:M, o % 2, 0:KB * 64].rearrange("p (b f) -> p b f", b=KB)
        out_psum = lambda o: k.ps[0:M, 6 + o % 2, 0:KB * 64].rearrange("p (b f) -> p b f", b=KB)

        @block.scalar
        def _(act):
            credit(act, back_copied, relued)

            def stage(q, i, o):
                act.wait_ge(mixed, q + 1)
                act.sem_inc(k.paced, 1)
                stage_acc(nc, k, P, q, o % 2).then_inc(staged, 1)

            def back(q, i, o):
                act.wait_ge(turned, q + 3)
                act.wait_ge(hidden, q + 1)
                act.sem_inc(k.paced, 1)
                nc.scalar.copy(k.back[:, o % 2, :], k.ps[:, 2 + o % 2, 0:C]).then_inc(back_copied, 1)

            def relu(q, i, o):
                act.wait_ge(hidden, q + 3)
                act.wait_ge(out_ready, q + 1)
                nc.scalar.activation(k.hid[:, o % 2, :], k.ps[:, 4 + o % 2, 0:C], ACT.Relu, bias=k.ub1[:, 0:1]).then_inc(relued, 1)

            staggered(act, k, stage, None, back, relu)

        @block.tensor
        def _(pe):
            credit(pe, mixed, turned, hidden, out_ready)

            def mix(q, i, o):
                pe.wait_ge(staged, q + 1)
                pe.wait_ge(joined, q + 1)
                for b in range(KB):
                    ins = nc.tensor.matmul(agg(o)[:, b, :], k.stage[:, o % 2, b, :], k.mw2[:, :], start=True, stop=True)
                ins.then_inc(mixed, 1)

            def turn(q, i, o):
                pe.wait_ge(joined, q + 3)
                pe.wait_ge(back_copied, q + 1)
                pe.sem_inc(k.paced, 1)
                turn_back(nc, k, 2 + o % 2, k.v_rows[:, o % 2, :, :], P).then_inc(turned, 1)

            def to_hidden(q, i, o):
                pe.wait_ge(back_copied, q + 3)
                pe.wait_ge(relued, q + 1)
                nc.tensor.matmul(k.ps[:, 4 + o % 2, 0:C], k.uw1[:, :], k.back[:, o % 2, :], start=True, stop=True).then_inc(hidden, 1)

            def to_out(q, i, o):
                pe.wait_ge(relued, q + 3)
                pe.wait_ge(added, q + 1)
                for b in range(KB):
                    ins = nc.tensor.matmul(out_psum(o)[:, b, :], k.hid[:, o % 2, M * b:M * b + M], k.uw2[:, :], start=True, stop=True)
                ins.then_inc(out_ready, 1)

            staggered(pe, k, mix, turn, to_hidden, to_out)

        @block.vector
        def _(dve):
            credit(dve, joined, added)

            def join(q, i, o):
                at = bass.ds(q * KB, KB)
                rows = k.v_rows[:, o % 2, :, :]
                dve.wait_ge(turned, q + 1)
                nc.vector.tensor_tensor(rows[:, :, 64:128], rows_of(k.mb2, M, 64), blocks(k.deg_d, at, M, 64), ALU.mult).then_inc(step, 1)
                nc.vector.tensor_copy(rows[:, :, 0:64], k.t[:, at, :]).then_inc(step, 1)
                dve.wait_ge(mixed, q + 3)
                dve.wait_ge(step, 2 * q + 2)
                nc.vector.tensor_tensor(rows[:, :, 64:128], rows[:, :, 64:128], agg(o), ALU.add).then_inc(joined, 1)

            def add(q, i, o):
                at = bass.ds(q * KB, KB)
                dve.wait_ge(out_ready, q + 3)
                nc.vector.tensor_tensor(k.x[:, at, :], k.x[:, at, :], out_psum(o), ALU.add).then_inc(added, 1)

            nc.vector.tensor_tensor(k.x[:, :, :], k.x[:, :, :], k.ub2[0:M, :].unsqueeze(1).to_broadcast([M, k.nb, 64]), ALU.add).then_inc(k.dve_step, 1)
            dve.wait_ge(k.dve_step, 1)
            staggered(dve, k, join, None, None, add)

        @block.sync
        def _(sp):
            def store(q, i, o):
                at = bass.ds(q * KB, KB)
                sp.wait_ge(added, q + 3)
                sp.sem_inc(k.paced, 1)
                sp.dma_start(out.rearrange("(p b) f -> p b f", b=k.nb)[:, at, :], k.x[:, at, :]).then_inc(stored, 16)

            staggered(sp, k, store)
            sp.wait_ge(stored, 16 * (k.nb // KB))


def bass_four_graph_layers(
        nc, x, src, dst, edge_attr_32, edge_type_500, edge_weight, L0_gnn_adaptive_weight,
        L1_gnn_W1, L1_gnn_b1, L1_gnn_W2, L1_gnn_b2, L1_gnn_W3, L1_gnn_b3, L1_gnn_W4, L1_gnn_b4,
        L2_gnn_rel_embed, L3_gnn_mW1, L3_gnn_mb1, L3_gnn_mW2, L3_gnn_mb2,
        L3_gnn_uW1, L3_gnn_ub1, L3_gnn_uW2, L3_gnn_ub2, out):
    a = Names()
    a.x = x
    a.src = src
    a.dst = dst
    a.edge_attr_32 = edge_attr_32
    a.edge_type_500 = edge_type_500
    a.edge_weight = edge_weight
    a.L0_gnn_adaptive_weight = L0_gnn_adaptive_weight
    a.L1_gnn_W1 = L1_gnn_W1
    a.L1_gnn_b1 = L1_gnn_b1
    a.L1_gnn_W2 = L1_gnn_W2
    a.L1_gnn_b2 = L1_gnn_b2
    a.L1_gnn_W3 = L1_gnn_W3
    a.L1_gnn_b3 = L1_gnn_b3
    a.L1_gnn_W4 = L1_gnn_W4
    a.L1_gnn_b4 = L1_gnn_b4
    a.L2_gnn_rel_embed = L2_gnn_rel_embed
    a.L3_gnn_mW1 = L3_gnn_mW1
    a.L3_gnn_mb1 = L3_gnn_mb1
    a.L3_gnn_mW2 = L3_gnn_mW2
    a.L3_gnn_mb2 = L3_gnn_mb2
    a.L3_gnn_uW1 = L3_gnn_uW1
    a.L3_gnn_ub1 = L3_gnn_ub1
    a.L3_gnn_uW2 = L3_gnn_uW2
    a.L3_gnn_ub2 = L3_gnn_ub2
    n = a.x.shape[0]
    e = a.src.shape[0]
    m = 125
    nb = n // m
    groups = -(-e // GE)
    assert n % m == 0 and nb % KB == 0 and groups % SLOTS == 0 and m <= P and nb <= P
    tiles = groups * U
    k = Names()
    k.n, k.e, k.m, k.nb, k.groups, k.rounds, k.windows = n, e, m, nb, groups, groups // SLOTS, -(-n // P)

    k.table = nc.dram_tensor("table", [n + P, 64], F32)
    k.edge_pad = [nc.dram_tensor(name, [groups * GE], I32) for name in ("src_pad", "dst_pad", "type_pad")]
    k.scattered = [nc.dram_tensor(f"scattered_{j}", [n + P + 1, 64], F32) for j in range(SCATTERS)]
    k.table_rows = k.table[0:n, :].rearrange("(p b) f -> p b f", b=nb)
    k.inv_row = nc.dram_tensor("inv_row", [n], F32)
    k.u_table = nc.dram_tensor("u_table", [n, P], F32)
    k.v_table = nc.dram_tensor("v_table", [n + P, P], F32)
    k.rel_embed = a.L2_gnn_rel_embed
    k.relations = k.rel_embed.shape[0] // 4
    assert k.relations * 4 == k.rel_embed.shape[0] <= 2048 and k.relations <= P

    with ExitStack() as ctx:
        sb = lambda name, shape, dt=F32: ctx.enter_context(nc.sbuf_tensor(name, shape, dt))
        k.x, k.t = sb("x", [m, nb, 64]), sb("t", [m, nb, 64])
        behind = max(nb * 64, 5 * GE)
        k.acc = sb("acc", [P, max(n + P, 2 * P * U, behind + 3 * tiles + P)])
        k.x1 = sb("x1", [P, max(n, 12288, 6 * tiles)])
        k.idx = sb("idx", [P, tiles], I32)
        k.wgt, k.rel = sb("wgt", [P, tiles]), sb("rel", [P, tiles])
        k.base, k.pos = sb("base", [P, 2 * groups]), sb("pos", [P, groups])
        k.base_i = sb("base_i", [P, groups], I32)
        k.spread_f, k.spread_i = sb("spread_f", [P, 1]), sb("spread_i", [P, 1], I32)
        k.row_f, k.part_f, k.ident = sb("row_f", [P, P]), sb("part_f", [P, 1]), sb("ident", [P, P])
        k.part_i = sb("part_i", [P, 1], I32)
        k.deg_s, k.deg_d, k.inv_s, k.inv_d = (sb(s, [m, nb]) for s in ("deg_s", "deg_d", "inv_s", "inv_d"))
        k.mean, k.var = sb("mean", [m, nb]), sb("var", [m, nb])
        k.w1, k.w2, k.w3, k.w4 = sb("w1", [64, P]), sb("w2", [P, 64]), sb("w3", [64, P]), sb("w4", [P, 64])
        k.b1, k.b2, k.b3, k.b4 = sb("b1", [P, 1]), sb("b2", [64, 1]), sb("b3", [P, 1]), sb("b4", [64, 1])
        k.w_uv, k.we, k.mb1 = sb("w_uv", [64, 2 * P]), sb("we", [P, 4 * P]), sb("mb1", [P, P])
        k.mw2, k.mb2 = sb("mw2", [P, 64]), sb("mb2", [P, 64])
        k.uw1, k.ub1, k.uw2, k.ub2 = sb("uw1", [P, P]), sb("ub1", [P, 1]), sb("uw2", [P, 64]), sb("ub2", [P, 64])
        k.zeros = sb("zeros", [P, 64])
        k.adapt = sb("adapt", [P, 1])
        k.idx_slot = sb("idx_slot", [P, SLOTS, U], I32)
        k.rel_parts = sb("rel_parts", [k.relations, 4, 3 * 64], BF16)
        work = sb("work", [P, max(2 * U * P, 6 * KB * P)])
        k.one_hot = work[:, 0:2 * U * P].rearrange("p (o u n) -> p o u n", o=2, u=U)
        cut = lambda v, at, size: v[:, at:at + size]
        two = lambda at: cut(work, at * KB * P, 2 * KB * m).rearrange("p (o c) -> p o c", o=2)
        k.stage = two(0).rearrange("p o (b n) -> p o b n", b=KB)
        k.back, k.hid = two(2), two(4)
        more = sb("more", [P, SLOTS * U * 65])
        k.rows = more[:, :].rearrange("p (s u f) -> p s u f", s=SLOTS, u=U)
        k.t_rows = more[0:m, 0:2 * KB * 64].rearrange("p (o b f) -> p o b f", o=2, b=KB)
        k.scale = more[0:64, 0:4 * KB * m].rearrange("p (o c) -> p o c", o=4)
        k.inv_turned = work[0:nb, 0:m]
        k.feature_t = two(0)[0:64, :, :]
        k.u_rows = more[0:m, 0:2 * KB * P].rearrange("p (o b f) -> p o b f", o=2, b=KB)
        k.v_rows = more[0:m, 2 * KB * P:4 * KB * P].rearrange("p (o b f) -> p o b f", o=2, b=KB)
        k.plain_rows = work[0:m, 0:2 * KB * 64].rearrange("p (o b f) -> p o b f", o=2, b=KB)
        k.ends = more[:, 0:2 * groups]
        k.row_i = more[:, 2 * groups:2 * groups + P].bitcast(I32)
        k.fill = work[:, 0:GE].bitcast(I32)
        k.src_i, k.dst_i = cut(k.x1, 0, tiles).bitcast(I32), cut(k.x1, tiles, tiles).bitcast(I32)
        k.src_f, k.dst_f, k.src_hi, k.src_lo = (cut(k.x1, j * tiles, tiles) for j in range(2, 6))
        k.s_msg = cut(k.x1, 0, 1024).rearrange("p (o u f) -> p o u f", o=2, u=U)
        k.s_rel = cut(k.x1, 1024, 256)[0:k.relations, :].rearrange("p (c f) -> p c f", c=4)
        k.s_type_at = cut(k.x1, 1280, 4)
        k.s_hot_type = cut(k.acc, 0, 4 * GE)[0:k.relations, :].bitcast(BF16).rearrange("p (o c e u) -> p o c e u", o=2, c=4, u=U)
        k.s_types_h = cut(k.acc, 4 * GE, GE).bitcast(F16).rearrange("p (o e) -> p o e", o=2)
        k.s_types = more[:, 0:2 * GE].bitcast(I32).rearrange("p (o e) -> p o e", o=2)
        k.s_src = cut(k.x1, 2048, 2048).bitcast(I32).rearrange("p (o e u) -> p o e u", o=2, u=U)
        k.s_dst = cut(k.x1, 4096, 2048).bitcast(I32).rearrange("p (o e) -> p o e", o=2)
        k.s_hot_t = cut(k.x1, 6144, 2048).rearrange("p (o e u) -> p o e u", o=2, u=U)
        k.s_same = cut(k.x1, 8192, 2048).rearrange("p (o u e) -> p o u e", o=2, u=U)
        k.s_earlier = cut(k.x1, 10240, 1024).rearrange("p (u e) -> p u e", u=U)
        k.s_win = cut(k.x1, 11264, 128).rearrange("p (o f) -> p o f", o=2)
        k.s_repeat, k.s_at = cut(k.x1, 11392, U), cut(k.x1, 11392 + U, U)
        k.s_idx = cut(k.x1, 11392 + 2 * U, SLOTS * U).bitcast(I32).rearrange("p (s u) -> p s u", s=SLOTS)
        k.s_out = work[:, 0:SLOTS * U * 64].rearrange("p (s u f) -> p s u f", s=SLOTS, u=U)
        k.s_src_f, k.s_to, k.s_weight = (cut(k.acc, behind + j * tiles, tiles) for j in range(3))
        k.s_before = cut(k.acc, behind + 3 * tiles, P)
        k.m_u = cut(k.x1, 0, 4096).rearrange("p (s u f) -> p s u f", s=SLOTS, u=U)
        k.m_hot_t = cut(k.x1, 4096, 2048).rearrange("p (o e u) -> p o e u", o=2, u=U)
        k.m_dst = cut(k.x1, 6144, 2048).bitcast(I32).rearrange("p (o e) -> p o e", o=2)
        k.m_ea = cut(k.x1, 8192, 512).rearrange("p (o c) -> p o c", o=2)
        k.m_ea_t = cut(k.x1, 8704, 512).rearrange("p (o c) -> p o c", o=2)
        k.m_v = cut(k.x1, 9216, 256).rearrange("p (o c) -> p o c", o=2)
        k.m_relu = cut(k.x1, 9472, 2048).rearrange("p (o u f) -> p o u f", o=2, u=U)
        k.ps = ctx.enter_context(nc.psum_tensor("ps", [P, 8, 512], F32))

        k.gather_sems = [[ctx.enter_context(nc.semaphore(f"gathered_{j}_{s}")) for s in range(SLOTS)] for j in range(6)]
        k.late_loaded = ctx.enter_context(nc.semaphore("late_loaded"))
        k.scattered_in = [ctx.enter_context(nc.semaphore(f"scattered_in_{j}")) for j in range(SCATTERS)]
        k.pass_sems, k.phase_sems, k.open_phases = [], [], ctx.enter_context(ExitStack())

        def sem(name):
            k.pass_sems.append(ctx.enter_context(nc.semaphore(name)))
            return k.pass_sems[-1]

        slots = lambda name: [sem(f"{name}_{s}") for s in range(SLOTS)]
        k.same_ready = slots("same_ready")
        k.types_ready = slots("types_ready")
        k.idx_out = slots("idx_out")
        k.msg_done = slots("msg_done")
        k.from_dst = slots("from_dst")
        k.merged = slots("merged")
        k.out_ready = slots("out_ready")
        k.out_free = slots("out_free")
        k.idx_ready = slots("idx_ready")
        k.group_done = slots("group_done")
        k.summed = slots("summed")
        k.hot_ready = slots("hot_ready")
        k.loaded = slots("loaded")
        k.window_loaded = slots("window_loaded")
        k.pre_half = slots("pre_half")
        k.pre_done = slots("pre_done")
        k.ea_turned = slots("ea_turned")
        k.ea_ready = slots("ea_ready")
        k.hot_t_ready = slots("hot_t_ready")
        k.summed_half = slots("summed_half")
        k.relued = slots("relued")
        k.paced = sem("paced")
        k.dve_step = sem("dve_step")
        k.repeat_step = sem("repeat_step")
        k.table_step = sem("table_step")
        k.tables_ready = sem("tables_ready")
        k.loads_issued = sem("loads_issued")
        k.loaded_rest = sem("loaded_rest")

        load_and_index(nc, k, a)
        count_src(nc, k)
        norm_relu(nc, k, "norm0", scale=k.inv_s, add_to_x=True, clear_acc=True, ones=True)
        sum_by_dst(nc, k, k.table[0:n, :], 65)
        add_adaptive_sum(nc, k)
        norm_relu(nc, k, "norm1", scale=k.inv_d, add_to_x=True, inv_from=k.deg_d)
        start_acc(nc, k)
        sum_by_dst(nc, k, k.table[0:n, :], 64)
        convolve_wide(nc, k, "first", k.w1, k.b1, k.w2, residual=False)
        sum_by_dst(nc, k, k.table[0:n, :], 64)
        convolve_second(nc, k)
        sum_by_dst(nc, k, k.table[0:n, :], 64)
        convolve_wide(nc, k, "third", k.w3, k.b3, k.w4, residual=True)
        sum_by_dst(nc, k, k.table[0:n, :], 64)
        add_fourth(nc, k)
        norm_relu(nc, k, "norm2", clear_acc=True, late=True)
        scatter_to_src(nc, k)
        add_scattered(nc, k)
        norm_relu(nc, k, "norm3", clear_acc=True, store=False)
        message_tables(nc, k)
        sum_messages(nc, k, a.edge_attr_32, a.dst)
        update_nodes(nc, k, out)


_INS = ["x", "src", "dst", "edge_attr_32", "edge_type_500", "edge_weight", "L0_gnn_adaptive_weight",
        "L1_gnn_W1", "L1_gnn_b1", "L1_gnn_W2", "L1_gnn_b2", "L1_gnn_W3", "L1_gnn_b3", "L1_gnn_W4", "L1_gnn_b4",
        "L2_gnn_rel_embed", "L3_gnn_mW1", "L3_gnn_mb1", "L3_gnn_mW2", "L3_gnn_mb2",
        "L3_gnn_uW1", "L3_gnn_ub1", "L3_gnn_uW2", "L3_gnn_ub2"]


def kernel(**inputs):
    import numpy as _np
    import concourse.bacc as _bacc
    from concourse import mybir as _mybir
    from concourse.bass_utils import run_bass_kernel_spmd as _run

    nc = _bacc.Bacc("TRN2", target_bir_lowering=False, num_devices=1)
    arrays, args = {}, []
    for name in _INS:
        v = _np.ascontiguousarray(inputs[name])
        arrays[f"in_{name}"] = v
        args.append(nc.dram_tensor(f"in_{name}", v.shape, _mybir.dt.from_np(v.dtype), kind="ExternalInput").ap())
    out = nc.dram_tensor("out_x", arrays["in_x"].shape, _mybir.dt.float32, kind="ExternalOutput").ap()
    bass_four_graph_layers(nc, *args, out)
    return _run(nc, [arrays], core_ids=[0]).results[0]["out_x"]
```
